# Optimizing a Trainium2 kernel written in Bass

```python
import numpy as np
import jax
import jax.numpy as jnp

def _softmax(x, axis=-1):
    return jax.nn.softmax(x, axis=axis)

def _gelu(x):
    return jax.nn.gelu(x, approximate=True)

def _silu(x):
    return jax.nn.silu(x)

def _sigmoid(x):
    return jax.nn.sigmoid(x)

def _layernorm(x, axis=-1, eps=1e-05):
    m = jnp.mean(x, axis=axis, keepdims=True)
    v = jnp.var(x, axis=axis, keepdims=True)
    return (x - m) / jnp.sqrt(v + eps)

def _scatter_add(tgt, idx, src, axis=0):
    return tgt.at[idx].add(src)

def _segment_sum(src, seg, n):
    return jax.ops.segment_sum(src, seg, n)
kernel_name = 'mk_adj_preln_d2_adj_r2_2acc98'

def setup_inputs(seed: int=0):
    np.random.seed(seed)
    _w = jnp.asarray

    def _rec_inputs():
        import jax
        import jax.numpy as jnp
        _gk = jax.random.key(seed)
        x = -0.000125 + 0.9999 * jax.random.normal(jax.random.fold_in(_gk, 1), (32, 256, 128), jnp.float32)
        _a = jax.random.bernoulli(jax.random.fold_in(_gk, 2), 0.015625, (256, 256))
        _a = jnp.logical_or(_a, jnp.swapaxes(_a, -1, -2))
        _a = jnp.logical_or(_a, jnp.eye(256, dtype=bool))
        _af = _a.astype(jnp.float32)
        _af = _af * jax.random.uniform(jax.random.fold_in(_gk, 3), (256, 256), jnp.float32, 0.05, 0.000488281)
        adj = _af
        return (x, adj)
    x, adj = _rec_inputs()

    def _L0_gnn_setup():
        import jax, jax.numpy as jnp
        import numpy as np
        B, T, D, H = (64, 1024, 128, 128)
        MAX_SKIP = 4

        def _lstm_last(Wih, Whh, bih, bhh, xs):
            N, _, Hd = xs.shape
            bias = bih + bhh

            def step(carry, x_t):
                h, c = carry
                g = x_t @ Wih.T + h @ Whh.T + bias
                i, f, gg, o = jnp.split(g, 4, axis=-1)
                c = jax.nn.sigmoid(f) * c + jax.nn.sigmoid(i) * jnp.tanh(gg)
                h = jax.nn.sigmoid(o) * jnp.tanh(c)
                return ((h, c), None)
            init = (jnp.zeros((N, Hd), xs.dtype), jnp.zeros((N, Hd), xs.dtype))
            (h_last, _), _ = jax.lax.scan(step, init, jnp.swapaxes(xs, 0, 1))
            return h_last
        key = jax.random.key(seed)
        ks = jax.random.split(key, 8)
        s = 0.05
        x = jax.random.normal(ks[0], (B, T, D), jnp.float32)
        adj = jax.random.uniform(ks[1], (T, T), jnp.float32) / T
        Wg0 = jax.random.normal(ks[2], (D, H), jnp.float32) * s
        bg0 = jnp.zeros((H,), jnp.float32)
        Wg1 = jax.random.normal(ks[3], (H, H), jnp.float32) * s
        bg1 = jnp.zeros((H,), jnp.float32)
        Wih = jax.random.normal(ks[4], (MAX_SKIP, 4 * H, H), jnp.float32) * s
        Whh = jax.random.normal(ks[5], (MAX_SKIP, 4 * H, H), jnp.float32) * s
        bih = jax.random.normal(ks[6], (MAX_SKIP, 4 * H), jnp.float32) * s
        bhh = jax.random.normal(ks[7], (MAX_SKIP, 4 * H), jnp.float32) * s
        return dict(x=x, adj=adj, Wg0=Wg0, bg0=bg0, Wg1=Wg1, bg1=bg1, Wih=Wih, Whh=Whh, bih=bih, bhh=bhh)
    _L0_gnn_all = _L0_gnn_setup()
    _L0_gnn_in = {k: v for k, v in _L0_gnn_all.items() if k in ('Wg0', 'bg0', 'Wg1', 'bg1', 'Wih', 'Whh', 'bih', 'bhh')}
    del _L0_gnn_all

    def _L1_gnn_setup():
        import jax, jax.numpy as jnp
        import numpy as np
        EPS_LN = 1e-05

        def _layernorm(x, g, b):
            mu = x.mean(-1, keepdims=True)
            var = ((x - mu) ** 2).mean(-1, keepdims=True)
            return (x - mu) / jnp.sqrt(var + EPS_LN) * g + b
        key = jax.random.key(seed)
        B, N, D, H = (4, 1024, 128, 4)
        hid = int(D * 2.0)
        ks = jax.random.split(key, 12)
        x = jax.random.normal(ks[0], (B, N, D), jnp.float32)
        Au = jax.random.uniform(ks[1], (N, N)) < 0.004
        A = jnp.logical_or(Au, Au.T)
        A = A.at[jnp.arange(N), jnp.arange(N)].set(False)
        Af = A.astype(jnp.float32)
        deg = Af.sum(axis=1)
        L = jnp.diag(deg) - Af
        adjacency = Af + jnp.eye(N, dtype=jnp.float32)
        s = lambda k, sh, f: jax.random.normal(k, sh, jnp.float32) * f
        sc = 1.0 / np.sqrt(D)
        Wc = s(ks[2], (D, D), sc)
        bc = jnp.zeros((D,), jnp.float32)
        Wq = s(ks[3], (D, D), sc)
        Wk = s(ks[4], (D, D), sc)
        Wv = s(ks[5], (D, D), sc)
        Wo = s(ks[6], (D, D), sc)
        bo = jnp.zeros((D,), jnp.float32)
        W1 = s(ks[7], (D, hid), sc)
        b1 = jnp.zeros((hid,), jnp.float32)
        W2 = s(ks[8], (hid, D), 1.0 / np.sqrt(hid))
        b2 = jnp.zeros((D,), jnp.float32)
        g1 = jnp.ones((D,), jnp.float32)
        be1 = jnp.zeros((D,), jnp.float32)
        g2 = jnp.ones((D,), jnp.float32)
        be2 = jnp.zeros((D,), jnp.float32)
        g3 = jnp.ones((D,), jnp.float32)
        be3 = jnp.zeros((D,), jnp.float32)
        return dict(x=x, L=L, adjacency=adjacency, Wc=Wc, bc=bc, g1=g1, be1=be1, Wq=Wq, Wk=Wk, Wv=Wv, Wo=Wo, bo=bo, g2=g2, be2=be2, W1=W1, b1=b1, W2=W2, b2=b2, g3=g3, be3=be3)
    _L1_gnn_all = _L1_gnn_setup()
    _L1_gnn_in = {k: v for k, v in _L1_gnn_all.items() if k in ('Wc', 'bc', 'g1', 'be1', 'Wq', 'Wk', 'Wv', 'Wo', 'bo', 'g2', 'be2', 'W1', 'b1', 'W2', 'b2', 'g3', 'be3')}
    del _L1_gnn_all
    return {'x': x, 'adj': adj, 'L0_gnn_Wg0': _L0_gnn_in['Wg0'], 'L0_gnn_bg0': _L0_gnn_in['bg0'], 'L0_gnn_Wg1': _L0_gnn_in['Wg1'], 'L0_gnn_bg1': _L0_gnn_in['bg1'], 'L0_gnn_Wih': _L0_gnn_in['Wih'], 'L0_gnn_Whh': _L0_gnn_in['Whh'], 'L0_gnn_bih': _L0_gnn_in['bih'], 'L0_gnn_bhh': _L0_gnn_in['bhh'], 'L1_gnn_Wc': _L1_gnn_in['Wc'], 'L1_gnn_bc': _L1_gnn_in['bc'], 'L1_gnn_g1': _L1_gnn_in['g1'], 'L1_gnn_be1': _L1_gnn_in['be1'], 'L1_gnn_Wq': _L1_gnn_in['Wq'], 'L1_gnn_Wk': _L1_gnn_in['Wk'], 'L1_gnn_Wv': _L1_gnn_in['Wv'], 'L1_gnn_Wo': _L1_gnn_in['Wo'], 'L1_gnn_bo': _L1_gnn_in['bo'], 'L1_gnn_g2': _L1_gnn_in['g2'], 'L1_gnn_be2': _L1_gnn_in['be2'], 'L1_gnn_W1': _L1_gnn_in['W1'], 'L1_gnn_b1': _L1_gnn_in['b1'], 'L1_gnn_W2': _L1_gnn_in['W2'], 'L1_gnn_b2': _L1_gnn_in['b2'], 'L1_gnn_g3': _L1_gnn_in['g3'], 'L1_gnn_be3': _L1_gnn_in['be3']}

def reference(x, adj, L0_gnn_Wg0, L0_gnn_bg0, L0_gnn_Wg1, L0_gnn_bg1, L0_gnn_Wih, L0_gnn_Whh, L0_gnn_bih, L0_gnn_bhh, L1_gnn_Wc, L1_gnn_bc, L1_gnn_g1, L1_gnn_be1, L1_gnn_Wq, L1_gnn_Wk, L1_gnn_Wv, L1_gnn_Wo, L1_gnn_bo, L1_gnn_g2, L1_gnn_be2, L1_gnn_W1, L1_gnn_b1, L1_gnn_W2, L1_gnn_b2, L1_gnn_g3, L1_gnn_be3):
    import jax
    import jax.numpy as jnp

    def _L0_gnn_ref(x, adj, Wg0, bg0, Wg1, bg1, Wih, Whh, bih, bhh):
        import jax, jax.numpy as jnp
        import numpy as np
        B, T, D, H = (64, 1024, 128, 128)
        MAX_SKIP = 4

        def _lstm_last(Wih, Whh, bih, bhh, xs):
            N, _, Hd = xs.shape
            bias = bih + bhh

            def step(carry, x_t):
                h, c = carry
                g = x_t @ Wih.T + h @ Whh.T + bias
                i, f, gg, o = jnp.split(g, 4, axis=-1)
                c = jax.nn.sigmoid(f) * c + jax.nn.sigmoid(i) * jnp.tanh(gg)
                h = jax.nn.sigmoid(o) * jnp.tanh(c)
                return ((h, c), None)
            init = (jnp.zeros((N, Hd), xs.dtype), jnp.zeros((N, Hd), xs.dtype))
            (h_last, _), _ = jax.lax.scan(step, init, jnp.swapaxes(xs, 0, 1))
            return h_last
        h = jax.nn.relu(jnp.einsum('ts,bsh->bth', adj, x @ Wg0 + bg0))
        h = jax.nn.relu(jnp.einsum('ts,bsh->bth', adj, h @ Wg1 + bg1))
        Bv, Tv, Hd = h.shape
        for p in range(1, MAX_SKIP + 1):
            nw = Tv // p
            wins = h[:, :nw * p, :].reshape(Bv * nw, p, Hd)
            last = _lstm_last(Wih[p - 1], Whh[p - 1], bih[p - 1], bhh[p - 1], wins)
            idx = jnp.arange(nw) * p + (p - 1)
            h = h.at[:, idx, :].set(last.reshape(Bv, nw, Hd))
        return h

    def _L1_gnn_ref(x, L, adjacency, Wc, bc, g1, be1, Wq, Wk, Wv, Wo, bo, g2, be2, W1, b1, W2, b2, g3, be3):
        import jax, jax.numpy as jnp
        import numpy as np
        EPS_LN = 1e-05

        def _layernorm(x, g, b):
            mu = x.mean(-1, keepdims=True)
            var = ((x - mu) ** 2).mean(-1, keepdims=True)
            return (x - mu) / jnp.sqrt(var + EPS_LN) * g + b
        B, N, D = x.shape
        H = 4
        hd = D // H
        eig = jnp.linalg.eigvalsh(L)
        lam_max = eig[-1] + 1e-08
        L_norm = 2.0 * L / lam_max - jnp.eye(N, dtype=L.dtype)
        xp = jnp.einsum('mn,bnf->bmf', L_norm, x)
        h = xp @ Wc + bc
        h = _layernorm(h, g1, be1)
        h = jax.nn.relu(h)
        x1 = h + x
        q = (x1 @ Wq).reshape(B, N, H, hd).transpose(0, 2, 1, 3)
        k = (x1 @ Wk).reshape(B, N, H, hd).transpose(0, 2, 1, 3)
        v = (x1 @ Wv).reshape(B, N, H, hd).transpose(0, 2, 1, 3)
        scores = jnp.einsum('bhnd,bhmd->bhnm', q, k) / np.sqrt(hd).astype(np.float32)
        scores = jnp.where(adjacency[None, None] > 0, scores, jnp.float32(-1000000000.0))
        attn = jax.nn.softmax(scores, axis=-1)
        o = jnp.einsum('bhnm,bhmd->bhnd', attn, v)
        o = o.transpose(0, 2, 1, 3).reshape(B, N, D)
        o = o @ Wo + bo
        x2 = _layernorm(x1 + o, g2, be2)
        m = jax.nn.gelu(x2 @ W1 + b1, approximate=False) @ W2 + b2
        return _layernorm(x2 + m, g3, be3)
    h = jnp.maximum(_layernorm(x, axis=-1), 0.0)
    x = x + _L0_gnn_ref(h, adj, L0_gnn_Wg0, L0_gnn_bg0, L0_gnn_Wg1, L0_gnn_bg1, L0_gnn_Wih, L0_gnn_Whh, L0_gnn_bih, L0_gnn_bhh)
    h = jnp.maximum(_layernorm(x, axis=-1), 0.0)
    x = x + _L1_gnn_ref(h, adj, adj, L1_gnn_Wc, L1_gnn_bc, L1_gnn_g1, L1_gnn_be1, L1_gnn_Wq, L1_gnn_Wk, L1_gnn_Wv, L1_gnn_Wo, L1_gnn_bo, L1_gnn_g2, L1_gnn_be2, L1_gnn_W1, L1_gnn_b1, L1_gnn_W2, L1_gnn_b2, L1_gnn_g3, L1_gnn_be3)
    return x

_drawn_inputs = setup_inputs


def setup_inputs(seed=0):
    import zlib

    import numpy as np

    out = dict(_drawn_inputs(seed))
    spreads = {'L0_gnn_bg0': (0.0, 0.8),
     'L0_gnn_bg1': (0.0, 0.8),
     'L1_gnn_bc': (0.0, 0.1),
     'L1_gnn_g1': (1.0, 0.2),
     'L1_gnn_be1': (0.0, 0.1),
     'L1_gnn_bo': (0.0, 0.1),
     'L1_gnn_g2': (1.0, 0.2),
     'L1_gnn_be2': (0.0, 0.1),
     'L1_gnn_b1': (0.0, 0.1),
     'L1_gnn_b2': (0.0, 0.1),
     'L1_gnn_g3': (1.0, 0.2),
     'L1_gnn_be3': (0.0, 0.1)}
    factors = {'L0_gnn_Wg0': 8.0,
     'L0_gnn_Wg1': 8.0,
     'L0_gnn_Wih': 8.0,
     'L0_gnn_Whh': 8.0,
     'L0_gnn_bih': 2.825,
     'L0_gnn_bhh': 2.929}
    for name, (base, spread) in spreads.items():
        noise = np.random.default_rng([zlib.crc32(name.encode()), seed]).standard_normal(out[name].shape)
        drawn = base * np.exp(spread * noise) if base else spread * noise
        out[name] = jnp.asarray(drawn.astype(out[name].dtype))
    for name, factor in factors.items():
        out[name] = (out[name] * factor).astype(out[name].dtype)
    return out
```

```python
from contextlib import ExitStack

import concourse.bass as bass
from concourse import mybir

F32 = mybir.dt.float32
F32R = mybir.dt.float32r
BF16 = mybir.dt.bfloat16
ALU = mybir.AluOpType
ACT = mybir.ActivationFunctionType
AX = mybir.AxisListType
RMAX = bass.bass_isa.ReduceOp.max

P = 128
NB, T, D = 32, 256, 128
TILES = NB * T // P
UB = 2
UT = UB * T // P
UW = UB * T
UNITS = NB // UB
CHUNK = 8
EPS = 1e-5
SQUARINGS = 16
MAX_SKIP = 4
HS = T + 2
HEADS, HD = 4, 32
HID = 256
MASKED = -(2.0 ** 100)
I, F, G, O = range(4)

LANE_B = 8
LANES = 2
LSTM_TURNS = NB // (LANE_B * LANES)


def lane_steps():
    steps = []
    for p, nb in ((1, 2), (2, 4), (3, 4), (4, 8)):
        windows = T // p + (T // p) % 2
        for b0 in range(0, LANE_B, nb):
            steps += [(p, b0, nb, windows, t) for t in range(p)]
    return steps


STEPS = lane_steps()


def last_writer(n):
    p, b0, nb, _, _ = STEPS[n]
    done = 0
    for m in range(n):
        q, c0, cb, _, t = STEPS[m]
        if q < p and t == q - 1 and c0 < b0 + nb and b0 < c0 + cb:
            done = m + 1
    return done


def recurrent(n):
    return sum(step[4] > 0 for step in STEPS[:n])


class Count:

    def __init__(self, sem, per=1):
        self.sem, self.per = sem, per

    def start(self, engine):
        engine.sem_inc(self.sem, 2 * self.per)

    def done(self, unit, n=None):
        return unit * self.per + (2 * self.per + (self.per if n is None else n))


def build(nc, d, out):
    with ExitStack() as top:
        def sem(name):
            return top.enter_context(nc.semaphore(name))

        def count(name, per=1):
            return Count(sem(name), per)

        def sb(name, shape, dt=F32, ctx=top):
            return ctx.enter_context(nc.sbuf_tensor(name, shape, dt))

        ps = top.enter_context(nc.psum_tensor("ps", [P, 8, 512], F32))

        X = sb("X", [P, TILES, D])
        adj_sb = sb("adj_sb", [P, 2, T])
        adjT = sb("adjT", [P, 2, T])
        LT = sb("LT", [P, 2, T])
        ident2 = sb("ident2", [P, 2, T])
        ident = ident2[:, 0, 0:P]
        identb = sb("identb", [P, P], BF16)
        maskb = sb("maskb", [P, 2, T], BF16)
        ones = sb("ones", [P, P])
        minus_half = sb("minus_half", [P, UT])
        eps = sb("eps", [P, UT])
        rows = sb("rows", [P, 9, D])
        cols = sb("cols", [P, 3])
        bn = sb("bn", [P, TILES, 6])
        mean2 = sb("mean2", [P, TILES])
        diff = sb("diff", [P, TILES])
        m2 = sb("m2", [P, TILES])
        var = sb("var", [P, TILES])
        std = sb("std", [P, TILES])
        rstd = sb("rstd", [P, TILES])
        nmr = sb("nmr", [P, TILES])
        BC, G1, BE1, BO, G2, BE2, B2, G3, BE3 = range(9)

        def row(n, tiles=UT):
            return rows[:, n, :].unsqueeze(1).broadcast_to([P, tiles, D])

        x_loaded = [sem(f"x_loaded{c}") for c in range(TILES // CHUNK)]
        consts_loaded = sem("consts_loaded")
        weights_loaded = sem("weights_loaded")
        const_made = sem("const_made")
        stats = sem("stats")
        bn_made = sem("bn_made")

        def layernorm_stats(dve, act, base):
            if dve is not None:
                h = [bn[:, :, k] for k in range(6)]
                nc.vector.tensor_tensor(mean2[:], h[1], h[4], ALU.add)
                nc.vector.tensor_tensor(diff[:], h[1], h[4], ALU.subtract)
                nc.vector.tensor_tensor(m2[:], h[2], h[5], ALU.add).then_inc(stats, 1)
                dve.wait_ge(stats, base + 1)
                nc.vector.scalar_tensor_tensor(std[:], diff[:], 0.25, diff[:], ALU.mult, ALU.mult).then_inc(stats, 1)
                dve.wait_ge(stats, base + 2)
                nc.vector.scalar_tensor_tensor(var[:], m2[:], 1.0 / D, std[:], ALU.mult, ALU.add).then_inc(stats, 1)
                dve.wait_ge(stats, base + 3)
                nc.vector.tensor_scalar(var[:], var[:], EPS, None, ALU.add).then_inc(stats, 1)
                dve.wait_ge(stats, base + 5)
                nc.vector.reciprocal(rstd[:], std[:]).then_inc(stats, 1)
                dve.wait_ge(stats, base + 6)
                nc.vector.scalar_tensor_tensor(nmr[:], mean2[:], -0.5, rstd[:], ALU.mult, ALU.mult).then_inc(stats, 1)
            if act is not None:
                act.wait_ge(stats, base + 4)
                nc.scalar.activation(std[:], var[:], ACT.Sqrt).then_inc(stats, 1)
                act.wait_ge(stats, base + 7)

        MEAN, VAR, SUM, DIFF, SQ, DIFF2 = range(6)

        def moments_of(dve, b, mo, made, unit, n):
            nc.vector.tensor_tensor(mo[:, SUM, :], b[:, :, 1], b[:, :, 4], ALU.add)
            nc.vector.tensor_tensor(mo[:, DIFF, :], b[:, :, 1], b[:, :, 4], ALU.subtract)
            nc.vector.tensor_tensor(mo[:, SQ, :], b[:, :, 2], b[:, :, 5], ALU.add).then_inc(made.sem, 1)
            dve.wait_ge(made.sem, made.done(unit, n + 1))
            nc.vector.tensor_scalar(mo[:, MEAN, :], mo[:, SUM, :], 0.5, None, ALU.mult)
            nc.vector.scalar_tensor_tensor(mo[:, DIFF2, :], mo[:, DIFF, :], 0.25, mo[:, DIFF, :], ALU.mult,
                                           ALU.mult).then_inc(made.sem, 1)
            dve.wait_ge(made.sem, made.done(unit, n + 2))
            nc.vector.scalar_tensor_tensor(mo[:, VAR, :], mo[:, SQ, :], 1.0 / D, mo[:, DIFF2, :], ALU.mult,
                                           ALU.add).then_inc(made.sem, 1)

        lstm_ctx = top.enter_context(ExitStack())
        Hhi = sb("Hhi", [P, NB, HS], F32R, lstm_ctx)
        Hlo = sb("Hlo", [P, NB, HS], F32R, lstm_ctx)
        WX = sb("WX", [P, 2, MAX_SKIP, 4 * D], F32R, lstm_ctx)
        WH = sb("WH", [P, 2, MAX_SKIP, 4 * D], F32R, lstm_ctx)
        bias = sb("bias", [P, MAX_SKIP * 4], F32, lstm_ctx)

        with ExitStack() as ctx:
            W_raw = sb("W_raw", [P, 2, MAX_SKIP * 4 * D], F32, ctx)
            bias_raw = sb("bias_raw", [P, 2, MAX_SKIP * 4], F32, ctx)
            Wg = sb("Wg", [P, 2, D], F32, ctx)
            bg0 = sb("bg0", [P, D], F32, ctx)
            rowsum = sb("rowsum", [P, 2], F32, ctx)
            rowsum_b = sb("rowsum_b", [P, 2, T], F32, ctx)
            bias0 = sb("bias0", [P, UT, D], F32, ctx)
            S = sb("S", [P, 2, T], F32, ctx)
            M = sb("M", [P, 2, T], F32, ctx)
            eig_junk = sb("eig_junk", [P, 2, T], F32, ctx)
            norms = sb("norms", [P, 2], F32, ctx)
            norm_all = sb("norm_all", [P, 2], F32, ctx)
            shift = sb("shift", [P, 1], F32, ctx)
            diag = sb("diag", [P, 1], F32, ctx)
            trace_r = sb("trace_r", [P, 1], F32, ctx)
            trace_r2 = sb("trace_r2", [P, 1], F32, ctx)
            quotient = sb("quotient", [P, 2], F32, ctx)
            lam = sb("lam", [P, 3], F32, ctx)
            u = sb("u0", [P, 2, UT, D], F32, ctx)
            A0 = sb("A0", [P, 2, UW], F32, ctx)
            y0 = sb("y0", [P, 2, UT, D], F32, ctx)
            h1 = sb("h1", [P, 2, UT, D], F32, ctx)
            A1 = sb("A1", [P, 2, UW], F32, ctx)
            y1 = sb("y1", [P, 2, UB, T], F32, ctx)

            u_made = count("u_made", 2)
            a0_mm = count("a0_mm", 2)
            a0_out = count("a0_out", 2)
            w0_mm = count("w0_mm", 2)
            y0_out = count("y0_out", 2)
            h1_made = count("h1_made", 2)
            a1_mm = count("a1_mm", 2)
            a1_out = count("a1_out", 2)
            w1_mm = count("w1_mm", 2)
            y1_out = count("y1_out", 2)
            hi_made = count("hi_made", 2)
            lo_made = count("lo_made", 2)
            sq_mm = count("sq_mm")
            tr_mm = count("tr_mm")
            tr_used = count("tr_used", 2)
            m_made = count("m_made")
            diag_made = count("diag_made")
            eig = sem("eig")
            lt_made = sem("lt_made")
            split = sem("split")
            PS_SQ, PS_TR = 7, 6
            per_turn = SQUARINGS // (UNITS // 2)

            with nc.Block() as block:
                @block.sync
                def _(sp):
                    sp.dma_start(adj_sb[:], d["adj"]).then_inc(consts_loaded, 16)
                    sp.dma_start(adjT[:], d["adjT"]).then_inc(consts_loaded, 16)
                    for c in range(TILES // CHUNK):
                        tiles = slice(c * CHUNK, (c + 1) * CHUNK)
                        sp.dma_start(X[:, tiles, :], d["x"][:, tiles, :]).then_inc(x_loaded[c], 16)
                        if c == 0:
                            sp.dma_start(Wg[:], d["Wg"]).then_inc(consts_loaded, 16)
                            sp.dma_start(bg0[:], d["bg0"].to_broadcast([P, D])).then_inc(consts_loaded, 16)
                            sp.dma_start(cols[:], d["cols"]).then_inc(consts_loaded, 16)
                    sp.dma_start(W_raw[:, 0, :], d["Wih"]).then_inc(weights_loaded, 16)
                    sp.dma_start(W_raw[:, 1, :], d["Whh"]).then_inc(weights_loaded, 16)
                    sp.dma_start(bias_raw[:], d["lstm_b"]).then_inc(weights_loaded, 16)
                    sp.dma_start(rows[:], d["rows"].unsqueeze(0).broadcast_to([P, 9, D])).then_inc(weights_loaded, 16)

                @block.gpsimd
                def _(pool):
                    nc.gpsimd.memset(ident2[:], 0.0).then_inc(const_made, 1)
                    nc.gpsimd.memset(ones[:], 1.0).then_inc(const_made, 1)
                    nc.gpsimd.memset(minus_half[:], -0.5).then_inc(const_made, 1)
                    nc.gpsimd.memset(eps[:], EPS).then_inc(const_made, 1)
                    pool.wait_ge(const_made, 4)
                    nc.gpsimd.affine_select(out=ident2[:], in_=ident2[:], compare_op=ALU.not_equal, fill=1.0, base=0,
                                            pattern=[[P, 2], [-1, T]], channel_multiplier=1).then_inc(const_made, 1)
                    pool.wait_ge(eig, 3)
                    nc.gpsimd.partition_all_reduce(norm_all[:], norms[:], P, RMAX).then_inc(eig, 1)
                    for H in (Hhi, Hlo):
                        nc.gpsimd.memset(H[:, :, T:HS].bitcast(F32), 0.0).then_inc(const_made, 1)
                    pool.wait_ge(weights_loaded, 64)
                    for n, W in enumerate((WX, WH)):
                        hi, lo = (W[:, k, :, :].rearrange("p a b -> p (a b)") for k in range(2))
                        nc.gpsimd.tensor_copy(hi, W_raw[:, n, :]).then_inc(split, 1)
                        pool.wait_ge(split, 2 * n + 1)
                        nc.gpsimd.tensor_tensor(lo, W_raw[:, n, :], hi.bitcast(F32), ALU.subtract).then_inc(split, 1)
                    nc.gpsimd.tensor_tensor(bias[:], bias_raw[:, 0, :], bias_raw[:, 1, :], ALU.add).then_inc(split, 1)
                    pool.wait_ge(split, 5)

                @block.vector
                def _(dve):
                    for c in (a0_out, y0_out, a1_out, y1_out, lo_made, tr_used, m_made, diag_made):
                        c.start(dve)
                    dve.wait_ge(consts_loaded, 80)
                    nc.vector.tensor_tensor(S[:], adj_sb[:], adjT[:], ALU.add).then_inc(eig, 1)
                    nc.vector.tensor_scalar(maskb[:], adj_sb[:], 0.0, MASKED, ALU.is_le, ALU.mult)
                    nc.vector.tensor_reduce(rowsum[:], adj_sb[:], AX.X, ALU.add).then_inc(stats, 1)
                    dve.wait_ge(eig, 1)
                    nc.vector.tensor_scalar(S[:], S[:], 0.5, None, ALU.mult).then_inc(eig, 1)
                    dve.wait_ge(eig, 2)
                    nc.vector.tensor_reduce(norms[:], S[:], AX.X, ALU.add, apply_absolute_value=True).then_inc(eig, 1)
                    dve.wait_ge(stats, 1)
                    for k in range(UT):
                        nc.vector.tensor_scalar(bias0[:, k, :], bg0[:], rowsum[:, k % 2:k % 2 + 1], None, ALU.mult)
                    dve.wait_ge(const_made, 5)
                    nc.vector.tensor_copy(identb[:], ident)
                    dve.wait_ge(eig, 4)
                    nc.vector.tensor_reduce(shift[:], norm_all[:], AX.X, ALU.max).then_inc(eig, 1)
                    dve.wait_ge(eig, 5)
                    nc.vector.tensor_scalar(shift[:], shift[:], 1e-12, None, ALU.add).then_inc(eig, 1)
                    dve.wait_ge(eig, 6)
                    nc.vector.scalar_tensor_tensor(M[:], ident2[:], shift[:], S[:], ALU.mult, ALU.add).then_inc(eig, 1)
                    dve.wait_ge(eig, 7)
                    nc.vector.tensor_tensor_reduce(eig_junk[:], M[:], ident2[:], 1.0, 0.0, ALU.mult, ALU.add,
                                                   diag[:]).then_inc(eig, 1)
                    dve.wait_ge(eig, 9)
                    for k in range(2):
                        last = nc.vector.tensor_copy(rowsum_b[:, k, :], ps[:, 0, 0:T])
                    last.then_inc(eig, 1)
                    for c in range(TILES // CHUNK):
                        dve.wait_ge(x_loaded[c], 16)
                        with dve.Fori(c * CHUNK, (c + 1) * CHUNK) as k:
                            nc.vector.bn_stats(bn[:, bass.ds(k, 1), :].rearrange("p a b -> p (a b)"),
                                               X[:, bass.ds(k, 1), :].rearrange("p a b -> p (a b)")).then_inc(bn_made, 1)
                    dve.wait_ge(bn_made, TILES)
                    layernorm_stats(dve, None, 1)

                    def squaring(n):
                        dve.wait_ge(tr_mm.sem, tr_mm.done(n))
                        nc.vector.reciprocal(trace_r[:], ps[:, PS_TR, 0:1]).then_inc(tr_used.sem, 1)
                        dve.wait_ge(tr_used.sem, tr_used.done(n, 1))
                        nc.vector.tensor_tensor(trace_r2[:], trace_r[:], trace_r[:], ALU.mult).then_inc(tr_used.sem, 1)
                        dve.wait_ge(tr_used.sem, tr_used.done(n))
                        dve.wait_ge(sq_mm.sem, sq_mm.done(n))
                        nc.vector.tensor_scalar(M[:].rearrange("p a b -> p (a b)"), ps[:, PS_SQ, :], trace_r2[:], None,
                                                ALU.mult).then_inc(m_made.sem, 1)
                        dve.wait_ge(m_made.sem, m_made.done(n))
                        nc.vector.tensor_tensor_reduce(eig_junk[:], M[:], ident2[:], 1.0, 0.0, ALU.mult, ALU.add,
                                                       diag[:]).then_inc(diag_made.sem, 1)

                    with dve.Fori(0, UNITS // 2) as g:
                        for s in range(2):
                            dve.wait_ge(a0_mm.sem, a0_mm.done(g, s + 1))
                            dve.wait_ge(w0_mm.sem, w0_mm.done(g - 1, s + 1))
                            nc.vector.tensor_copy(A0[:, s, :], ps[:, s, :]).then_inc(a0_out.sem, 1)
                        squaring(g * per_turn)
                        for s in range(2):
                            dve.wait_ge(w0_mm.sem, w0_mm.done(g, s + 1))
                            dve.wait_ge(h1_made.sem, h1_made.done(g - 1, s + 1))
                            nc.vector.tensor_tensor(y0[:, s, :, :].rearrange("p a b -> p (a b)"), ps[:, 2 + s, :],
                                                    bias0[:].rearrange("p a b -> p (a b)"),
                                                    ALU.add).then_inc(y0_out.sem, 1)
                        for s in range(2):
                            dve.wait_ge(a1_mm.sem, a1_mm.done(g, s + 1))
                            dve.wait_ge(w1_mm.sem, w1_mm.done(g - 1, s + 1))
                            nc.vector.tensor_copy(A1[:, s, :], ps[:, 4 + s, :]).then_inc(a1_out.sem, 1)
                        squaring(g * per_turn + 1)
                        for s in range(2):
                            dve.wait_ge(w1_mm.sem, w1_mm.done(g, s + 1))
                            dve.wait_ge(hi_made.sem, hi_made.done(g - 1, s + 1))
                            nc.vector.scalar_tensor_tensor(
                                y1[:, s, :, :].rearrange("p a b -> p (a b)"), rowsum_b[:].rearrange("p a b -> p (a b)"),
                                cols[:, 0:1], ps[:, s, :], ALU.mult, ALU.add).then_inc(y1_out.sem, 1)
                        for s in range(2):
                            dve.wait_ge(hi_made.sem, hi_made.done(g, s + 1))
                            b = bass.ds(g * (2 * UB) + s * UB, UB)
                            nc.vector.scalar_tensor_tensor(
                                Hlo[:, b, 0:T], y1[:, s, :, :], 0.0, Hhi[:, b, 0:T].bitcast(F32),
                                ALU.max, ALU.subtract).then_inc(lo_made.sem, 1)
                    dve.wait_ge(sq_mm.sem, sq_mm.done(SQUARINGS))
                    nc.vector.tensor_tensor_reduce(eig_junk[:].rearrange("p a b -> p (a b)"),
                                                   M[:].rearrange("p a b -> p (a b)"), ps[:, PS_SQ, :], 1.0, 0.0,
                                                   ALU.mult, ALU.add, quotient[:, 0:1]).then_inc(eig, 1)
                    dve.wait_ge(eig, 11)
                    nc.vector.tensor_tensor_reduce(eig_junk[:], M[:], M[:], 1.0, 0.0, ALU.mult, ALU.add,
                                                   quotient[:, 1:2]).then_inc(eig, 1)
                    dve.wait_ge(eig, 13)
                    nc.vector.reciprocal(lam[:, 0:1], ps[:, PS_TR, 1:2]).then_inc(eig, 1)
                    dve.wait_ge(eig, 14)
                    nc.vector.tensor_tensor(lam[:, 1:2], ps[:, PS_TR, 0:1], lam[:, 0:1], ALU.mult).then_inc(eig, 1)
                    dve.wait_ge(eig, 15)
                    nc.vector.tensor_scalar(lam[:, 1:2], lam[:, 1:2], 1e-8, 0.5, ALU.add, ALU.mult).then_inc(eig, 1)
                    dve.wait_ge(eig, 16)
                    nc.vector.reciprocal(lam[:, 2:3], lam[:, 1:2]).then_inc(eig, 1)
                    dve.wait_ge(eig, 17)
                    nc.vector.scalar_tensor_tensor(LT[:], adjT[:], lam[:, 2:3], ident2[:], ALU.mult,
                                                   ALU.subtract).then_inc(lt_made, 1)
                    dve.wait_ge(lt_made, 1)

                @block.scalar
                def _(act):
                    for c in (u_made, h1_made, hi_made):
                        c.start(act)
                    for c in range(TILES // CHUNK):
                        act.wait_ge(x_loaded[c], 16)
                    layernorm_stats(None, act, 1)
                    with act.Fori(0, UNITS // 2) as g:
                        for s in range(2):
                            act.wait_ge(a0_mm.sem, a0_mm.done(g - 1, s + 1))
                            for k in range(UT):
                                tile = bass.ds(g * (2 * UT) + (s * UT + k), 1)
                                last = nc.scalar.activation(u[:, s, k, :],
                                                            X[:, tile, :].rearrange("p a b -> p (a b)"),
                                                            ACT.Relu, bias=nmr[:, tile], scale=rstd[:, tile])
                            last.then_inc(u_made.sem, 1)
                        for s in range(2):
                            act.wait_ge(y0_out.sem, y0_out.done(g, s + 1))
                            act.wait_ge(a1_mm.sem, a1_mm.done(g - 1, s + 1))
                            nc.scalar.activation(h1[:, s, :, :], y0[:, s, :, :], ACT.Relu).then_inc(h1_made.sem, 1)
                        for s in range(2):
                            act.wait_ge(y1_out.sem, y1_out.done(g, s + 1))
                            nc.scalar.activation(Hhi[:, bass.ds(g * (2 * UB) + s * UB, UB), 0:T], y1[:, s, :, :],
                                                 ACT.Relu).then_inc(hi_made.sem, 1)

                @block.tensor
                def _(pe):
                    for c in (a0_mm, w0_mm, a1_mm, w1_mm, sq_mm, tr_mm):
                        c.start(pe)
                    pe.wait_ge(const_made, 5)
                    pe.wait_ge(consts_loaded, 80)
                    pe.wait_ge(eig, 8)
                    for k in range(2):
                        last = nc.tensor.matmul(ps[:, 0, 0:T], ones[:], adjT[:, k, :], start=k == 0, stop=k == 1)
                    last.then_inc(eig, 1)
                    pe.wait_ge(eig, 10)

                    def product(lhs, sem, value):
                        for m in range(2):
                            for k in range(2):
                                last = nc.tensor.matmul(ps[:, PS_SQ, m * T:(m + 1) * T], lhs[:, k, m * P:(m + 1) * P],
                                                        M[:, k, :], start=k == 0, stop=k == 1)
                        last.then_inc(sem, value)

                    def squaring(n):
                        pe.wait_ge(m_made.sem, m_made.done(n - 1))
                        product(M, sq_mm.sem, 1)
                        pe.wait_ge(diag_made.sem, diag_made.done(n - 1))
                        pe.wait_ge(tr_used.sem, tr_used.done(n - 1))
                        nc.tensor.matmul(ps[:, PS_TR, 0:1], ones[:], diag[:], start=True,
                                         stop=True).then_inc(tr_mm.sem, 1)

                    def graph(src, s, bank):
                        for b in range(UB):
                            for k in range(2):
                                last = nc.tensor.matmul(ps[:, bank, b * T:(b + 1) * T], src[:, s, 2 * b + k, :],
                                                        adjT[:, k, :], start=k == 0, stop=k == 1)
                        return last

                    with pe.Fori(0, UNITS // 2) as g:
                        for s in range(2):
                            pe.wait_ge(u_made.sem, u_made.done(g, s + 1))
                            pe.wait_ge(y1_out.sem, y1_out.done(g - 1, s + 1))
                            graph(u, s, s).then_inc(a0_mm.sem, 1)
                        squaring(g * per_turn)
                        for s in range(2):
                            pe.wait_ge(a0_out.sem, a0_out.done(g, s + 1))
                            pe.wait_ge(y0_out.sem, y0_out.done(g - 1, s + 1))
                            for k in range(UT):
                                last = nc.tensor.matmul(ps[:, 2 + s, k * P:(k + 1) * P], A0[:, s, k * P:(k + 1) * P],
                                                        Wg[:, 0, :], start=True, stop=True)
                            last.then_inc(w0_mm.sem, 1)
                        for s in range(2):
                            pe.wait_ge(h1_made.sem, h1_made.done(g, s + 1))
                            pe.wait_ge(a1_out.sem, a1_out.done(g - 1, s + 1))
                            graph(h1, s, 4 + s).then_inc(a1_mm.sem, 1)
                        squaring(g * per_turn + 1)
                        for s in range(2):
                            pe.wait_ge(a1_out.sem, a1_out.done(g, s + 1))
                            nc.tensor.matmul(ps[:, s, :], Wg[:, 1, :], A1[:, s, :], start=True,
                                             stop=True).then_inc(w1_mm.sem, 1)
                    pe.wait_ge(m_made.sem, m_made.done(SQUARINGS - 1))
                    product(S, sq_mm.sem, 1)
                    pe.wait_ge(eig, 12)
                    nc.tensor.matmul(ps[:, PS_TR, 0:2], ones[:], quotient[:], start=True, stop=True).then_inc(eig, 1)

        with ExitStack() as ctx:
            names = ("gi", "gf", "gg", "go", "cell", "ig", "fc", "tc", "h32")
            buf = {n: sb(f"{n}_l", [P, LANES, 512], F32, ctx) for n in names}
            hhi = sb("hhi_l", [P, LANES, 512], F32R, ctx)
            hlo = sb("hlo_l", [P, LANES, 512], F32R, ctx)
            NSTEP = len(STEPS)
            RSTEP = recurrent(NSTEP)
            gate_mm = [[count(f"gate_mm{L}_{g}", RSTEP if g == F else NSTEP) for g in range(4)] for L in range(LANES)]
            gate_act = [[count(f"gate_act{L}_{g}", RSTEP if g == F else NSTEP) for g in range(4)] for L in range(LANES)]
            terms = [count(f"terms{L}", 2 * RSTEP) for L in range(LANES)]
            cell_made = [count(f"cell_made{L}", NSTEP) for L in range(LANES)]
            tanh_made = [count(f"tanh_made{L}", NSTEP) for L in range(LANES)]
            h_made = [count(f"h_made{L}", NSTEP) for L in range(LANES)]
            h_hi = [count(f"h_hi{L}", NSTEP) for L in range(LANES)]
            h_lo = [count(f"h_lo{L}", NSTEP) for L in range(LANES)]

            def width(n):
                return STEPS[n][2] * STEPS[n][3]

            def state(H, turn, L, n, t, windows):
                p, b0, nb, _, _ = STEPS[n]
                return H[:, bass.ds(turn * (LANES * LANE_B) + (L * LANE_B + b0), nb), t:t + (windows - 1) * p + 1:p]

            with nc.Block() as block:
                @block.tensor
                def _(pe):
                    for L in range(LANES):
                        for g in range(4):
                            gate_mm[L][g].start(pe)

                    def step(turn, L, n):
                        p, b0, nb, windows, t = STEPS[n]
                        N = width(n)
                        pe.wait_ge(gate_act[L][O].sem, gate_act[L][O].done(turn, n))
                        if t == 0 and last_writer(n):
                            pe.wait_ge(h_lo[L].sem, h_lo[L].done(turn, last_writer(n)))
                        xs = [state(H, turn, L, n, t, windows) for H in (Hhi, Hlo)]
                        hs = [H[:, L, 0:N] for H in (hhi, hlo)]
                        order = (I, G, F, O) if t else (I, G, O)
                        def mm(W, g, w, v, start=False, stop=False):
                            return nc.tensor.matmul(ps[:, 4 * L + g, 0:N], W[:, w, p - 1, g * P:(g + 1) * P], v,
                                                    start=start, stop=stop)
                        for g in order:
                            mm(WX, g, 0, xs[0], start=True)
                            mm(WX, g, 0, xs[1])
                            last = mm(WX, g, 1, xs[0], stop=t == 0)
                            if t == 0:
                                last.then_inc(gate_mm[L][g].sem, 1)
                        if t == 0:
                            return
                        pe.wait_ge(h_hi[L].sem, h_hi[L].done(turn, n))
                        for g in (I, G):
                            mm(WH, g, 0, hs[0])
                            mm(WH, g, 1, hs[0])
                        pe.wait_ge(h_lo[L].sem, h_lo[L].done(turn, n))
                        for g in (I, G):
                            mm(WH, g, 0, hs[1], stop=True).then_inc(gate_mm[L][g].sem, 1)
                        for g in (F, O):
                            mm(WH, g, 0, hs[0])
                            mm(WH, g, 1, hs[0])
                            mm(WH, g, 0, hs[1], stop=True).then_inc(gate_mm[L][g].sem, 1)

                    with pe.Fori(0, LSTM_TURNS) as turn:
                        for n in range(NSTEP):
                            for L in range(LANES):
                                step(turn, L, n)

                @block.scalar
                def _(act):
                    for L in range(LANES):
                        tanh_made[L].start(act)
                        for g in range(4):
                            gate_act[L][g].start(act)
                    dst = {I: "gi", F: "gf", G: "gg", O: "go"}

                    def step(turn, L, n):
                        p, b0, nb, windows, t = STEPS[n]
                        N = width(n)
                        act.wait_ge(cell_made[L].sem, cell_made[L].done(turn, n))
                        act.wait_ge(h_made[L].sem, h_made[L].done(turn, n))
                        for g in ((I, G, F, O) if t else (I, G, O)):
                            seen = recurrent(n + 1) if g == F else n + 1
                            act.wait_ge(gate_mm[L][g].sem, gate_mm[L][g].done(turn, seen))
                            a = nc.scalar.activation(buf[dst[g]][:, L, 0:N], ps[:, 4 * L + g, 0:N],
                                                     ACT.Tanh if g == G else ACT.Sigmoid,
                                                     bias=bias[:, 4 * (p - 1) + g:4 * (p - 1) + g + 1])
                            a.then_inc(gate_act[L][g].sem, 1)
                        act.wait_ge(cell_made[L].sem, cell_made[L].done(turn, n + 1))
                        nc.scalar.activation(buf["tc"][:, L, 0:N], buf["cell"][:, L, 0:N],
                                             ACT.Tanh).then_inc(tanh_made[L].sem, 1)

                    with act.Fori(0, LSTM_TURNS) as turn:
                        for n in range(NSTEP):
                            for L in range(LANES):
                                step(turn, L, n)

                @block.vector
                def _(dve):
                    for L in range(LANES):
                        for c in (terms, cell_made, h_made, h_hi, h_lo):
                            c[L].start(dve)

                    def step(turn, L, n):
                        p, b0, nb, windows, t = STEPS[n]
                        N = width(n)
                        v = {k: b[:, L, 0:N] for k, b in buf.items()}
                        dve.wait_ge(gate_act[L][G].sem, gate_act[L][G].done(turn, n + 1))
                        if t == 0:
                            dve.wait_ge(tanh_made[L].sem, tanh_made[L].done(turn, n))
                            nc.vector.tensor_tensor(v["cell"], v["gi"], v["gg"], ALU.mult).then_inc(cell_made[L].sem, 1)
                        else:
                            nc.vector.tensor_tensor(v["ig"], v["gi"], v["gg"], ALU.mult).then_inc(terms[L].sem, 1)
                            dve.wait_ge(gate_act[L][F].sem, gate_act[L][F].done(turn, recurrent(n + 1)))
                            nc.vector.tensor_tensor(v["fc"], v["gf"], v["cell"], ALU.mult).then_inc(terms[L].sem, 1)
                            dve.wait_ge(terms[L].sem, terms[L].done(turn, 2 * recurrent(n + 1)))
                            nc.vector.tensor_tensor(v["cell"], v["ig"], v["fc"], ALU.add).then_inc(cell_made[L].sem, 1)
                        dve.wait_ge(tanh_made[L].sem, tanh_made[L].done(turn, n + 1))
                        nc.vector.tensor_tensor(v["h32"], v["go"], v["tc"], ALU.mult).then_inc(h_made[L].sem, 1)
                        dve.wait_ge(h_made[L].sem, h_made[L].done(turn, n + 1))
                        if t < p - 1:
                            h, hi, lo = v["h32"], hhi[:, L, 0:N], hlo[:, L, 0:N]
                        else:
                            h = v["h32"].rearrange("p (b w) -> p b w", b=nb)[:, :, 0:T // p]
                            hi, lo = (state(H, turn, L, n, t, T // p) for H in (Hhi, Hlo))
                        nc.vector.tensor_copy(hi, h).then_inc(h_hi[L].sem, 1)
                        dve.wait_ge(h_hi[L].sem, h_hi[L].done(turn, n + 1))
                        nc.vector.tensor_tensor(lo, h, hi.bitcast(F32), ALU.subtract).then_inc(h_lo[L].sem, 1)

                    with dve.Fori(0, LSTM_TURNS) as turn:
                        for n in range(NSTEP):
                            for L in range(LANES):
                                step(turn, L, n)

        with ExitStack() as ctx:
            h32 = sb("h_sum", [P, 2, UB, T], F32, ctx)
            sum_made = count("sum_made", 2)
            h_turned = count("h_turned", 2)
            x_added = count("x_added", 2)
            with nc.Block() as block:
                @block.vector
                def _(dve):
                    sum_made.start(dve)
                    x_added.start(dve)
                    with dve.Fori(0, UNITS // 2) as g:
                        for s in range(2):
                            b = bass.ds(g * (2 * UB) + s * UB, UB)
                            dve.wait_ge(h_turned.sem, h_turned.done(g - 1, s + 1))
                            nc.vector.tensor_tensor(h32[:, s, :, :], Hhi[:, b, 0:T].bitcast(F32),
                                                    Hlo[:, b, 0:T].bitcast(F32), ALU.add).then_inc(sum_made.sem, 1)
                        for s in range(2):
                            dve.wait_ge(h_turned.sem, h_turned.done(g, s + 1))
                            tiles = X[:, bass.ds(g * (2 * UT) + s * UT, UT), :]
                            nc.vector.tensor_tensor(tiles, ps[:, s, :].rearrange("p (a b) -> p a b", a=UT), tiles,
                                                    ALU.add).then_inc(x_added.sem, 1)
                            dve.wait_ge(x_added.sem, x_added.done(g, s + 1))
                            for k in range(UT):
                                tile = bass.ds(g * (2 * UT) + (s * UT + k), 1)
                                nc.vector.bn_stats(bn[:, tile, :].rearrange("p a b -> p (a b)"),
                                                   X[:, tile, :].rearrange("p a b -> p (a b)")).then_inc(bn_made, 1)
                    dve.wait_ge(bn_made, 2 * TILES)
                    layernorm_stats(dve, None, 8)

                @block.scalar
                def _(act):
                    layernorm_stats(None, act, 8)

                @block.tensor
                def _(pe):
                    h_turned.start(pe)
                    with pe.Fori(0, UNITS // 2) as g:
                        for s in range(2):
                            pe.wait_ge(sum_made.sem, sum_made.done(g, s + 1))
                            pe.wait_ge(x_added.sem, x_added.done(g - 1, s + 1))
                            for k in range(UT):
                                last = nc.tensor.transpose(
                                    ps[:, s, k * P:(k + 1) * P],
                                    h32[:, s, k // 2, (k % 2) * P:(k % 2 + 1) * P], ident)
                            last.then_inc(h_turned.sem, 1)
        lstm_ctx.close()

        X2 = sb("X2", [P, TILES, D])
        X2T = sb("X2T", [P, NB * T])
        W1 = sb("W1", [P, HID])
        W2 = sb("W2", [P, 2, D])
        late_loaded = sem("late_loaded")
        with ExitStack() as ctx:
            Wc, Wq, Wk, Wv, Wo = (sb(n, [P, D], F32, ctx) for n in ("Wc", "Wq", "Wk", "Wv", "Wo"))
            u = sb("u1", [P, 2, UT, D], F32, ctx)
            xpT = sb("xpT", [P, UW], F32, ctx)
            t1 = sb("t1", [P, UT, D], F32, ctx)
            z1 = sb("z1", [P, UT, D], F32, ctx)
            x1 = sb("x1", [P, UT, D], F32, ctx)
            x1b = sb("x1b", [P, 2, UT, D], F32, ctx)
            x1T = sb("x1T", [P, 2, UW], F32, ctx)
            bn1 = sb("bn1", [P, 2, UT, 6], F32, ctx)
            mo1 = sb("mo1", [P, 2, 6, UT], F32, ctx)
            ve1 = sb("ve1", [P, 2, UT], F32, ctx)
            rs1 = sb("rs1", [P, 2, UT], F32, ctx)
            qT = sb("qT", [P, UW], F32, ctx)
            kT = sb("kT", [P, UW], F32, ctx)
            V1 = sb("V1", [P, UT, HEADS, HD + 1], F32, ctx)
            negmax = sb("negmax", [P, 2, HEADS], F32, ctx)
            prob = sb("prob", [P, 2, HEADS, T], F32, ctx)
            probT = sb("probT", [P, 2, 2 * HEADS, P], F32, ctx)
            rden = sb("rden", [P, HEADS], F32, ctx)
            o_sb = sb("o_sb", [P, UT, D], F32, ctx)
            oT = sb("oT", [P, UW], F32, ctx)
            y2 = sb("y2", [P, UT, D], F32, ctx)
            z2 = sb("z2", [P, UT, D], F32, ctx)
            x2 = sb("x2", [P, UT, D], F32, ctx)

            u1_made = count("u1_made")
            xp_mm = count("xp_mm")
            xp_out = count("xp_out")
            wc_mm = count("wc_mm")
            t1_out = count("t1_out")
            ln_stats = [count("ln1_stats", 4), count("ln2_stats", 4)]
            ln_rstd = [count("ln1_rstd", 2), count("ln2_rstd", 2)]
            z_made = [count("z1_made"), count("z2_made")]
            zg_made = [count("zg1_made"), count("zg2_made")]
            zb_made = [count("zb1_made"), count("zb2_made")]
            x1_made = count("x1_made")
            x1b_made = count("x1b_made")
            x1T_mm = count("x1T_mm")
            x1T_out = count("x1T_out")
            q_mm = count("q_mm")
            k_mm = count("k_mm")
            v_mm = count("v_mm")
            q_out = count("q_out")
            k_out = count("k_out")
            v_out = count("v_out")
            s_half = count("s_half", UT)
            s_mm = count("s_mm", UT)
            max_made = count("max_made", UT)
            exp_made = count("exp_made", UT)
            pT_mm = count("pT_mm", 2 * UT)
            pT_act = count("pT_act", UT)
            pT_dve = count("pT_dve", UT)
            o_mm = count("o_mm", UT)
            rden_made = count("rden_made", UT)
            o_out = count("o_out", UT)
            oT_mm = count("oT_mm")
            oT_out = count("oT_out")
            wo_mm = count("wo_mm")
            y2_out = count("y2_out")
            x2_kept = count("x2_kept")
            x2T_mm = count("x2T_mm")
            x2T_out = count("x2T_out")
            v_ones = sem("v_ones")
            att_loaded = sem("att_loaded")
            PS_T, PS_O, PS_G = 4, 6, 7

            def scores(s):
                return ps[:, 2 * (s % 2):2 * (s % 2) + 2, :].rearrange("p a (b c) -> p (a b) c", b=2)

            def head(j):
                return j // 2 + 2 * (j % 2)

            def walk(engine, body):
                body(0, 0, True, True)
                with engine.Fori(0, UNITS // 2 - 1) as g:
                    body(g * 2 + 1, 1, False, True)
                    body(g * 2 + 2, 0, False, True)
                body(UNITS - 1, 1, False, False)

            with nc.Block() as block:
                @block.sync
                def _(sp):
                    for W, n in ((Wc, "Wc"), (Wq, "Wq"), (Wk, "Wk"), (Wv, "Wv"), (Wo, "Wo")):
                        sp.dma_start(W[:], d[n]).then_inc(att_loaded, 16)
                    sp.dma_start(W1[:], d["W1"]).then_inc(late_loaded, 16)
                    sp.dma_start(W2[:], d["W2"]).then_inc(late_loaded, 16)

                @block.gpsimd
                def _(pool):
                    for c in (*ln_rstd, *zg_made, *zb_made, x1b_made):
                        c.start(pool)
                    nc.gpsimd.memset(V1[:, :, :, HD:HD + 1], 1.0).then_inc(v_ones, 1)

                    def norm(n, unit, z, gain, shift, dst):
                        pool.wait_ge(ln_stats[n].sem, ln_stats[n].done(unit))
                        nc.gpsimd.tensor_tensor(ve1[:, n, :], mo1[:, n, VAR, :], eps[:],
                                                ALU.add).then_inc(ln_rstd[n].sem, 1)
                        pool.wait_ge(ln_rstd[n].sem, ln_rstd[n].done(unit, 1))
                        nc.gpsimd.tensor_tensor(rs1[:, n, :], ve1[:, n, :], minus_half[:],
                                                ALU.pow).then_inc(ln_rstd[n].sem, 1)
                        pool.wait_ge(z_made[n].sem, z_made[n].done(unit))
                        nc.gpsimd.tensor_tensor(z[:], z[:], row(gain), ALU.mult).then_inc(zg_made[n].sem, 1)
                        pool.wait_ge(zg_made[n].sem, zg_made[n].done(unit))
                        nc.gpsimd.tensor_tensor(dst[:], z[:], row(shift), ALU.add).then_inc(zb_made[n].sem, 1)

                    def front(unit, par):
                        norm(0, unit, z1, G1, BE1, z1)
                        pool.wait_ge(x1_made.sem, x1_made.done(unit))
                        pool.wait_ge(y2_out.sem, y2_out.done(unit - 2))
                        nc.gpsimd.tensor_tensor(x1b[:, par, :, :], x1[:], row(BO), ALU.add).then_inc(x1b_made.sem, 1)

                    def back(unit):
                        pool.wait_ge(x2T_mm.sem, x2T_mm.done(unit - 1))
                        pool.wait_ge(x2_kept.sem, x2_kept.done(unit - 1))
                        norm(1, unit, z2, G2, BE2, x2)

                    def body(unit, par, first, more):
                        if not first:
                            back(unit - 1)
                        if more:
                            front(unit + 1, 1 - par)

                    front(0, 0)
                    walk(pool, body)
                    back(UNITS - 1)

                @block.scalar
                def _(act):
                    for c in (u1_made, x1T_out, q_out, exp_made, pT_act, oT_out, x2T_out):
                        c.start(act)

                    def make_u(unit, par):
                        act.wait_ge(x1_made.sem, x1_made.done(unit - 2))
                        for k in range(UT):
                            tile = bass.ds(unit * UT + k, 1)
                            last = nc.scalar.activation(u[:, par, k, :], X[:, tile, :].rearrange("p a b -> p (a b)"),
                                                        ACT.Relu, bias=nmr[:, tile], scale=rstd[:, tile])
                        last.then_inc(u1_made.sem, 1)

                    def turn_x1(unit, par):
                        act.wait_ge(x1T_mm.sem, x1T_mm.done(unit))
                        act.wait_ge(v_mm.sem, v_mm.done(unit - 2))
                        nc.scalar.activation(x1T[:, par, :], ps[:, PS_G, :], ACT.Copy).then_inc(x1T_out.sem, 1)

                    def turn_o(unit):
                        act.wait_ge(oT_mm.sem, oT_mm.done(unit))
                        act.wait_ge(wo_mm.sem, wo_mm.done(unit - 1))
                        nc.scalar.activation(oT[:], ps[:, PS_G, :], ACT.Copy).then_inc(oT_out.sem, 1)

                    def turn_x2(unit):
                        act.wait_ge(x2T_mm.sem, x2T_mm.done(unit))
                        nc.scalar.activation(X2T[:, bass.ds(unit * UW, UW)], ps[:, PS_G, :],
                                             ACT.Copy).then_inc(x2T_out.sem, 1)

                    def exps(unit, s):
                        act.wait_ge(max_made.sem, max_made.done(unit, s + 1))
                        act.wait_ge(pT_mm.sem, pT_mm.done(unit, 2 * (s - 1)))
                        for h in range(HEADS):
                            last = nc.scalar.activation(prob[:, s % 2, h, :], scores(s)[:, h, :], ACT.Exp,
                                                        bias=negmax[:, s % 2, h:h + 1])
                        last.then_inc(exp_made.sem, 1)

                    def turn_p(unit, s):
                        act.wait_ge(pT_mm.sem, pT_mm.done(unit, 2 * s + 1))
                        act.wait_ge(o_mm.sem, o_mm.done(unit, s - 1))
                        nc.scalar.activation(probT[:, s % 2, 0:HEADS, :].rearrange("p a b -> p (a b)"), ps[:, PS_T, :],
                                             ACT.Copy).then_inc(pT_act.sem, 1)

                    def body(unit, par, first, more):
                        act.wait_ge(q_mm.sem, q_mm.done(unit))
                        act.wait_ge(s_mm.sem, s_mm.done(unit - 1))
                        nc.scalar.activation(qT[:], ps[:, 0, :], ACT.Copy, scale=HD ** -0.5).then_inc(q_out.sem, 1)
                        if more:
                            make_u(unit + 1, 1 - par)
                        exps(unit, 0)
                        if not first:
                            turn_o(unit - 1)
                        exps(unit, 1)
                        turn_p(unit, 0)
                        exps(unit, 2)
                        turn_p(unit, 1)
                        exps(unit, 3)
                        turn_p(unit, 2)
                        if more:
                            turn_x1(unit + 1, 1 - par)
                        turn_p(unit, 3)
                        if not first:
                            turn_x2(unit - 1)

                    make_u(0, 0)
                    turn_x1(0, 0)
                    walk(act, body)
                    turn_o(UNITS - 1)
                    turn_x2(UNITS - 1)

                @block.vector
                def _(dve):
                    for c in (xp_out, t1_out, *ln_stats, *z_made, x1_made, k_out, v_out, max_made, pT_dve, rden_made,
                              o_out, y2_out, x2_kept):
                        c.start(dve)

                    def moments(n, unit, src):
                        for k in range(UT):
                            last = nc.vector.bn_stats(bn1[:, n, k, :], src[:, k, :])
                        last.then_inc(ln_stats[n].sem, 1)
                        dve.wait_ge(ln_stats[n].sem, ln_stats[n].done(unit, 1))
                        moments_of(dve, bn1[:, n, :, :], mo1[:, n, :, :], ln_stats[n], unit, 1)

                    def normalise(n, unit, src, z):
                        dve.wait_ge(ln_rstd[n].sem, ln_rstd[n].done(unit))
                        for k in range(UT):
                            last = nc.vector.tensor_scalar(z[:, k, :], src[:, k, :], mo1[:, n, MEAN, k:k + 1],
                                                           rs1[:, n, k:k + 1], ALU.subtract, ALU.mult)
                        last.then_inc(z_made[n].sem, 1)

                    def xp(unit):
                        dve.wait_ge(xp_mm.sem, xp_mm.done(unit))
                        dve.wait_ge(wc_mm.sem, wc_mm.done(unit - 1))
                        nc.vector.tensor_copy(xpT[:], ps[:, PS_G, :]).then_inc(xp_out.sem, 1)

                    def conv(unit):
                        dve.wait_ge(wc_mm.sem, wc_mm.done(unit))
                        nc.vector.tensor_tensor(t1[:], ps[:, PS_G, :].rearrange("p (a b) -> p a b", a=UT), row(BC),
                                                ALU.add).then_inc(t1_out.sem, 1)
                        dve.wait_ge(t1_out.sem, t1_out.done(unit))
                        moments(0, unit, t1)

                    def make_x1(unit, par):
                        dve.wait_ge(zb_made[0].sem, zb_made[0].done(unit))
                        dve.wait_ge(x1T_mm.sem, x1T_mm.done(unit - 1))
                        dve.wait_ge(x1b_made.sem, x1b_made.done(unit - 1))
                        nc.vector.scalar_tensor_tensor(x1[:].rearrange("p a b -> p (a b)"),
                                                       z1[:].rearrange("p a b -> p (a b)"), 0.0,
                                                       u[:, par, :, :].rearrange("p a b -> p (a b)"),
                                                       ALU.max, ALU.add).then_inc(x1_made.sem, 1)

                    def row_max(unit, s):
                        dve.wait_ge(s_mm.sem, s_mm.done(unit, s + 1))
                        dve.wait_ge(exp_made.sem, exp_made.done(unit, s - 1))
                        nc.vector.tensor_reduce(negmax[:, s % 2, :], scores(s), AX.X, ALU.max,
                                                negate=True).then_inc(max_made.sem, 1)

                    def turn_p(unit, s):
                        dve.wait_ge(pT_mm.sem, pT_mm.done(unit, 2 * s + 2))
                        dve.wait_ge(o_mm.sem, o_mm.done(unit, s - 1))
                        nc.vector.tensor_copy(probT[:, s % 2, HEADS:, :].rearrange("p a b -> p (a b)"),
                                              ps[:, PS_T + 1, :]).then_inc(pT_dve.sem, 1)

                    def make_o(unit, s):
                        dve.wait_ge(o_mm.sem, o_mm.done(unit, s + 1))
                        acc = ps[:, PS_O, 0:HEADS * (HD + 1)].rearrange("p (h c) -> p h c", h=HEADS)
                        nc.vector.reciprocal(rden[:].unsqueeze(2), acc[:, :, HD:HD + 1]).then_inc(rden_made.sem, 1)
                        dve.wait_ge(rden_made.sem, rden_made.done(unit, s + 1))
                        dve.wait_ge(oT_mm.sem, oT_mm.done(unit - 1))
                        nc.vector.tensor_tensor(o_sb[:, s, :].rearrange("p (h c) -> p h c", h=HEADS), acc[:, :, 0:HD],
                                                rden[:].unsqueeze(2).broadcast_to([P, HEADS, HD]),
                                                ALU.mult).then_inc(o_out.sem, 1)

                    def add_o(unit, par):
                        dve.wait_ge(wo_mm.sem, wo_mm.done(unit))
                        dve.wait_ge(x1b_made.sem, x1b_made.done(unit))
                        nc.vector.tensor_tensor(y2[:], ps[:, PS_O, :].rearrange("p (a b) -> p a b", a=UT),
                                                x1b[:, par, :, :], ALU.add).then_inc(y2_out.sem, 1)
                        dve.wait_ge(y2_out.sem, y2_out.done(unit))
                        moments(1, unit, y2)

                    def keep_x2(unit):
                        dve.wait_ge(zb_made[1].sem, zb_made[1].done(unit))
                        nc.vector.tensor_copy(X2[:, bass.ds(unit * UT, UT), :], x2[:]).then_inc(x2_kept.sem, 1)

                    def body(unit, par, first, more):
                        dve.wait_ge(k_mm.sem, k_mm.done(unit))
                        dve.wait_ge(s_mm.sem, s_mm.done(unit - 1))
                        nc.vector.tensor_copy(kT[:], ps[:, 1, :]).then_inc(k_out.sem, 1)
                        dve.wait_ge(v_mm.sem, v_mm.done(unit))
                        dve.wait_ge(o_mm.sem, o_mm.done(unit - 1))
                        for k in range(UT):
                            last = nc.vector.tensor_copy(
                                V1[:, k, :, 0:HD],
                                ps[:, 2, k * D:(k + 1) * D].rearrange("p (h c) -> p h c", h=HEADS))
                        last.then_inc(v_out.sem, 1)
                        row_max(unit, 0)
                        row_max(unit, 1)
                        if not first:
                            add_o(unit - 1, 1 - par)
                        turn_p(unit, 0)
                        if more:
                            xp(unit + 1)
                        row_max(unit, 2)
                        make_o(unit, 0)
                        turn_p(unit, 1)
                        if not first:
                            normalise(1, unit - 1, y2, z2)
                        if more:
                            conv(unit + 1)
                        row_max(unit, 3)
                        make_o(unit, 1)
                        if more:
                            normalise(0, unit + 1, t1, z1)
                        turn_p(unit, 2)
                        if more:
                            make_x1(unit + 1, 1 - par)
                        if not first:
                            keep_x2(unit - 1)
                        make_o(unit, 2)
                        turn_p(unit, 3)
                        make_o(unit, 3)

                    xp(0)
                    conv(0)
                    normalise(0, 0, t1, z1)
                    make_x1(0, 0)
                    dve.wait_ge(v_ones, 1)
                    walk(dve, body)
                    add_o(UNITS - 1, 1)
                    normalise(1, UNITS - 1, y2, z2)
                    keep_x2(UNITS - 1)

                @block.tensor
                def _(pe):
                    for c in (s_half, xp_mm, wc_mm, x1T_mm, q_mm, k_mm, v_mm, s_mm, pT_mm, o_mm, oT_mm, wo_mm, x2T_mm):
                        c.start(pe)
                    pe.wait_ge(att_loaded, 80)

                    def xp(unit, par):
                        pe.wait_ge(u1_made.sem, u1_made.done(unit))
                        pe.wait_ge(oT_out.sem, oT_out.done(unit - 2))
                        for b in range(UB):
                            for k in range(2):
                                last = nc.tensor.matmul(ps[:, PS_G, b * T:(b + 1) * T], u[:, par, 2 * b + k, :],
                                                        LT[:, k, :], start=k == 0, stop=k == 1)
                        last.then_inc(xp_mm.sem, 1)

                    def conv(unit):
                        pe.wait_ge(xp_out.sem, xp_out.done(unit))
                        for k in range(UT):
                            last = nc.tensor.matmul(ps[:, PS_G, k * P:(k + 1) * P], xpT[:, k * P:(k + 1) * P], Wc[:],
                                                    start=True, stop=True)
                        last.then_inc(wc_mm.sem, 1)

                    def turn(src, unit, sem):
                        for k in range(UT):
                            last = nc.tensor.transpose(ps[:, PS_G, k * P:(k + 1) * P], src[:, k, :], ident)
                        last.then_inc(sem, 1)

                    def turn_x1(unit):
                        pe.wait_ge(x1_made.sem, x1_made.done(unit))
                        turn(x1, unit, x1T_mm.sem)

                    def turn_o(unit):
                        pe.wait_ge(o_out.sem, o_out.done(unit))
                        pe.wait_ge(x2T_out.sem, x2T_out.done(unit - 1))
                        pe.wait_ge(x1T_out.sem, x1T_out.done(unit))
                        turn(o_sb, unit, oT_mm.sem)

                    def out_proj(unit):
                        pe.wait_ge(oT_out.sem, oT_out.done(unit))
                        for k in range(UT):
                            last = nc.tensor.matmul(ps[:, PS_O, k * P:(k + 1) * P], oT[:, k * P:(k + 1) * P], Wo[:],
                                                    start=True, stop=True)
                        last.then_inc(wo_mm.sem, 1)

                    def turn_x2(unit):
                        pe.wait_ge(zb_made[1].sem, zb_made[1].done(unit))
                        turn(x2, unit, x2T_mm.sem)

                    def qkv(unit, par):
                        pe.wait_ge(x1T_out.sem, x1T_out.done(unit))
                        pe.wait_ge(exp_made.sem, exp_made.done(unit - 1))
                        nc.tensor.matmul(ps[:, 0, :], Wq[:], x1T[:, par, :], start=True, stop=True)\
                            .then_inc(q_mm.sem, 1)
                        nc.tensor.matmul(ps[:, 1, :], Wk[:], x1T[:, par, :], start=True, stop=True)\
                            .then_inc(k_mm.sem, 1)
                        for k in range(UT):
                            last = nc.tensor.matmul(ps[:, 2, k * P:(k + 1) * P], x1T[:, par, k * P:(k + 1) * P], Wv[:],
                                                    start=True, stop=True)
                        last.then_inc(v_mm.sem, 1)

                    def score(unit, s):
                        if s == 0:
                            pe.wait_ge(q_out.sem, q_out.done(unit))
                            pe.wait_ge(k_out.sem, k_out.done(unit))
                        if s == 1:
                            pe.wait_ge(v_out.sem, v_out.done(unit))
                        pe.wait_ge(exp_made.sem, exp_made.done(unit, s - 1))
                        b, qt = divmod(s, 2)
                        for half in range(2):
                            for bank in range(2):
                                nc.tensor.matmul(scores(s)[:, 2 * bank + half, :], identb[:], maskb[:, qt, :],
                                                 start=True, stop=False)
                            for bank in range(2):
                                j = 2 * bank + half
                                rows_h = slice(head(j) * HD, (head(j) + 1) * HD)
                                last = nc.tensor.matmul(scores(s)[:, j, :], qT[rows_h, s * P:(s + 1) * P],
                                                        kT[rows_h, b * T:(b + 1) * T], start=False, stop=True)
                            if half == 0:
                                last.then_inc(s_half.sem, 1)
                                pe.wait_ge(s_half.sem, s_half.done(unit, s + 1))
                        last.then_inc(s_mm.sem, 1)

                    def turn_p(unit, s):
                        pe.wait_ge(exp_made.sem, exp_made.done(unit, s + 1))
                        pe.wait_ge(pT_act.sem, pT_act.done(unit, s))
                        pe.wait_ge(pT_dve.sem, pT_dve.done(unit, s))
                        for h in range(HEADS):
                            for k in range(2):
                                at = (h % 2 * 2 + k) * P
                                last = nc.tensor.transpose(ps[:, PS_T + h // 2, at:at + P],
                                                           prob[:, s % 2, h, k * P:(k + 1) * P], ident)
                            if h % 2:
                                last.then_inc(pT_mm.sem, 1)

                    def weigh_v(unit, s):
                        pe.wait_ge(pT_act.sem, pT_act.done(unit, s + 1))
                        pe.wait_ge(pT_dve.sem, pT_dve.done(unit, s + 1))
                        pe.wait_ge(o_out.sem, o_out.done(unit, s))
                        if s == 0:
                            pe.wait_ge(y2_out.sem, y2_out.done(unit - 1))
                        for j in range(HEADS):
                            h = head(j)
                            for k in range(2):
                                last = nc.tensor.matmul(ps[:, PS_O, h * (HD + 1):(h + 1) * (HD + 1)],
                                                        probT[:, s % 2, 2 * j + k, :], V1[:, s // 2 * 2 + k, h, :],
                                                        start=k == 0, stop=k == 1)
                        last.then_inc(o_mm.sem, 1)

                    def body(unit, par, first, more):
                        qkv(unit, par)
                        score(unit, 0)
                        if not first:
                            turn_o(unit - 1)
                        score(unit, 1)
                        if not first:
                            out_proj(unit - 1)
                        turn_p(unit, 0)
                        if more:
                            xp(unit + 1, 1 - par)
                        score(unit, 2)
                        weigh_v(unit, 0)
                        turn_p(unit, 1)
                        if more:
                            conv(unit + 1)
                        score(unit, 3)
                        weigh_v(unit, 1)
                        turn_p(unit, 2)
                        weigh_v(unit, 2)
                        if more:
                            turn_x1(unit + 1)
                        turn_p(unit, 3)
                        if not first:
                            if more:
                                pe.wait_ge(x1T_out.sem, x1T_out.done(unit + 1))
                            turn_x2(unit - 1)
                        weigh_v(unit, 3)

                    xp(0, 0)
                    conv(0)
                    pe.wait_ge(t1_out.sem, t1_out.done(0))
                    turn_x1(0)
                    walk(pe, body)
                    turn_o(UNITS - 1)
                    out_proj(UNITS - 1)
                    turn_x2(UNITS - 1)

        with ExitStack() as ctx:
            hid = sb("hid", [P, 2, 2, UW], F32, ctx)
            x2b = sb("x2b", [P, 2, UT, D], F32, ctx)
            y3 = sb("y3", [P, 2, UT, D], F32, ctx)
            z3 = sb("z3", [P, 2, UT, D], F32, ctx)
            xr = sb("xr", [P, 2, UT, D], F32, ctx)
            res = sb("res", [P, 2, UT, D], F32, ctx)
            bn3 = sb("bn3", [P, 2, UT, 6], F32, ctx)
            mo3 = sb("mo3", [P, 2, 6, UT], F32, ctx)
            ve3 = sb("ve3", [P, 2, UT], F32, ctx)
            rs3 = sb("rs3", [P, 2, UT], F32, ctx)
            hid_mm = count("hid_mm", 4)
            gelu_made = count("gelu_made", 4)
            m_mm = count("m_mm", 2)
            x2b_made = count("x2b_made", 2)
            xr_made = count("xr_made", 2)
            y3_out = count("y3_out", 2)
            st3 = count("st3", 8)
            rs3_made = count("rs3_made", 4)
            z3_made = count("z3_made", 2)
            zg3_made = count("zg3_made", 2)
            res_made = count("res_made", 2)
            stored = [count(f"stored{s}", 16) for s in range(2)]

            with nc.Block() as block:
                @block.sync
                def _(sp):
                    for s in range(2):
                        stored[s].start(sp)
                    with sp.Fori(0, UNITS // 2) as g:
                        for s in range(2):
                            sp.wait_ge(res_made.sem, res_made.done(g, s + 1))
                            sp.dma_start(out[:, bass.ds(g * (2 * UT) + s * UT, UT), :],
                                         res[:, s, :, :]).then_inc(stored[s].sem, 16)
                    for s in range(2):
                        sp.wait_ge(stored[s].sem, stored[s].done(UNITS // 2 - 1))

                @block.tensor
                def _(pe):
                    hid_mm.start(pe)
                    m_mm.start(pe)
                    pe.wait_ge(late_loaded, 32)
                    with pe.Fori(0, UNITS // 2) as g:
                        for s in range(2):
                            for j in range(2):
                                pe.wait_ge(gelu_made.sem, gelu_made.done(g - 1, 2 * s + j + 1))
                                nc.tensor.matmul(ps[:, 2 * s + j, :], W1[:, j * P:(j + 1) * P],
                                                 X2T[:, bass.ds(g * (2 * UW) + s * UW, UW)], start=True,
                                                 stop=True).then_inc(hid_mm.sem, 1)
                        for s in range(2):
                            pe.wait_ge(gelu_made.sem, gelu_made.done(g, 2 * s + 2))
                            pe.wait_ge(y3_out.sem, y3_out.done(g - 1, s + 1))
                            for k in range(UT):
                                for j in range(2):
                                    last = nc.tensor.matmul(ps[:, 4 + s, k * P:(k + 1) * P],
                                                            hid[:, s, j, k * P:(k + 1) * P], W2[:, j, :],
                                                            start=j == 0, stop=j == 1)
                            last.then_inc(m_mm.sem, 1)

                @block.scalar
                def _(act):
                    gelu_made.start(act)
                    with act.Fori(0, UNITS // 2) as g:
                        for s in range(2):
                            act.wait_ge(m_mm.sem, m_mm.done(g - 1, s + 1))
                            for j in range(2):
                                act.wait_ge(hid_mm.sem, hid_mm.done(g, 2 * s + j + 1))
                                nc.scalar.activation(hid[:, s, j, :], ps[:, 2 * s + j, :], ACT.Gelu,
                                                     bias=cols[:, 1 + j:2 + j]).then_inc(gelu_made.sem, 1)

                @block.gpsimd
                def _(pool):
                    for c in (x2b_made, xr_made, rs3_made, zg3_made):
                        c.start(pool)
                    with pool.Fori(0, UNITS // 2) as g:
                        for s in range(2):
                            tiles = bass.ds(g * (2 * UT) + s * UT, UT)
                            pool.wait_ge(y3_out.sem, y3_out.done(g - 1, s + 1))
                            nc.gpsimd.tensor_tensor(x2b[:, s, :, :], X2[:, tiles, :], row(B2),
                                                    ALU.add).then_inc(x2b_made.sem, 1)
                            pool.wait_ge(res_made.sem, res_made.done(g - 1, s + 1))
                            nc.gpsimd.tensor_tensor(xr[:, s, :, :], X[:, tiles, :], row(BE3),
                                                    ALU.add).then_inc(xr_made.sem, 1)
                        for s in range(2):
                            pool.wait_ge(st3.sem, st3.done(g, 4 * s + 4))
                            nc.gpsimd.tensor_tensor(ve3[:, s, :], mo3[:, s, VAR, :], eps[:],
                                                    ALU.add).then_inc(rs3_made.sem, 1)
                            pool.wait_ge(rs3_made.sem, rs3_made.done(g, 2 * s + 1))
                            nc.gpsimd.tensor_tensor(rs3[:, s, :], ve3[:, s, :], minus_half[:],
                                                    ALU.pow).then_inc(rs3_made.sem, 1)
                            pool.wait_ge(z3_made.sem, z3_made.done(g, s + 1))
                            nc.gpsimd.tensor_tensor(z3[:, s, :, :], z3[:, s, :, :], row(G3),
                                                    ALU.mult).then_inc(zg3_made.sem, 1)

                @block.vector
                def _(dve):
                    for c in (y3_out, st3, z3_made, res_made):
                        c.start(dve)
                    with dve.Fori(0, UNITS // 2) as g:
                        for s in range(2):
                            dve.wait_ge(m_mm.sem, m_mm.done(g, s + 1))
                            dve.wait_ge(x2b_made.sem, x2b_made.done(g, s + 1))
                            nc.vector.tensor_tensor(y3[:, s, :, :],
                                                    ps[:, 4 + s, :].rearrange("p (a b) -> p a b", a=UT),
                                                    x2b[:, s, :, :], ALU.add).then_inc(y3_out.sem, 1)
                            dve.wait_ge(y3_out.sem, y3_out.done(g, s + 1))
                            for k in range(UT):
                                last = nc.vector.bn_stats(bn3[:, s, k, :], y3[:, s, k, :])
                            last.then_inc(st3.sem, 1)
                            dve.wait_ge(st3.sem, st3.done(g, 4 * s + 1))
                            moments_of(dve, bn3[:, s, :, :], mo3[:, s, :, :], st3, g, 4 * s + 1)
                        for s in range(2):
                            dve.wait_ge(rs3_made.sem, rs3_made.done(g, 2 * s + 2))
                            for k in range(UT):
                                last = nc.vector.tensor_scalar(z3[:, s, k, :], y3[:, s, k, :], mo3[:, s, MEAN, k:k + 1],
                                                               rs3[:, s, k:k + 1], ALU.subtract, ALU.mult)
                            last.then_inc(z3_made.sem, 1)
                        for s in range(2):
                            dve.wait_ge(zg3_made.sem, zg3_made.done(g, s + 1))
                            dve.wait_ge(xr_made.sem, xr_made.done(g, s + 1))
                            dve.wait_ge(stored[s].sem, stored[s].done(g - 1))
                            nc.vector.tensor_tensor(res[:, s, :, :], z3[:, s, :, :], xr[:, s, :, :],
                                                    ALU.add).then_inc(res_made.sem, 1)


def kernel(**inputs):
    import numpy as np
    import concourse.bacc as bacc
    from concourse.bass_utils import run_bass_kernel_spmd

    a = {k: np.asarray(v) for k, v in inputs.items()}

    def halves(m):
        return m.reshape(2, P, -1).transpose(1, 0, 2)

    def lstm(m):
        return m.transpose(2, 0, 1).reshape(D, -1)

    def lstm_bias(m):
        return m.reshape(MAX_SKIP * 4, D).T

    n0, n1 = "L0_gnn_", "L1_gnn_"
    arrays = {
        "x": a["x"].reshape(TILES, P, D).transpose(1, 0, 2),
        "adj": halves(a["adj"]),
        "adjT": halves(a["adj"].T),
        "Wg": np.stack([a[n0 + "Wg0"], a[n0 + "Wg1"]], 1),
        "bg0": a[n0 + "bg0"][None],
        "Wih": lstm(a[n0 + "Wih"]),
        "Whh": lstm(a[n0 + "Whh"]),
        "lstm_b": np.stack([lstm_bias(a[n0 + "bih"]), lstm_bias(a[n0 + "bhh"])], 1),
        "rows": np.stack([a[n1 + k] for k in ("bc", "g1", "be1", "bo", "g2", "be2", "b2", "g3", "be3")]),
        "cols": np.stack([a[n0 + "bg1"], *a[n1 + "b1"].reshape(2, D)], 1),
        "Wc": a[n1 + "Wc"], "Wq": a[n1 + "Wq"], "Wk": a[n1 + "Wk"], "Wv": a[n1 + "Wv"], "Wo": a[n1 + "Wo"],
        "W1": a[n1 + "W1"], "W2": halves(a[n1 + "W2"]),
    }
    arrays = {k: np.ascontiguousarray(v) for k, v in arrays.items()}
    nc = bacc.Bacc("TRN2", target_bir_lowering=False, num_devices=1)
    d = {k: nc.dram_tensor(f"in_{k}", v.shape, F32, kind="ExternalInput").ap() for k, v in arrays.items()}
    out = nc.dram_tensor("out", (P, TILES, D), F32, kind="ExternalOutput").ap()
    build(nc, d, out)
    r = run_bass_kernel_spmd(nc, [{f"in_{k}": v for k, v in arrays.items()}], core_ids=[0])
    return r.results[0]["out"].transpose(1, 0, 2).reshape(NB, T, D)
```

```python
from contextlib import ExitStack

import concourse.bass as bass
from concourse import mybir

F32 = mybir.dt.float32
F32R = mybir.dt.float32r
BF16 = mybir.dt.bfloat16
F16 = mybir.dt.float16
ALU = mybir.AluOpType
ACT = mybir.ActivationFunctionType
AX = mybir.AxisListType
RMAX = bass.bass_isa.ReduceOp.max

P = 128
NB, T, D = 32, 256, 128
TILES = NB * T // P
UB = 2
UT = UB * T // P
UW = UB * T
UNITS = NB // UB
CHUNK = 8
EPS = 1e-5
SQUARINGS = 16
MAX_SKIP = 4
HS = T + 2
HEADS, HD = 4, 32
HID = 256
SCALE = HD ** -0.5
MASKED = -(2.0 ** 100)
I, F, G, O = range(4)

LANE_B = 8
LANES = 2
LSTM_TURNS = NB // (LANE_B * LANES)


def lane_steps():
    steps = []
    for p, nb in ((1, 2), (2, 4), (3, 4), (4, 8)):
        windows = T // p + (T // p) % 2
        for b0 in range(0, LANE_B, nb):
            steps += [(p, b0, nb, windows, t) for t in range(p)]
    return steps


STEPS = lane_steps()


def last_writer(n):
    p, b0, nb, _, _ = STEPS[n]
    done = 0
    for m in range(n):
        q, c0, cb, _, t = STEPS[m]
        if q < p and t == q - 1 and c0 < b0 + nb and b0 < c0 + cb:
            done = m + 1
    return done


def recurrent(n):
    return sum(step[4] > 0 for step in STEPS[:n])


class Count:

    def __init__(self, sem, per=1):
        self.sem, self.per = sem, per

    def start(self, engine):
        engine.sem_inc(self.sem, 2 * self.per)

    def done(self, unit, n=None):
        return unit * self.per + (2 * self.per + (self.per if n is None else n))


def build(nc, d, out):
    with ExitStack() as top:
        def sem(name):
            return top.enter_context(nc.semaphore(name))

        def count(name, per=1):
            return Count(sem(name), per)

        def sb(name, shape, dt=F32, ctx=top):
            return ctx.enter_context(nc.sbuf_tensor(name, shape, dt))

        ps = top.enter_context(nc.psum_tensor("ps", [P, 8, 512], F32))

        X = sb("X", [P, TILES, D])
        adj_sb = sb("adj_sb", [P, 2, T])
        adjT = sb("adjT", [P, 2, T])
        LT = sb("LT", [P, 2, T])
        ident2 = sb("ident2", [P, 2, T])
        ident = ident2[:, 0, 0:P]
        identb = sb("identb", [P, P], BF16)
        maskb = sb("maskb", [P, 2, T], BF16)
        ones = sb("ones", [P, P])
        minus_half = sb("minus_half", [P, UT])
        eps = sb("eps", [P, UT])
        rows = sb("rows", [P, 9, D])
        cols = sb("cols", [P, 3])
        bn = sb("bn", [P, TILES, 6])
        mean2 = sb("mean2", [P, TILES])
        diff = sb("diff", [P, TILES])
        m2 = sb("m2", [P, TILES])
        var = sb("var", [P, TILES])
        std = sb("std", [P, TILES])
        rstd = sb("rstd", [P, TILES])
        nmr = sb("nmr", [P, TILES])
        BC, G1, BE1, BO, G2, BE2, B2, G3, BE3 = range(9)

        def row(n, tiles=UT):
            return rows[:, n, :].unsqueeze(1).broadcast_to([P, tiles, D])

        x_loaded = [sem(f"x_loaded{c}") for c in range(TILES // CHUNK)]
        consts_loaded = sem("consts_loaded")
        weights_loaded = sem("weights_loaded")
        const_made = sem("const_made")
        stats = sem("stats")
        bn_made = sem("bn_made")

        def layernorm_stats(dve, act, base):
            if dve is not None:
                h = [bn[:, :, k] for k in range(6)]
                nc.vector.tensor_tensor(mean2[:], h[1], h[4], ALU.add)
                nc.vector.tensor_tensor(diff[:], h[1], h[4], ALU.subtract)
                nc.vector.tensor_tensor(m2[:], h[2], h[5], ALU.add).then_inc(stats, 1)
                dve.wait_ge(stats, base + 1)
                nc.vector.scalar_tensor_tensor(std[:], diff[:], 0.25, diff[:], ALU.mult, ALU.mult).then_inc(stats, 1)
                dve.wait_ge(stats, base + 2)
                nc.vector.scalar_tensor_tensor(var[:], m2[:], 1.0 / D, std[:], ALU.mult, ALU.add).then_inc(stats, 1)
                dve.wait_ge(stats, base + 3)
                nc.vector.tensor_scalar(var[:], var[:], EPS, None, ALU.add).then_inc(stats, 1)
                dve.wait_ge(stats, base + 5)
                nc.vector.reciprocal(rstd[:], std[:]).then_inc(stats, 1)
                dve.wait_ge(stats, base + 6)
                nc.vector.scalar_tensor_tensor(nmr[:], mean2[:], -0.5, rstd[:], ALU.mult, ALU.mult).then_inc(stats, 1)
            if act is not None:
                act.wait_ge(stats, base + 4)
                nc.scalar.activation(std[:], var[:], ACT.Sqrt).then_inc(stats, 1)
                act.wait_ge(stats, base + 7)

        NMEAN, VAR, SUM, DIFF, SQ, DIFF2 = range(6)

        def moments_of(dve, b, mo, made, unit, n):
            nc.vector.tensor_tensor(mo[:, SUM, :], b[:, :, 1], b[:, :, 4], ALU.add)
            nc.vector.tensor_tensor(mo[:, DIFF, :], b[:, :, 1], b[:, :, 4], ALU.subtract)
            nc.vector.tensor_tensor(mo[:, SQ, :], b[:, :, 2], b[:, :, 5], ALU.add).then_inc(made.sem, 1)
            dve.wait_ge(made.sem, made.done(unit, n + 1))
            nc.vector.tensor_scalar(mo[:, NMEAN, :], mo[:, SUM, :], -0.5, None, ALU.mult)
            nc.vector.scalar_tensor_tensor(mo[:, DIFF2, :], mo[:, DIFF, :], 0.25, mo[:, DIFF, :], ALU.mult,
                                           ALU.mult).then_inc(made.sem, 1)
            dve.wait_ge(made.sem, made.done(unit, n + 2))
            nc.vector.scalar_tensor_tensor(mo[:, VAR, :], mo[:, SQ, :], 1.0 / D, mo[:, DIFF2, :], ALU.mult,
                                           ALU.add).then_inc(made.sem, 1)

        lstm_ctx = top.enter_context(ExitStack())
        Hhi = sb("Hhi", [P, NB, HS], F32R, lstm_ctx)
        Hlo = sb("Hlo", [P, NB, HS], F32R, lstm_ctx)
        WX = sb("WX", [P, 2, MAX_SKIP, 4 * D], F32R, lstm_ctx)
        WH = sb("WH", [P, 2, MAX_SKIP, 4 * D], F32R, lstm_ctx)
        bias = sb("bias", [P, MAX_SKIP * 4], F32, lstm_ctx)

        with ExitStack() as ctx:
            W_raw = sb("W_raw", [P, 2, MAX_SKIP * 4 * D], F32, ctx)
            bias_raw = sb("bias_raw", [P, 2, MAX_SKIP * 4], F32, ctx)
            Wg = sb("Wg", [P, 2, D], F32, ctx)
            bg0 = sb("bg0", [P, D], F32, ctx)
            rowsum = sb("rowsum", [P, 2], F32, ctx)
            rowsum_b = sb("rowsum_b", [P, 2, T], F32, ctx)
            bias0 = sb("bias0", [P, UT, D], F32, ctx)
            S = sb("S", [P, 2, T], F32, ctx)
            M = sb("M", [P, 2, T], F32, ctx)
            eig_junk = sb("eig_junk", [P, 2, T], F32, ctx)
            norms = sb("norms", [P, 2], F32, ctx)
            norm_all = sb("norm_all", [P, 2], F32, ctx)
            shift = sb("shift", [P, 1], F32, ctx)
            diag = sb("diag", [P, 1], F32, ctx)
            trace_r = sb("trace_r", [P, 1], F32, ctx)
            trace_r2 = sb("trace_r2", [P, 1], F32, ctx)
            quotient = sb("quotient", [P, 2], F32, ctx)
            lam = sb("lam", [P, 3], F32, ctx)
            u = sb("u0", [P, 2, UT, D], F32, ctx)
            A0 = sb("A0", [P, 2, UW], F32, ctx)
            y0 = sb("y0", [P, 2, UT, D], F32, ctx)
            h1 = sb("h1", [P, 2, UT, D], F32, ctx)
            A1 = sb("A1", [P, 2, UW], F32, ctx)
            y1 = sb("y1", [P, 2, UB, T], F32, ctx)

            u_made = count("u_made", 2)
            a0_mm = count("a0_mm", 2)
            a0_out = count("a0_out", 2)
            w0_mm = count("w0_mm", 2)
            y0_out = count("y0_out", 2)
            h1_made = count("h1_made", 2)
            a1_mm = count("a1_mm", 2)
            a1_out = count("a1_out", 2)
            w1_mm = count("w1_mm", 2)
            y1_out = count("y1_out", 2)
            hi_made = count("hi_made", 2)
            lo_made = count("lo_made", 2)
            sq_mm = count("sq_mm")
            tr_mm = count("tr_mm")
            tr_used = count("tr_used", 2)
            m_made = count("m_made")
            diag_made = count("diag_made")
            eig = sem("eig")
            lt_made = sem("lt_made")
            split = sem("split")
            PS_SQ, PS_TR = 7, 6
            per_turn = SQUARINGS // (UNITS // 2)

            with nc.Block() as block:
                @block.sync
                def _(sp):
                    sp.dma_start(adj_sb[:], d["adj"]).then_inc(consts_loaded, 16)
                    sp.dma_start(adjT[:], d["adjT"]).then_inc(consts_loaded, 16)
                    for c in range(TILES // CHUNK):
                        tiles = slice(c * CHUNK, (c + 1) * CHUNK)
                        sp.dma_start(X[:, tiles, :], d["x"][:, tiles, :]).then_inc(x_loaded[c], 16)
                        if c == 0:
                            sp.dma_start(Wg[:], d["Wg"]).then_inc(consts_loaded, 16)
                            sp.dma_start(bg0[:], d["bg0"].to_broadcast([P, D])).then_inc(consts_loaded, 16)
                            sp.dma_start(cols[:], d["cols"]).then_inc(consts_loaded, 16)
                    sp.dma_start(W_raw[:, 0, :], d["Wih"]).then_inc(weights_loaded, 16)
                    sp.dma_start(W_raw[:, 1, :], d["Whh"]).then_inc(weights_loaded, 16)
                    sp.dma_start(bias_raw[:], d["lstm_b"]).then_inc(weights_loaded, 16)
                    sp.dma_start(rows[:], d["rows"].unsqueeze(0).broadcast_to([P, 9, D])).then_inc(weights_loaded, 16)

                @block.gpsimd
                def _(pool):
                    nc.gpsimd.memset(ident2[:], 0.0).then_inc(const_made, 1)
                    nc.gpsimd.memset(ones[:], 1.0).then_inc(const_made, 1)
                    nc.gpsimd.memset(minus_half[:], -0.5).then_inc(const_made, 1)
                    nc.gpsimd.memset(eps[:], EPS).then_inc(const_made, 1)
                    pool.wait_ge(const_made, 4)
                    nc.gpsimd.affine_select(out=ident2[:], in_=ident2[:], compare_op=ALU.not_equal, fill=1.0, base=0,
                                            pattern=[[P, 2], [-1, T]], channel_multiplier=1).then_inc(const_made, 1)
                    pool.wait_ge(eig, 3)
                    nc.gpsimd.partition_all_reduce(norm_all[:], norms[:], P, RMAX).then_inc(eig, 1)
                    for H in (Hhi, Hlo):
                        nc.gpsimd.memset(H[:, :, T:HS].bitcast(F32), 0.0).then_inc(const_made, 1)
                    pool.wait_ge(weights_loaded, 64)
                    for n, W in enumerate((WX, WH)):
                        hi, lo = (W[:, k, :, :].rearrange("p a b -> p (a b)") for k in range(2))
                        nc.gpsimd.tensor_copy(hi, W_raw[:, n, :]).then_inc(split, 1)
                        pool.wait_ge(split, 2 * n + 1)
                        nc.gpsimd.tensor_tensor(lo, W_raw[:, n, :], hi.bitcast(F32), ALU.subtract).then_inc(split, 1)
                    nc.gpsimd.tensor_tensor(bias[:], bias_raw[:, 0, :], bias_raw[:, 1, :], ALU.add).then_inc(split, 1)
                    pool.wait_ge(split, 5)

                @block.vector
                def _(dve):
                    for c in (a0_out, y0_out, a1_out, y1_out, lo_made, tr_used, m_made, diag_made):
                        c.start(dve)
                    dve.wait_ge(consts_loaded, 80)
                    nc.vector.tensor_tensor(S[:], adj_sb[:], adjT[:], ALU.add).then_inc(eig, 1)
                    nc.vector.tensor_scalar(maskb[:], adj_sb[:], 0.0, MASKED, ALU.is_le, ALU.mult)
                    nc.vector.tensor_reduce(rowsum[:], adj_sb[:], AX.X, ALU.add).then_inc(stats, 1)
                    dve.wait_ge(eig, 1)
                    nc.vector.tensor_scalar(S[:], S[:], 0.5, None, ALU.mult).then_inc(eig, 1)
                    dve.wait_ge(eig, 2)
                    nc.vector.tensor_reduce(norms[:], S[:], AX.X, ALU.add, apply_absolute_value=True).then_inc(eig, 1)
                    dve.wait_ge(stats, 1)
                    for k in range(UT):
                        nc.vector.tensor_scalar(bias0[:, k, :], bg0[:], rowsum[:, k % 2:k % 2 + 1], None, ALU.mult)
                    dve.wait_ge(const_made, 5)
                    nc.vector.tensor_copy(identb[:], ident)
                    dve.wait_ge(eig, 4)
                    nc.vector.tensor_reduce(shift[:], norm_all[:], AX.X, ALU.max).then_inc(eig, 1)
                    dve.wait_ge(eig, 5)
                    nc.vector.tensor_scalar(shift[:], shift[:], 1e-12, None, ALU.add).then_inc(eig, 1)
                    dve.wait_ge(eig, 6)
                    nc.vector.scalar_tensor_tensor(M[:], ident2[:], shift[:], S[:], ALU.mult, ALU.add).then_inc(eig, 1)
                    dve.wait_ge(eig, 7)
                    nc.vector.tensor_tensor_reduce(eig_junk[:], M[:], ident2[:], 1.0, 0.0, ALU.mult, ALU.add,
                                                   diag[:]).then_inc(eig, 1)
                    dve.wait_ge(eig, 9)
                    for k in range(2):
                        last = nc.vector.tensor_copy(rowsum_b[:, k, :], ps[:, 0, 0:T])
                    last.then_inc(eig, 1)
                    for c in range(TILES // CHUNK):
                        dve.wait_ge(x_loaded[c], 16)
                        with dve.Fori(c * CHUNK, (c + 1) * CHUNK) as k:
                            nc.vector.bn_stats(bn[:, bass.ds(k, 1), :].rearrange("p a b -> p (a b)"),
                                               X[:, bass.ds(k, 1), :].rearrange("p a b -> p (a b)")).then_inc(bn_made, 1)
                    dve.wait_ge(bn_made, TILES)
                    layernorm_stats(dve, None, 1)

                    def squaring(n):
                        dve.wait_ge(tr_mm.sem, tr_mm.done(n))
                        nc.vector.reciprocal(trace_r[:], ps[:, PS_TR, 0:1]).then_inc(tr_used.sem, 1)
                        dve.wait_ge(tr_used.sem, tr_used.done(n, 1))
                        nc.vector.tensor_tensor(trace_r2[:], trace_r[:], trace_r[:], ALU.mult).then_inc(tr_used.sem, 1)
                        dve.wait_ge(tr_used.sem, tr_used.done(n))
                        dve.wait_ge(sq_mm.sem, sq_mm.done(n))
                        nc.vector.tensor_scalar(M[:].rearrange("p a b -> p (a b)"), ps[:, PS_SQ, :], trace_r2[:], None,
                                                ALU.mult).then_inc(m_made.sem, 1)
                        dve.wait_ge(m_made.sem, m_made.done(n))
                        nc.vector.tensor_tensor_reduce(eig_junk[:], M[:], ident2[:], 1.0, 0.0, ALU.mult, ALU.add,
                                                       diag[:]).then_inc(diag_made.sem, 1)

                    with dve.Fori(0, UNITS // 2) as g:
                        for s in range(2):
                            dve.wait_ge(a0_mm.sem, a0_mm.done(g, s + 1))
                            dve.wait_ge(w0_mm.sem, w0_mm.done(g - 1, s + 1))
                            nc.vector.tensor_copy(A0[:, s, :], ps[:, s, :]).then_inc(a0_out.sem, 1)
                        squaring(g * per_turn)
                        for s in range(2):
                            dve.wait_ge(w0_mm.sem, w0_mm.done(g, s + 1))
                            dve.wait_ge(h1_made.sem, h1_made.done(g - 1, s + 1))
                            nc.vector.tensor_tensor(y0[:, s, :, :].rearrange("p a b -> p (a b)"), ps[:, 2 + s, :],
                                                    bias0[:].rearrange("p a b -> p (a b)"),
                                                    ALU.add).then_inc(y0_out.sem, 1)
                        for s in range(2):
                            dve.wait_ge(a1_mm.sem, a1_mm.done(g, s + 1))
                            dve.wait_ge(w1_mm.sem, w1_mm.done(g - 1, s + 1))
                            nc.vector.tensor_copy(A1[:, s, :], ps[:, 4 + s, :]).then_inc(a1_out.sem, 1)
                        squaring(g * per_turn + 1)
                        for s in range(2):
                            dve.wait_ge(w1_mm.sem, w1_mm.done(g, s + 1))
                            dve.wait_ge(hi_made.sem, hi_made.done(g - 1, s + 1))
                            nc.vector.scalar_tensor_tensor(
                                y1[:, s, :, :].rearrange("p a b -> p (a b)"), rowsum_b[:].rearrange("p a b -> p (a b)"),
                                cols[:, 0:1], ps[:, s, :], ALU.mult, ALU.add).then_inc(y1_out.sem, 1)
                        for s in range(2):
                            dve.wait_ge(hi_made.sem, hi_made.done(g, s + 1))
                            b = bass.ds(g * (2 * UB) + s * UB, UB)
                            nc.vector.scalar_tensor_tensor(
                                Hlo[:, b, 0:T], y1[:, s, :, :], 0.0, Hhi[:, b, 0:T].bitcast(F32),
                                ALU.max, ALU.subtract).then_inc(lo_made.sem, 1)
                    dve.wait_ge(sq_mm.sem, sq_mm.done(SQUARINGS))
                    nc.vector.tensor_tensor_reduce(eig_junk[:].rearrange("p a b -> p (a b)"),
                                                   M[:].rearrange("p a b -> p (a b)"), ps[:, PS_SQ, :], 1.0, 0.0,
                                                   ALU.mult, ALU.add, quotient[:, 0:1]).then_inc(eig, 1)
                    dve.wait_ge(eig, 11)
                    nc.vector.tensor_tensor_reduce(eig_junk[:], M[:], M[:], 1.0, 0.0, ALU.mult, ALU.add,
                                                   quotient[:, 1:2]).then_inc(eig, 1)
                    dve.wait_ge(eig, 13)
                    nc.vector.reciprocal(lam[:, 0:1], ps[:, PS_TR, 1:2]).then_inc(eig, 1)
                    dve.wait_ge(eig, 14)
                    nc.vector.tensor_tensor(lam[:, 1:2], ps[:, PS_TR, 0:1], lam[:, 0:1], ALU.mult).then_inc(eig, 1)
                    dve.wait_ge(eig, 15)
                    nc.vector.tensor_scalar(lam[:, 1:2], lam[:, 1:2], 1e-8, 0.5, ALU.add, ALU.mult).then_inc(eig, 1)
                    dve.wait_ge(eig, 16)
                    nc.vector.reciprocal(lam[:, 2:3], lam[:, 1:2]).then_inc(eig, 1)
                    dve.wait_ge(eig, 17)
                    nc.vector.scalar_tensor_tensor(LT[:], adjT[:], lam[:, 2:3], ident2[:], ALU.mult,
                                                   ALU.subtract).then_inc(lt_made, 1)
                    dve.wait_ge(lt_made, 1)

                @block.scalar
                def _(act):
                    for c in (u_made, h1_made, hi_made):
                        c.start(act)
                    for c in range(TILES // CHUNK):
                        act.wait_ge(x_loaded[c], 16)
                    layernorm_stats(None, act, 1)
                    with act.Fori(0, UNITS // 2) as g:
                        for s in range(2):
                            act.wait_ge(a0_mm.sem, a0_mm.done(g - 1, s + 1))
                            for k in range(UT):
                                tile = bass.ds(g * (2 * UT) + (s * UT + k), 1)
                                last = nc.scalar.activation(u[:, s, k, :],
                                                            X[:, tile, :].rearrange("p a b -> p (a b)"),
                                                            ACT.Relu, bias=nmr[:, tile], scale=rstd[:, tile])
                            last.then_inc(u_made.sem, 1)
                        for s in range(2):
                            act.wait_ge(y0_out.sem, y0_out.done(g, s + 1))
                            act.wait_ge(a1_mm.sem, a1_mm.done(g - 1, s + 1))
                            nc.scalar.activation(h1[:, s, :, :], y0[:, s, :, :], ACT.Relu).then_inc(h1_made.sem, 1)
                        for s in range(2):
                            act.wait_ge(y1_out.sem, y1_out.done(g, s + 1))
                            nc.scalar.activation(Hhi[:, bass.ds(g * (2 * UB) + s * UB, UB), 0:T], y1[:, s, :, :],
                                                 ACT.Relu).then_inc(hi_made.sem, 1)

                @block.tensor
                def _(pe):
                    for c in (a0_mm, w0_mm, a1_mm, w1_mm, sq_mm, tr_mm):
                        c.start(pe)
                    pe.wait_ge(const_made, 5)
                    pe.wait_ge(consts_loaded, 80)
                    pe.wait_ge(eig, 8)
                    for k in range(2):
                        last = nc.tensor.matmul(ps[:, 0, 0:T], ones[:], adjT[:, k, :], start=k == 0, stop=k == 1)
                    last.then_inc(eig, 1)
                    pe.wait_ge(eig, 10)

                    def product(lhs, sem, value):
                        for m in range(2):
                            for k in range(2):
                                last = nc.tensor.matmul(ps[:, PS_SQ, m * T:(m + 1) * T], lhs[:, k, m * P:(m + 1) * P],
                                                        M[:, k, :], start=k == 0, stop=k == 1)
                        last.then_inc(sem, value)

                    def squaring(n):
                        pe.wait_ge(m_made.sem, m_made.done(n - 1))
                        product(M, sq_mm.sem, 1)
                        pe.wait_ge(diag_made.sem, diag_made.done(n - 1))
                        pe.wait_ge(tr_used.sem, tr_used.done(n - 1))
                        nc.tensor.matmul(ps[:, PS_TR, 0:1], ones[:], diag[:], start=True,
                                         stop=True).then_inc(tr_mm.sem, 1)

                    def graph(src, s, bank):
                        for b in range(UB):
                            for k in range(2):
                                last = nc.tensor.matmul(ps[:, bank, b * T:(b + 1) * T], src[:, s, 2 * b + k, :],
                                                        adjT[:, k, :], start=k == 0, stop=k == 1)
                        return last

                    with pe.Fori(0, UNITS // 2) as g:
                        for s in range(2):
                            pe.wait_ge(u_made.sem, u_made.done(g, s + 1))
                            pe.wait_ge(y1_out.sem, y1_out.done(g - 1, s + 1))
                            graph(u, s, s).then_inc(a0_mm.sem, 1)
                        squaring(g * per_turn)
                        for s in range(2):
                            pe.wait_ge(a0_out.sem, a0_out.done(g, s + 1))
                            pe.wait_ge(y0_out.sem, y0_out.done(g - 1, s + 1))
                            for k in range(UT):
                                last = nc.tensor.matmul(ps[:, 2 + s, k * P:(k + 1) * P], A0[:, s, k * P:(k + 1) * P],
                                                        Wg[:, 0, :], start=True, stop=True)
                            last.then_inc(w0_mm.sem, 1)
                        for s in range(2):
                            pe.wait_ge(h1_made.sem, h1_made.done(g, s + 1))
                            pe.wait_ge(a1_out.sem, a1_out.done(g - 1, s + 1))
                            graph(h1, s, 4 + s).then_inc(a1_mm.sem, 1)
                        squaring(g * per_turn + 1)
                        for s in range(2):
                            pe.wait_ge(a1_out.sem, a1_out.done(g, s + 1))
                            nc.tensor.matmul(ps[:, s, :], Wg[:, 1, :], A1[:, s, :], start=True,
                                             stop=True).then_inc(w1_mm.sem, 1)
                    pe.wait_ge(m_made.sem, m_made.done(SQUARINGS - 1))
                    product(S, sq_mm.sem, 1)
                    pe.wait_ge(eig, 12)
                    nc.tensor.matmul(ps[:, PS_TR, 0:2], ones[:], quotient[:], start=True, stop=True).then_inc(eig, 1)

        with ExitStack() as ctx:
            names = ("gi", "gf", "gg", "go", "cell", "ig", "fc", "tc", "h32")
            buf = {n: sb(f"{n}_l", [P, LANES, 512], F32, ctx) for n in names}
            hhi = sb("hhi_l", [P, LANES, 512], F32R, ctx)
            hlo = sb("hlo_l", [P, LANES, 512], F32R, ctx)
            NSTEP = len(STEPS)
            RSTEP = recurrent(NSTEP)
            gate_mm = [[count(f"gate_mm{L}_{g}", RSTEP if g == F else NSTEP) for g in range(4)] for L in range(LANES)]
            gate_act = [[count(f"gate_act{L}_{g}", RSTEP if g == F else NSTEP) for g in range(4)] for L in range(LANES)]
            terms = [count(f"terms{L}", 2 * RSTEP) for L in range(LANES)]
            cell_made = [count(f"cell_made{L}", NSTEP) for L in range(LANES)]
            tanh_made = [count(f"tanh_made{L}", NSTEP) for L in range(LANES)]
            h_made = [count(f"h_made{L}", NSTEP) for L in range(LANES)]
            h_hi = [count(f"h_hi{L}", NSTEP) for L in range(LANES)]
            h_lo = [count(f"h_lo{L}", NSTEP) for L in range(LANES)]

            def width(n):
                return STEPS[n][2] * STEPS[n][3]

            def state(H, turn, L, n, t, windows):
                p, b0, nb, _, _ = STEPS[n]
                return H[:, bass.ds(turn * (LANES * LANE_B) + (L * LANE_B + b0), nb), t:t + (windows - 1) * p + 1:p]

            with nc.Block() as block:
                @block.tensor
                def _(pe):
                    for L in range(LANES):
                        for g in range(4):
                            gate_mm[L][g].start(pe)

                    def step(turn, L, n):
                        p, b0, nb, windows, t = STEPS[n]
                        N = width(n)
                        pe.wait_ge(gate_act[L][O].sem, gate_act[L][O].done(turn, n))
                        if t == 0 and last_writer(n):
                            pe.wait_ge(h_lo[L].sem, h_lo[L].done(turn, last_writer(n)))
                        xs = [state(H, turn, L, n, t, windows) for H in (Hhi, Hlo)]
                        hs = [H[:, L, 0:N] for H in (hhi, hlo)]
                        order = (I, G, F, O) if t else (I, G, O)
                        def mm(W, g, w, v, start=False, stop=False):
                            return nc.tensor.matmul(ps[:, 4 * L + g, 0:N], W[:, w, p - 1, g * P:(g + 1) * P], v,
                                                    start=start, stop=stop)
                        for g in order:
                            mm(WX, g, 0, xs[0], start=True)
                            mm(WX, g, 0, xs[1])
                            last = mm(WX, g, 1, xs[0], stop=t == 0)
                            if t == 0:
                                last.then_inc(gate_mm[L][g].sem, 1)
                        if t == 0:
                            return
                        pe.wait_ge(h_hi[L].sem, h_hi[L].done(turn, n))
                        for g in (I, G):
                            mm(WH, g, 0, hs[0])
                            mm(WH, g, 1, hs[0])
                        pe.wait_ge(h_lo[L].sem, h_lo[L].done(turn, n))
                        for g in (I, G):
                            mm(WH, g, 0, hs[1], stop=True).then_inc(gate_mm[L][g].sem, 1)
                        for g in (F, O):
                            mm(WH, g, 0, hs[0])
                            mm(WH, g, 1, hs[0])
                            mm(WH, g, 0, hs[1], stop=True).then_inc(gate_mm[L][g].sem, 1)

                    with pe.Fori(0, LSTM_TURNS) as turn:
                        for n in range(NSTEP):
                            for L in range(LANES):
                                step(turn, L, n)

                @block.scalar
                def _(act):
                    for L in range(LANES):
                        tanh_made[L].start(act)
                        for g in range(4):
                            gate_act[L][g].start(act)
                    dst = {I: "gi", F: "gf", G: "gg", O: "go"}

                    def step(turn, L, n):
                        p, b0, nb, windows, t = STEPS[n]
                        N = width(n)
                        act.wait_ge(cell_made[L].sem, cell_made[L].done(turn, n))
                        act.wait_ge(h_made[L].sem, h_made[L].done(turn, n))
                        for g in ((I, G, F, O) if t else (I, G, O)):
                            seen = recurrent(n + 1) if g == F else n + 1
                            act.wait_ge(gate_mm[L][g].sem, gate_mm[L][g].done(turn, seen))
                            a = nc.scalar.activation(buf[dst[g]][:, L, 0:N], ps[:, 4 * L + g, 0:N],
                                                     ACT.Tanh if g == G else ACT.Sigmoid,
                                                     bias=bias[:, 4 * (p - 1) + g:4 * (p - 1) + g + 1])
                            a.then_inc(gate_act[L][g].sem, 1)
                        act.wait_ge(cell_made[L].sem, cell_made[L].done(turn, n + 1))
                        nc.scalar.activation(buf["tc"][:, L, 0:N], buf["cell"][:, L, 0:N],
                                             ACT.Tanh).then_inc(tanh_made[L].sem, 1)

                    with act.Fori(0, LSTM_TURNS) as turn:
                        for n in range(NSTEP):
                            for L in range(LANES):
                                step(turn, L, n)

                @block.vector
                def _(dve):
                    for L in range(LANES):
                        for c in (terms, cell_made, h_made, h_hi, h_lo):
                            c[L].start(dve)

                    def step(turn, L, n):
                        p, b0, nb, windows, t = STEPS[n]
                        N = width(n)
                        v = {k: b[:, L, 0:N] for k, b in buf.items()}
                        dve.wait_ge(gate_act[L][G].sem, gate_act[L][G].done(turn, n + 1))
                        if t == 0:
                            dve.wait_ge(tanh_made[L].sem, tanh_made[L].done(turn, n))
                            nc.vector.tensor_tensor(v["cell"], v["gi"], v["gg"], ALU.mult).then_inc(cell_made[L].sem, 1)
                        else:
                            nc.vector.tensor_tensor(v["ig"], v["gi"], v["gg"], ALU.mult).then_inc(terms[L].sem, 1)
                            dve.wait_ge(gate_act[L][F].sem, gate_act[L][F].done(turn, recurrent(n + 1)))
                            nc.vector.tensor_tensor(v["fc"], v["gf"], v["cell"], ALU.mult).then_inc(terms[L].sem, 1)
                            dve.wait_ge(terms[L].sem, terms[L].done(turn, 2 * recurrent(n + 1)))
                            nc.vector.tensor_tensor(v["cell"], v["ig"], v["fc"], ALU.add).then_inc(cell_made[L].sem, 1)
                        dve.wait_ge(tanh_made[L].sem, tanh_made[L].done(turn, n + 1))
                        nc.vector.tensor_tensor(v["h32"], v["go"], v["tc"], ALU.mult).then_inc(h_made[L].sem, 1)
                        dve.wait_ge(h_made[L].sem, h_made[L].done(turn, n + 1))
                        if t < p - 1:
                            h, hi, lo = v["h32"], hhi[:, L, 0:N], hlo[:, L, 0:N]
                        else:
                            h = v["h32"].rearrange("p (b w) -> p b w", b=nb)[:, :, 0:T // p]
                            hi, lo = (state(H, turn, L, n, t, T // p) for H in (Hhi, Hlo))
                        nc.vector.tensor_copy(hi, h).then_inc(h_hi[L].sem, 1)
                        dve.wait_ge(h_hi[L].sem, h_hi[L].done(turn, n + 1))
                        nc.vector.tensor_tensor(lo, h, hi.bitcast(F32), ALU.subtract).then_inc(h_lo[L].sem, 1)

                    with dve.Fori(0, LSTM_TURNS) as turn:
                        for n in range(NSTEP):
                            for L in range(LANES):
                                step(turn, L, n)

        with ExitStack() as ctx:
            h32 = sb("h_sum", [P, 2, UB, T], F32, ctx)
            sum_made = count("sum_made", 2)
            h_turned = count("h_turned", 2)
            x_added = count("x_added", 2)
            with nc.Block() as block:
                @block.vector
                def _(dve):
                    sum_made.start(dve)
                    x_added.start(dve)
                    with dve.Fori(0, UNITS // 2) as g:
                        for s in range(2):
                            b = bass.ds(g * (2 * UB) + s * UB, UB)
                            dve.wait_ge(h_turned.sem, h_turned.done(g - 1, s + 1))
                            nc.vector.tensor_tensor(h32[:, s, :, :], Hhi[:, b, 0:T].bitcast(F32),
                                                    Hlo[:, b, 0:T].bitcast(F32), ALU.add).then_inc(sum_made.sem, 1)
                        for s in range(2):
                            dve.wait_ge(h_turned.sem, h_turned.done(g, s + 1))
                            tiles = X[:, bass.ds(g * (2 * UT) + s * UT, UT), :]
                            nc.vector.tensor_tensor(tiles, ps[:, s, :].rearrange("p (a b) -> p a b", a=UT), tiles,
                                                    ALU.add).then_inc(x_added.sem, 1)
                            dve.wait_ge(x_added.sem, x_added.done(g, s + 1))
                            for k in range(UT):
                                tile = bass.ds(g * (2 * UT) + (s * UT + k), 1)
                                nc.vector.bn_stats(bn[:, tile, :].rearrange("p a b -> p (a b)"),
                                                   X[:, tile, :].rearrange("p a b -> p (a b)")).then_inc(bn_made, 1)
                    dve.wait_ge(bn_made, 2 * TILES)
                    layernorm_stats(dve, None, 8)

                @block.scalar
                def _(act):
                    layernorm_stats(None, act, 8)

                @block.tensor
                def _(pe):
                    h_turned.start(pe)
                    with pe.Fori(0, UNITS // 2) as g:
                        for s in range(2):
                            pe.wait_ge(sum_made.sem, sum_made.done(g, s + 1))
                            pe.wait_ge(x_added.sem, x_added.done(g - 1, s + 1))
                            for k in range(UT):
                                last = nc.tensor.transpose(
                                    ps[:, s, k * P:(k + 1) * P],
                                    h32[:, s, k // 2, (k % 2) * P:(k % 2 + 1) * P], ident)
                            last.then_inc(h_turned.sem, 1)
        lstm_ctx.close()

        X2 = sb("X2", [P, TILES, D])
        X2T = sb("X2T", [P, NB * T])
        W1 = sb("W1", [P, HID])
        W2 = sb("W2", [P, 2, D])
        late_loaded = sem("late_loaded")
        with ExitStack() as ctx:
            Wc, Wq, Wk, Wv, Wo = (sb(n, [P, D], F32, ctx) for n in ("Wc", "Wq", "Wk", "Wv", "Wo"))
            u = sb("u1", [P, 2, UT, D], F32, ctx)
            xpT = sb("xpT", [P, UW], F32, ctx)
            t1 = sb("t1", [P, UT, D], F32, ctx)
            z1 = sb("z1", [P, UT, D], F32, ctx)
            x1 = sb("x1", [P, UT, D], F32, ctx)
            x1b = sb("x1b", [P, 2, UT, D], F32, ctx)
            x1T = sb("x1T", [P, 2, UW], F32, ctx)
            bn1 = sb("bn1", [P, 2, UT, 6], F32, ctx)
            mo1 = sb("mo1", [P, 2, 6, UT], F32, ctx)
            ve1 = sb("ve1", [P, 2, UT], F32, ctx)
            rs1 = sb("rs1", [P, 2, UT], F32, ctx)
            nm1 = sb("nm1", [P, 2, UT], F32, ctx)
            q = [sb(f"q_{n}", [P, UW], F32R, ctx) for n in ("hi", "lo")]
            k_ = [sb(f"k_{n}", [P, UW], F32R, ctx) for n in ("hi", "lo")]
            V3 = sb("V3", [P, 2, 3, UT, HEADS, HD + 1], BF16, ctx)
            zero = sb("zero", [P, HD], F32, ctx)
            vrest = sb("vrest", [P, UT, HEADS, HD], F32, ctx)
            negmax = sb("negmax", [P, 2, HEADS], F32, ctx)
            prob = sb("prob", [P, 2, HEADS, T], F32, ctx)
            probT = sb("probT", [P, 2, 2, 2 * HEADS, P], F16, ctx)
            rden = sb("rden", [P, HEADS], F32, ctx)
            o_sb = sb("o_sb", [P, UT, D], F32, ctx)
            oT = sb("oT", [P, UW], F32, ctx)
            y2 = sb("y2", [P, UT, D], F32, ctx)
            z2 = sb("z2", [P, UT, D], F32, ctx)
            x2 = sb("x2", [P, UT, D], F32, ctx)

            u1_made = count("u1_made")
            xp_mm = count("xp_mm")
            xp_out = count("xp_out")
            wc_mm = count("wc_mm")
            t1_out = count("t1_out")
            ln_stats = [count("ln1_stats", 4), count("ln2_stats", 4)]
            ln_rstd = [count("ln1_rstd", 3), count("ln2_rstd", 3)]
            z_made = [count("z1_made"), count("z2_made")]
            zg_made = [count("zg1_made"), count("zg2_made")]
            zb_made = [count("zb1_made"), count("zb2_made")]
            x1_made = count("x1_made")
            x1b_made = count("x1b_made")
            x1T_mm = count("x1T_mm")
            x1T_out = count("x1T_out")
            q_mm = count("q_mm")
            k_mm = count("k_mm")
            v_mm = count("v_mm")
            q_hi = count("q_hi")
            q_lo = count("q_lo")
            k_hi = count("k_hi")
            k_lo = count("k_lo")
            v_1 = count("v_1")
            v_rest = count("v_rest")
            v_2 = count("v_2")
            v_3 = count("v_3")
            s_half = count("s_half", UT)
            s_mm = count("s_mm", UT)
            max_made = count("max_made", UT)
            exp_made = count("exp_made", UT)
            pT_mm = count("pT_mm", UT)
            pT_hi = count("pT_hi", UT)
            pT_lo = count("pT_lo", UT)
            o_mm = count("o_mm", UT)
            rden_made = count("rden_made", UT)
            o_out = count("o_out", UT)
            oT_mm = count("oT_mm")
            oT_out = count("oT_out")
            wo_mm = count("wo_mm")
            y2_out = count("y2_out")
            x2_kept = count("x2_kept", 16)
            x2T_mm = count("x2T_mm")
            x2T_out = count("x2T_out")
            v_ones = sem("v_ones")
            att_loaded = sem("att_loaded")
            PS_T, PS_O, PS_G = 4, 6, 7

            def scores(s):
                return ps[:, 2 * (s % 2):2 * (s % 2) + 2, :].rearrange("p a (b c) -> p (a b) c", b=2)

            def head(j):
                return j // 2 + 2 * (j % 2)

            def walk(engine, body):
                body(0, 0, 0, 2)
                body(1, 1, 1, 2)
                with engine.Fori(0, UNITS // 2 - 2) as g:
                    body(g * 2 + 2, 0, 2, 2)
                    body(g * 2 + 3, 1, 2, 2)
                body(UNITS - 2, 0, 2, 1)
                body(UNITS - 1, 1, 2, 0)

            with nc.Block() as block:
                @block.sync
                def _(sp):
                    for W, n in ((Wc, "Wc"), (Wq, "Wq"), (Wk, "Wk"), (Wv, "Wv"), (Wo, "Wo")):
                        sp.dma_start(W[:], d[n]).then_inc(att_loaded, 16)
                    sp.dma_start(W1[:], d["W1"]).then_inc(late_loaded, 16)
                    sp.dma_start(W2[:], d["W2"]).then_inc(late_loaded, 16)
                    x2_kept.start(sp)
                    with sp.Fori(0, UNITS) as unit:
                        sp.wait_ge(zb_made[1].sem, zb_made[1].done(unit))
                        sp.dma_start(X2[:, bass.ds(unit * UT, UT), :], x2[:]).then_inc(x2_kept.sem, 16)
                    sp.wait_ge(x2_kept.sem, x2_kept.done(UNITS - 1))

                @block.gpsimd
                def _(pool):
                    for c in (*ln_rstd, *zg_made, *zb_made, x1b_made, v_2, v_3):
                        c.start(pool)
                    nc.gpsimd.memset(zero[:], 0.0).then_inc(v_ones, 1)
                    for par in range(2):
                        for part in range(3):
                            nc.gpsimd.memset(V3[:, par, part, :, :, HD:HD + 1], float(part == 0)).then_inc(v_ones, 1)

                    pool.wait_ge(v_ones, 7)

                    def rstd_of(n, unit):
                        pool.wait_ge(ln_stats[n].sem, ln_stats[n].done(unit))
                        nc.gpsimd.tensor_tensor(ve1[:, n, :], mo1[:, n, VAR, :], eps[:],
                                                ALU.add).then_inc(ln_rstd[n].sem, 1)
                        pool.wait_ge(ln_rstd[n].sem, ln_rstd[n].done(unit, 1))
                        nc.gpsimd.tensor_tensor(rs1[:, n, :], ve1[:, n, :], minus_half[:],
                                                ALU.pow).then_inc(ln_rstd[n].sem, 1)
                        pool.wait_ge(ln_rstd[n].sem, ln_rstd[n].done(unit, 2))
                        nc.gpsimd.tensor_tensor(nm1[:, n, :], mo1[:, n, NMEAN, :], rs1[:, n, :],
                                                ALU.mult).then_inc(ln_rstd[n].sem, 1)

                    def scale(n, unit, z, gain, shift, dst):
                        pool.wait_ge(z_made[n].sem, z_made[n].done(unit))
                        nc.gpsimd.tensor_tensor(z[:], z[:], row(gain), ALU.mult).then_inc(zg_made[n].sem, 1)
                        pool.wait_ge(zg_made[n].sem, zg_made[n].done(unit))
                        nc.gpsimd.tensor_tensor(dst[:], z[:], row(shift), ALU.add).then_inc(zb_made[n].sem, 1)

                    def keep_x1(unit, par):
                        pool.wait_ge(x1_made.sem, x1_made.done(unit))
                        pool.wait_ge(y2_out.sem, y2_out.done(unit - 2))
                        nc.gpsimd.tensor_tensor(x1b[:, par, :, :], x1[:], row(BO), ALU.add).then_inc(x1b_made.sem, 1)

                    def split_v(unit, par):
                        parts = [V3[:, par, n, :, :, 0:HD].rearrange("p a h c -> p (a h) c") for n in range(3)]
                        rest = vrest[:].rearrange("p a h c -> p (a h) c")
                        zeros = zero[:].unsqueeze(1).broadcast_to([P, UT * HEADS, HD])
                        pool.wait_ge(v_rest.sem, v_rest.done(unit))
                        nc.gpsimd.tensor_tensor(parts[1], rest, zeros, ALU.add).then_inc(v_2.sem, 1)
                        pool.wait_ge(v_2.sem, v_2.done(unit))
                        nc.gpsimd.tensor_tensor(parts[2], rest, parts[1], ALU.subtract).then_inc(v_3.sem, 1)

                    def make_x2(unit):
                        pool.wait_ge(x2T_mm.sem, x2T_mm.done(unit - 1))
                        pool.wait_ge(x2_kept.sem, x2_kept.done(unit - 1))
                        scale(1, unit, z2, G2, BE2, x2)

                    def body(unit, par, back, more):
                        if more:
                            rstd_of(0, unit + 1)
                        if back > 1:
                            make_x2(unit - 2)
                        if more:
                            scale(0, unit + 1, z1, G1, BE1, z1)
                            keep_x1(unit + 1, 1 - par)
                            split_v(unit + 1, 1 - par)
                        if back:
                            rstd_of(1, unit - 1)

                    rstd_of(0, 0)
                    scale(0, 0, z1, G1, BE1, z1)
                    keep_x1(0, 0)
                    split_v(0, 0)
                    walk(pool, body)
                    make_x2(UNITS - 2)
                    rstd_of(1, UNITS - 1)
                    make_x2(UNITS - 1)

                @block.scalar
                def _(act):
                    for c in (u1_made, xp_out, *z_made, x1T_out, q_hi, k_hi, v_1, exp_made, pT_hi, oT_out, x2T_out):
                        c.start(act)

                    def make_u(unit, par):
                        act.wait_ge(x1_made.sem, x1_made.done(unit - 2))
                        for k in range(UT):
                            tile = bass.ds(unit * UT + k, 1)
                            last = nc.scalar.activation(u[:, par, k, :], X[:, tile, :].rearrange("p a b -> p (a b)"),
                                                        ACT.Relu, bias=nmr[:, tile], scale=rstd[:, tile])
                        last.then_inc(u1_made.sem, 1)

                    def take(unit, mm, dst, out):
                        act.wait_ge(mm.sem, mm.done(unit))
                        nc.scalar.activation(dst, ps[:, PS_G, :], ACT.Copy).then_inc(out.sem, 1)

                    def xp(unit):
                        act.wait_ge(wc_mm.sem, wc_mm.done(unit - 1))
                        take(unit, xp_mm, xpT[:], xp_out)

                    def turn_x1(unit, par):
                        act.wait_ge(v_mm.sem, v_mm.done(unit - 2))
                        take(unit, x1T_mm, x1T[:, par, :], x1T_out)

                    def turn_o(unit):
                        act.wait_ge(wo_mm.sem, wo_mm.done(unit - 1))
                        take(unit, oT_mm, oT[:], oT_out)

                    def turn_x2(unit):
                        take(unit, x2T_mm, X2T[:, bass.ds(unit * UW, UW)], x2T_out)

                    def normalise(n, unit, src, z):
                        act.wait_ge(ln_rstd[n].sem, ln_rstd[n].done(unit))
                        act.wait_ge((x1_made if n == 0 else zb_made[1]).sem,
                                    (x1_made if n == 0 else zb_made[1]).done(unit - 1))
                        for k in range(UT):
                            last = nc.scalar.activation(z[:, k, :], src[:, k, :], ACT.Identity,
                                                        bias=nm1[:, n, k:k + 1], scale=rs1[:, n, k:k + 1])
                        last.then_inc(z_made[n].sem, 1)

                    def qkv(unit, par):
                        act.wait_ge(q_mm.sem, q_mm.done(unit))
                        nc.scalar.activation(q[0][:], ps[:, 0, :], ACT.Copy, scale=SCALE).then_inc(q_hi.sem, 1)
                        act.wait_ge(k_mm.sem, k_mm.done(unit))
                        nc.scalar.activation(k_[0][:], ps[:, 1, :], ACT.Copy).then_inc(k_hi.sem, 1)
                        act.wait_ge(v_mm.sem, v_mm.done(unit))
                        act.wait_ge(o_mm.sem, o_mm.done(unit - 2))
                        nc.scalar.activation(V3[:, par, 0, :, :, 0:HD].rearrange("p a h c -> p (a h) c"),
                                             ps[:, PS_G, :].rearrange("p (a c) -> p a c", c=HD),
                                             ACT.Copy).then_inc(v_1.sem, 1)

                    def exps(unit, s):
                        act.wait_ge(max_made.sem, max_made.done(unit, s + 1))
                        act.wait_ge(pT_mm.sem, pT_mm.done(unit, s - 1))
                        for h in range(HEADS):
                            last = nc.scalar.activation(prob[:, s % 2, h, :], scores(s)[:, h, :], ACT.Exp,
                                                        bias=negmax[:, s % 2, h:h + 1])
                        last.then_inc(exp_made.sem, 1)

                    def turn_p(unit, s):
                        act.wait_ge(pT_mm.sem, pT_mm.done(unit, s + 1))
                        act.wait_ge(o_mm.sem, o_mm.done(unit, s - 1))
                        nc.scalar.activation(probT[:, s % 2, 0, :, :].rearrange("p a b -> p (a b)"),
                                             ps[:, PS_T:PS_T + 2, :].rearrange("p a b -> p (a b)"),
                                             ACT.Copy).then_inc(pT_hi.sem, 1)

                    def body(unit, par, back, more):
                        if back > 1:
                            normalise(1, unit - 2, y2, z2)
                        exps(unit, 1)
                        turn_p(unit, 0)
                        if back:
                            turn_o(unit - 1)
                        if more:
                            normalise(0, unit + 1, t1, z1)
                        exps(unit, 2)
                        turn_p(unit, 1)
                        if back > 1:
                            turn_x2(unit - 2)
                        if more > 1:
                            make_u(unit + 2, par)
                        exps(unit, 3)
                        turn_p(unit, 2)
                        if more:
                            turn_x1(unit + 1, 1 - par)
                            qkv(unit + 1, 1 - par)
                        turn_p(unit, 3)
                        if more > 1:
                            xp(unit + 2)
                        if more:
                            exps(unit + 1, 0)

                    make_u(0, 0)
                    xp(0)
                    make_u(1, 1)
                    normalise(0, 0, t1, z1)
                    turn_x1(0, 0)
                    qkv(0, 0)
                    xp(1)
                    exps(0, 0)
                    walk(act, body)
                    normalise(1, UNITS - 2, y2, z2)
                    turn_o(UNITS - 1)
                    turn_x2(UNITS - 2)
                    normalise(1, UNITS - 1, y2, z2)
                    turn_x2(UNITS - 1)

                @block.vector
                def _(dve):
                    for c in (t1_out, *ln_stats, x1_made, q_lo, k_lo, v_rest, max_made, pT_lo, rden_made, o_out,
                              y2_out):
                        c.start(dve)

                    def moments(n, unit, src):
                        for k in range(UT):
                            last = nc.vector.bn_stats(bn1[:, n, k, :], src[:, k, :])
                        last.then_inc(ln_stats[n].sem, 1)
                        dve.wait_ge(ln_stats[n].sem, ln_stats[n].done(unit, 1))
                        moments_of(dve, bn1[:, n, :, :], mo1[:, n, :, :], ln_stats[n], unit, 1)

                    def conv(unit):
                        dve.wait_ge(wc_mm.sem, wc_mm.done(unit))
                        dve.wait_ge(z_made[0].sem, z_made[0].done(unit - 1))
                        nc.vector.tensor_tensor(t1[:], ps[:, PS_G, :].rearrange("p (a b) -> p a b", a=UT), row(BC),
                                                ALU.add).then_inc(t1_out.sem, 1)
                        dve.wait_ge(t1_out.sem, t1_out.done(unit))
                        moments(0, unit, t1)

                    def make_x1(unit, par):
                        dve.wait_ge(zb_made[0].sem, zb_made[0].done(unit))
                        dve.wait_ge(x1T_mm.sem, x1T_mm.done(unit - 1))
                        dve.wait_ge(x1b_made.sem, x1b_made.done(unit - 1))
                        nc.vector.scalar_tensor_tensor(x1[:].rearrange("p a b -> p (a b)"),
                                                       z1[:].rearrange("p a b -> p (a b)"), 0.0,
                                                       u[:, par, :, :].rearrange("p a b -> p (a b)"),
                                                       ALU.max, ALU.add).then_inc(x1_made.sem, 1)

                    def qkv(unit, par):
                        dve.wait_ge(q_hi.sem, q_hi.done(unit))
                        nc.vector.scalar_tensor_tensor(q[1][:], ps[:, 0, :], SCALE, q[0][:].bitcast(F32), ALU.mult,
                                                       ALU.subtract).then_inc(q_lo.sem, 1)
                        dve.wait_ge(k_hi.sem, k_hi.done(unit))
                        nc.vector.tensor_tensor(k_[1][:], ps[:, 1, :], k_[0][:].bitcast(F32),
                                                ALU.subtract).then_inc(k_lo.sem, 1)
                        dve.wait_ge(v_1.sem, v_1.done(unit))
                        dve.wait_ge(v_3.sem, v_3.done(unit - 1))
                        nc.vector.tensor_tensor(vrest[:].rearrange("p a h c -> p (a h) c"),
                                                ps[:, PS_G, :].rearrange("p (a c) -> p a c", c=HD),
                                                V3[:, par, 0, :, :, 0:HD].rearrange("p a h c -> p (a h) c"),
                                                ALU.subtract).then_inc(v_rest.sem, 1)

                    def row_max(unit, s):
                        dve.wait_ge(s_mm.sem, s_mm.done(unit, s + 1))
                        dve.wait_ge(exp_made.sem, exp_made.done(unit, s - 1))
                        nc.vector.tensor_reduce(negmax[:, s % 2, :], scores(s), AX.X, ALU.max,
                                                negate=True).then_inc(max_made.sem, 1)

                    def turn_p(unit, s):
                        dve.wait_ge(pT_hi.sem, pT_hi.done(unit, s + 1))
                        hi, lo = (probT[:, s % 2, n, :, :].rearrange("p a b -> p (a b)") for n in range(2))
                        nc.vector.tensor_tensor(lo, ps[:, PS_T:PS_T + 2, :].rearrange("p a b -> p (a b)"), hi,
                                                ALU.subtract).then_inc(pT_lo.sem, 1)

                    def make_o(unit, s):
                        dve.wait_ge(o_mm.sem, o_mm.done(unit, s + 1))
                        acc = ps[:, PS_O, 0:HEADS * (HD + 1)].rearrange("p (h c) -> p h c", h=HEADS)
                        nc.vector.reciprocal(rden[:].unsqueeze(2), acc[:, :, HD:HD + 1]).then_inc(rden_made.sem, 1)
                        dve.wait_ge(rden_made.sem, rden_made.done(unit, s + 1))
                        dve.wait_ge(oT_mm.sem, oT_mm.done(unit - 1))
                        nc.vector.tensor_tensor(o_sb[:, s, :].rearrange("p (h c) -> p h c", h=HEADS), acc[:, :, 0:HD],
                                                rden[:].unsqueeze(2).broadcast_to([P, HEADS, HD]),
                                                ALU.mult).then_inc(o_out.sem, 1)

                    def add_o(unit, par):
                        dve.wait_ge(wo_mm.sem, wo_mm.done(unit))
                        dve.wait_ge(x1b_made.sem, x1b_made.done(unit))
                        dve.wait_ge(z_made[1].sem, z_made[1].done(unit - 1))
                        nc.vector.tensor_tensor(y2[:], ps[:, PS_O, :].rearrange("p (a b) -> p a b", a=UT),
                                                x1b[:, par, :, :], ALU.add).then_inc(y2_out.sem, 1)

                    def moments_y2(unit):
                        dve.wait_ge(y2_out.sem, y2_out.done(unit))
                        moments(1, unit, y2)

                    def body(unit, par, back, more):
                        row_max(unit, 1)
                        if more:
                            conv(unit + 1)
                        if back:
                            make_o(unit - 1, 3)
                        turn_p(unit, 0)
                        row_max(unit, 2)
                        make_o(unit, 0)
                        turn_p(unit, 1)
                        row_max(unit, 3)
                        make_o(unit, 1)
                        if more:
                            make_x1(unit + 1, 1 - par)
                        turn_p(unit, 2)
                        if back:
                            add_o(unit - 1, 1 - par)
                        if more:
                            qkv(unit + 1, 1 - par)
                        make_o(unit, 2)
                        turn_p(unit, 3)
                        if back:
                            moments_y2(unit - 1)
                        if more:
                            row_max(unit + 1, 0)

                    conv(0)
                    make_x1(0, 0)
                    dve.wait_ge(v_ones, 7)
                    qkv(0, 0)
                    row_max(0, 0)
                    walk(dve, body)
                    make_o(UNITS - 1, 3)
                    add_o(UNITS - 1, 1)
                    moments_y2(UNITS - 1)

                @block.tensor
                def _(pe):
                    for c in (s_half, xp_mm, wc_mm, x1T_mm, q_mm, k_mm, v_mm, s_mm, pT_mm, o_mm, oT_mm, wo_mm, x2T_mm):
                        c.start(pe)
                    pe.wait_ge(att_loaded, 80)

                    def xp(unit, par):
                        pe.wait_ge(u1_made.sem, u1_made.done(unit))
                        pe.wait_ge(v_rest.sem, v_rest.done(unit - 1))
                        for b in range(UB):
                            for k in range(2):
                                last = nc.tensor.matmul(ps[:, PS_G, b * T:(b + 1) * T], u[:, par, 2 * b + k, :],
                                                        LT[:, k, :], start=k == 0, stop=k == 1)
                        last.then_inc(xp_mm.sem, 1)

                    def conv(unit):
                        pe.wait_ge(xp_out.sem, xp_out.done(unit))
                        for k in range(UT):
                            last = nc.tensor.matmul(ps[:, PS_G, k * P:(k + 1) * P], xpT[:, k * P:(k + 1) * P], Wc[:],
                                                    start=True, stop=True)
                        last.then_inc(wc_mm.sem, 1)

                    def turn(src, unit, sem):
                        for k in range(UT):
                            last = nc.tensor.transpose(ps[:, PS_G, k * P:(k + 1) * P], src[:, k, :], ident)
                        last.then_inc(sem, 1)

                    def turn_o(unit):
                        pe.wait_ge(o_out.sem, o_out.done(unit))
                        turn(o_sb, unit, oT_mm.sem)

                    def turn_x1(unit):
                        pe.wait_ge(x1_made.sem, x1_made.done(unit))
                        pe.wait_ge(oT_out.sem, oT_out.done(unit - 2))
                        pe.wait_ge(x2T_out.sem, x2T_out.done(unit - 3))
                        turn(x1, unit, x1T_mm.sem)

                    def turn_x2(unit):
                        pe.wait_ge(zb_made[1].sem, zb_made[1].done(unit))
                        pe.wait_ge(oT_out.sem, oT_out.done(unit + 1))
                        turn(x2, unit, x2T_mm.sem)

                    def out_proj(unit):
                        pe.wait_ge(oT_out.sem, oT_out.done(unit))
                        for k in range(UT):
                            last = nc.tensor.matmul(ps[:, PS_O, k * P:(k + 1) * P], oT[:, k * P:(k + 1) * P], Wo[:],
                                                    start=True, stop=True)
                        last.then_inc(wo_mm.sem, 1)

                    def qkv(unit, par):
                        pe.wait_ge(x1T_out.sem, x1T_out.done(unit))
                        pe.wait_ge(exp_made.sem, exp_made.done(unit - 1, 3))
                        nc.tensor.matmul(ps[:, 0, :], Wq[:], x1T[:, par, :], start=True, stop=True)\
                            .then_inc(q_mm.sem, 1)
                        nc.tensor.matmul(ps[:, 1, :], Wk[:], x1T[:, par, :], start=True, stop=True)\
                            .then_inc(k_mm.sem, 1)
                        for k in range(UT):
                            last = nc.tensor.matmul(ps[:, PS_G, k * P:(k + 1) * P], x1T[:, par, k * P:(k + 1) * P],
                                                    Wv[:], start=True, stop=True)
                        last.then_inc(v_mm.sem, 1)

                    def score(unit, s):
                        if s == 0:
                            pe.wait_ge(q_lo.sem, q_lo.done(unit))
                            pe.wait_ge(k_lo.sem, k_lo.done(unit))
                        pe.wait_ge(exp_made.sem, exp_made.done(unit, s - 1))
                        b, qt = divmod(s, 2)
                        for half in range(2):
                            for bank in range(2):
                                nc.tensor.matmul(scores(s)[:, 2 * bank + half, :], identb[:], maskb[:, qt, :],
                                                 start=True, stop=False)
                            for n, (a, c) in enumerate(((0, 0), (0, 1), (1, 0))):
                                for bank in range(2):
                                    j = 2 * bank + half
                                    rows_h = slice(head(j) * HD, (head(j) + 1) * HD)
                                    last = nc.tensor.matmul(scores(s)[:, j, :], q[a][rows_h, s * P:(s + 1) * P],
                                                            k_[c][rows_h, b * T:(b + 1) * T], start=False,
                                                            stop=n == 2)
                            if half == 0:
                                last.then_inc(s_half.sem, 1)
                                pe.wait_ge(s_half.sem, s_half.done(unit, s + 1))
                        last.then_inc(s_mm.sem, 1)

                    def turn_p(unit, s):
                        pe.wait_ge(exp_made.sem, exp_made.done(unit, s + 1))
                        pe.wait_ge(pT_lo.sem, pT_lo.done(unit, s))
                        for j in range(HEADS):
                            for k in range(2):
                                at = (j % 2 * 2 + k) * P
                                last = nc.tensor.transpose(ps[:, PS_T + j // 2, at:at + P],
                                                           prob[:, s % 2, j, k * P:(k + 1) * P], ident)
                        last.then_inc(pT_mm.sem, 1)

                    def weigh_v(unit, par, s):
                        pe.wait_ge(pT_lo.sem, pT_lo.done(unit, s + 1))
                        pe.wait_ge(o_out.sem, o_out.done(unit, s))
                        if s == 0:
                            pe.wait_ge(v_3.sem, v_3.done(unit))
                        if s == 2:
                            pe.wait_ge(y2_out.sem, y2_out.done(unit - 1))
                        for j in range(HEADS):
                            h = head(j)
                            for k in range(2):
                                for n, (a, c) in enumerate(((0, 0), (0, 1), (0, 2), (1, 0), (1, 1))):
                                    last = nc.tensor.matmul(ps[:, PS_O, h * (HD + 1):(h + 1) * (HD + 1)],
                                                            probT[:, s % 2, a, 2 * j + k, :],
                                                            V3[:, par, c, s // 2 * 2 + k, h, :],
                                                            start=k + n == 0, stop=(k, n) == (1, 4))
                        last.then_inc(o_mm.sem, 1)

                    def body(unit, par, back, more):
                        score(unit, 1)
                        if more:
                            conv(unit + 1)
                        if back:
                            weigh_v(unit - 1, 1 - par, 3)
                        turn_p(unit, 0)
                        score(unit, 2)
                        if more:
                            pe.wait_ge(t1_out.sem, t1_out.done(unit + 1))
                        if back:
                            turn_o(unit - 1)
                        weigh_v(unit, par, 0)
                        turn_p(unit, 1)
                        score(unit, 3)
                        if back > 1:
                            turn_x2(unit - 2)
                        weigh_v(unit, par, 1)
                        turn_p(unit, 2)
                        if more:
                            turn_x1(unit + 1)
                        if back:
                            pe.wait_ge(o_out.sem, o_out.done(unit, 2))
                            out_proj(unit - 1)
                        if more:
                            qkv(unit + 1, 1 - par)
                        weigh_v(unit, par, 2)
                        turn_p(unit, 3)
                        if more > 1:
                            xp(unit + 2, par)
                        if more:
                            score(unit + 1, 0)

                    xp(0, 0)
                    conv(0)
                    turn_x1(0)
                    qkv(0, 0)
                    xp(1, 1)
                    score(0, 0)
                    walk(pe, body)
                    weigh_v(UNITS - 1, 1, 3)
                    turn_o(UNITS - 1)
                    turn_x2(UNITS - 2)
                    out_proj(UNITS - 1)
                    pe.wait_ge(x2T_out.sem, x2T_out.done(UNITS - 2))
                    pe.wait_ge(zb_made[1].sem, zb_made[1].done(UNITS - 1))
                    turn(x2, UNITS - 1, x2T_mm.sem)

        with ExitStack() as ctx:
            hid = sb("hid", [P, 2, 2, UW], F32, ctx)
            x2b = sb("x2b", [P, 2, UT, D], F32, ctx)
            y3 = sb("y3", [P, 2, UT, D], F32, ctx)
            z3 = sb("z3", [P, 2, UT, D], F32, ctx)
            xr = sb("xr", [P, 2, UT, D], F32, ctx)
            res = sb("res", [P, 2, UT, D], F32, ctx)
            bn3 = sb("bn3", [P, 2, UT, 6], F32, ctx)
            mo3 = sb("mo3", [P, 2, 6, UT], F32, ctx)
            ve3 = sb("ve3", [P, 2, UT], F32, ctx)
            rs3 = sb("rs3", [P, 2, UT], F32, ctx)
            hid_mm = count("hid_mm", 4)
            gelu_made = count("gelu_made", 4)
            m_mm = count("m_mm", 2)
            x2b_made = count("x2b_made", 2)
            xr_made = count("xr_made", 2)
            y3_out = count("y3_out", 2)
            st3 = count("st3", 8)
            rs3_made = count("rs3_made", 4)
            z3_made = count("z3_made", 2)
            zg3_made = count("zg3_made", 2)
            res_made = count("res_made", 2)
            stored = [count(f"stored{s}", 16) for s in range(2)]

            with nc.Block() as block:
                @block.sync
                def _(sp):
                    for s in range(2):
                        stored[s].start(sp)
                    with sp.Fori(0, UNITS // 2) as g:
                        for s in range(2):
                            sp.wait_ge(res_made.sem, res_made.done(g, s + 1))
                            sp.dma_start(out[:, bass.ds(g * (2 * UT) + s * UT, UT), :],
                                         res[:, s, :, :]).then_inc(stored[s].sem, 16)
                    for s in range(2):
                        sp.wait_ge(stored[s].sem, stored[s].done(UNITS // 2 - 1))

                @block.tensor
                def _(pe):
                    hid_mm.start(pe)
                    m_mm.start(pe)
                    pe.wait_ge(late_loaded, 32)
                    with pe.Fori(0, UNITS // 2) as g:
                        for s in range(2):
                            for j in range(2):
                                pe.wait_ge(gelu_made.sem, gelu_made.done(g - 1, 2 * s + j + 1))
                                nc.tensor.matmul(ps[:, 2 * s + j, :], W1[:, j * P:(j + 1) * P],
                                                 X2T[:, bass.ds(g * (2 * UW) + s * UW, UW)], start=True,
                                                 stop=True).then_inc(hid_mm.sem, 1)
                        for s in range(2):
                            pe.wait_ge(gelu_made.sem, gelu_made.done(g, 2 * s + 2))
                            pe.wait_ge(y3_out.sem, y3_out.done(g - 1, s + 1))
                            for k in range(UT):
                                for j in range(2):
                                    last = nc.tensor.matmul(ps[:, 4 + s, k * P:(k + 1) * P],
                                                            hid[:, s, j, k * P:(k + 1) * P], W2[:, j, :],
                                                            start=j == 0, stop=j == 1)
                            last.then_inc(m_mm.sem, 1)

                @block.scalar
                def _(act):
                    gelu_made.start(act)
                    with act.Fori(0, UNITS // 2) as g:
                        for s in range(2):
                            act.wait_ge(m_mm.sem, m_mm.done(g - 1, s + 1))
                            for j in range(2):
                                act.wait_ge(hid_mm.sem, hid_mm.done(g, 2 * s + j + 1))
                                nc.scalar.activation(hid[:, s, j, :], ps[:, 2 * s + j, :], ACT.Gelu,
                                                     bias=cols[:, 1 + j:2 + j]).then_inc(gelu_made.sem, 1)

                @block.gpsimd
                def _(pool):
                    for c in (x2b_made, xr_made, rs3_made, zg3_made):
                        c.start(pool)
                    with pool.Fori(0, UNITS // 2) as g:
                        for s in range(2):
                            tiles = bass.ds(g * (2 * UT) + s * UT, UT)
                            pool.wait_ge(y3_out.sem, y3_out.done(g - 1, s + 1))
                            nc.gpsimd.tensor_tensor(x2b[:, s, :, :], X2[:, tiles, :], row(B2),
                                                    ALU.add).then_inc(x2b_made.sem, 1)
                            pool.wait_ge(res_made.sem, res_made.done(g - 1, s + 1))
                            nc.gpsimd.tensor_tensor(xr[:, s, :, :], X[:, tiles, :], row(BE3),
                                                    ALU.add).then_inc(xr_made.sem, 1)
                        for s in range(2):
                            pool.wait_ge(st3.sem, st3.done(g, 4 * s + 4))
                            nc.gpsimd.tensor_tensor(ve3[:, s, :], mo3[:, s, VAR, :], eps[:],
                                                    ALU.add).then_inc(rs3_made.sem, 1)
                            pool.wait_ge(rs3_made.sem, rs3_made.done(g, 2 * s + 1))
                            nc.gpsimd.tensor_tensor(rs3[:, s, :], ve3[:, s, :], minus_half[:],
                                                    ALU.pow).then_inc(rs3_made.sem, 1)
                            pool.wait_ge(z3_made.sem, z3_made.done(g, s + 1))
                            nc.gpsimd.tensor_tensor(z3[:, s, :, :], z3[:, s, :, :], row(G3),
                                                    ALU.mult).then_inc(zg3_made.sem, 1)

                @block.vector
                def _(dve):
                    for c in (y3_out, st3, z3_made, res_made):
                        c.start(dve)
                    with dve.Fori(0, UNITS // 2) as g:
                        for s in range(2):
                            dve.wait_ge(m_mm.sem, m_mm.done(g, s + 1))
                            dve.wait_ge(x2b_made.sem, x2b_made.done(g, s + 1))
                            nc.vector.tensor_tensor(y3[:, s, :, :],
                                                    ps[:, 4 + s, :].rearrange("p (a b) -> p a b", a=UT),
                                                    x2b[:, s, :, :], ALU.add).then_inc(y3_out.sem, 1)
                            dve.wait_ge(y3_out.sem, y3_out.done(g, s + 1))
                            for k in range(UT):
                                last = nc.vector.bn_stats(bn3[:, s, k, :], y3[:, s, k, :])
                            last.then_inc(st3.sem, 1)
                            dve.wait_ge(st3.sem, st3.done(g, 4 * s + 1))
                            moments_of(dve, bn3[:, s, :, :], mo3[:, s, :, :], st3, g, 4 * s + 1)
                        for s in range(2):
                            dve.wait_ge(rs3_made.sem, rs3_made.done(g, 2 * s + 2))
                            for k in range(UT):
                                last = nc.vector.tensor_scalar(z3[:, s, k, :], y3[:, s, k, :], mo3[:, s, NMEAN, k:k + 1],
                                                               rs3[:, s, k:k + 1], ALU.add, ALU.mult)
                            last.then_inc(z3_made.sem, 1)
                        for s in range(2):
                            dve.wait_ge(zg3_made.sem, zg3_made.done(g, s + 1))
                            dve.wait_ge(xr_made.sem, xr_made.done(g, s + 1))
                            dve.wait_ge(stored[s].sem, stored[s].done(g - 1))
                            nc.vector.tensor_tensor(res[:, s, :, :], z3[:, s, :, :], xr[:, s, :, :],
                                                    ALU.add).then_inc(res_made.sem, 1)


def kernel(**inputs):
    import numpy as np
    import concourse.bacc as bacc
    from concourse.bass_utils import run_bass_kernel_spmd

    a = {k: np.asarray(v) for k, v in inputs.items()}

    def halves(m):
        return m.reshape(2, P, -1).transpose(1, 0, 2)

    def lstm(m):
        return m.transpose(2, 0, 1).reshape(D, -1)

    def lstm_bias(m):
        return m.reshape(MAX_SKIP * 4, D).T

    n0, n1 = "L0_gnn_", "L1_gnn_"
    arrays = {
        "x": a["x"].reshape(TILES, P, D).transpose(1, 0, 2),
        "adj": halves(a["adj"]),
        "adjT": halves(a["adj"].T),
        "Wg": np.stack([a[n0 + "Wg0"], a[n0 + "Wg1"]], 1),
        "bg0": a[n0 + "bg0"][None],
        "Wih": lstm(a[n0 + "Wih"]),
        "Whh": lstm(a[n0 + "Whh"]),
        "lstm_b": np.stack([lstm_bias(a[n0 + "bih"]), lstm_bias(a[n0 + "bhh"])], 1),
        "rows": np.stack([a[n1 + k] for k in ("bc", "g1", "be1", "bo", "g2", "be2", "b2", "g3", "be3")]),
        "cols": np.stack([a[n0 + "bg1"], *a[n1 + "b1"].reshape(2, D)], 1),
        "Wc": a[n1 + "Wc"], "Wq": a[n1 + "Wq"], "Wk": a[n1 + "Wk"], "Wv": a[n1 + "Wv"], "Wo": a[n1 + "Wo"],
        "W1": a[n1 + "W1"], "W2": halves(a[n1 + "W2"]),
    }
    arrays = {k: np.ascontiguousarray(v) for k, v in arrays.items()}
    nc = bacc.Bacc("TRN2", target_bir_lowering=False, num_devices=1)
    d = {k: nc.dram_tensor(f"in_{k}", v.shape, F32, kind="ExternalInput").ap() for k, v in arrays.items()}
    out = nc.dram_tensor("out", (P, TILES, D), F32, kind="ExternalOutput").ap()
    build(nc, d, out)
    r = run_bass_kernel_spmd(nc, [{f"in_{k}": v for k, v in arrays.items()}], core_ids=[0])
    return r.results[0]["out"].transpose(1, 0, 2).reshape(NB, T, D)
```

```python
from contextlib import ExitStack

import concourse.bass as bass
from concourse import mybir

F32 = mybir.dt.float32
F32R = mybir.dt.float32r
BF16 = mybir.dt.bfloat16
F16 = mybir.dt.float16
ALU = mybir.AluOpType
ACT = mybir.ActivationFunctionType
AX = mybir.AxisListType
RMAX = bass.bass_isa.ReduceOp.max

P = 128
NB, T, D = 32, 256, 128
TILES = NB * T // P
UB = 2
UT = UB * T // P
UW = UB * T
UNITS = NB // UB
CHUNK = 8
EPS = 1e-5
SQUARINGS = 16
MAX_SKIP = 4
HS = T + 2
HEADS, HD = 4, 32
HID = 256
SCALE = HD ** -0.5
MASKED = -(2.0 ** 100)
I, F, G, O = range(4)

LANE_B = 8
LANES = 2
LSTM_TURNS = NB // (LANE_B * LANES)


def lane_steps():
    steps = []
    for p, nb in ((1, 2), (2, 4), (3, 4), (4, 8)):
        windows = T // p + (T // p) % 2
        for b0 in range(0, LANE_B, nb):
            steps += [(p, b0, nb, windows, t) for t in range(p)]
    return steps


STEPS = lane_steps()


def last_writer(n):
    p, b0, nb, _, _ = STEPS[n]
    done = 0
    for m in range(n):
        q, c0, cb, _, t = STEPS[m]
        if q < p and t == q - 1 and c0 < b0 + nb and b0 < c0 + cb:
            done = m + 1
    return done


def recurrent(n):
    return sum(step[4] > 0 for step in STEPS[:n])


class Count:

    def __init__(self, sem, per=1):
        self.sem, self.per = sem, per

    def start(self, engine):
        engine.sem_inc(self.sem, 2 * self.per)

    def done(self, unit, n=None):
        return unit * self.per + (2 * self.per + (self.per if n is None else n))


def build(nc, d, out):
    with ExitStack() as top:
        def sem(name):
            return top.enter_context(nc.semaphore(name))

        def count(name, per=1):
            return Count(sem(name), per)

        def sb(name, shape, dt=F32, ctx=top):
            return ctx.enter_context(nc.sbuf_tensor(name, shape, dt))

        ps = top.enter_context(nc.psum_tensor("ps", [P, 8, 512], F32))

        X = sb("X", [P, TILES, D])
        adj_sb = sb("adj_sb", [P, 2, T])
        adjT = sb("adjT", [P, 2, T])
        LT = sb("LT", [P, 2, T])
        ident2 = sb("ident2", [P, 2, T])
        ident = ident2[:, 0, 0:P]
        identb = sb("identb", [P, P], BF16)
        maskb = sb("maskb", [P, 2, T], BF16)
        ones = sb("ones", [P, P])
        minus_half = sb("minus_half", [P, UT])
        eps = sb("eps", [P, UT])
        rows = sb("rows", [P, 9, D])
        cols = sb("cols", [P, 3])
        Wc, Wq, Wk, Wv, Wo = (sb(n, [P, D]) for n in ("Wc", "Wq", "Wk", "Wv", "Wo"))
        W1 = sb("W1", [P, HID])
        W2 = sb("W2", [P, 2, D])
        bn = sb("bn", [P, TILES, 6])
        mean2 = sb("mean2", [P, TILES])
        diff = sb("diff", [P, TILES])
        m2 = sb("m2", [P, TILES])
        var = sb("var", [P, TILES])
        std = sb("std", [P, TILES])
        rstd = sb("rstd", [P, TILES])
        nmr = sb("nmr", [P, TILES])
        BC, G1, BE1, BO, G2, BE2, B2, G3, BE3 = range(9)

        def row(n, tiles=UT):
            return rows[:, n, :].unsqueeze(1).broadcast_to([P, tiles, D])

        x_loaded = [sem(f"x_loaded{c}") for c in range(TILES // CHUNK)]
        consts_loaded = sem("consts_loaded")
        weights_loaded = sem("weights_loaded")
        l1_loaded = sem("l1_loaded")
        const_made = sem("const_made")
        stats = sem("stats")
        bn_made = sem("bn_made")

        def layernorm_stats(dve, act, base):
            if dve is not None:
                h = [bn[:, :, k] for k in range(6)]
                nc.vector.tensor_tensor(mean2[:], h[1], h[4], ALU.add)
                nc.vector.tensor_tensor(diff[:], h[1], h[4], ALU.subtract)
                nc.vector.tensor_tensor(m2[:], h[2], h[5], ALU.add).then_inc(stats, 1)
                dve.wait_ge(stats, base + 1)
                nc.vector.scalar_tensor_tensor(std[:], diff[:], 0.25, diff[:], ALU.mult, ALU.mult).then_inc(stats, 1)
                dve.wait_ge(stats, base + 2)
                nc.vector.scalar_tensor_tensor(var[:], m2[:], 1.0 / D, std[:], ALU.mult, ALU.add).then_inc(stats, 1)
                dve.wait_ge(stats, base + 3)
                nc.vector.tensor_scalar(var[:], var[:], EPS, None, ALU.add).then_inc(stats, 1)
                dve.wait_ge(stats, base + 5)
                nc.vector.reciprocal(rstd[:], std[:]).then_inc(stats, 1)
                dve.wait_ge(stats, base + 6)
                nc.vector.scalar_tensor_tensor(nmr[:], mean2[:], -0.5, rstd[:], ALU.mult, ALU.mult).then_inc(stats, 1)
            if act is not None:
                act.wait_ge(stats, base + 4)
                nc.scalar.activation(std[:], var[:], ACT.Sqrt).then_inc(stats, 1)
                act.wait_ge(stats, base + 7)

        def walk(engine, body):
            body(0, 0, 0, 2)
            body(1, 1, 1, 2)
            with engine.Fori(0, UNITS // 2 - 2) as g:
                body(g * 2 + 2, 0, 2, 2)
                body(g * 2 + 3, 1, 2, 2)
            body(UNITS - 2, 0, 2, 1)
            body(UNITS - 1, 1, 2, 0)

        NMEAN, VAR, SUM, DIFF, SQ, DIFF2 = range(6)

        def moments_of(dve, b, mo, made, unit, n):
            nc.vector.tensor_tensor(mo[:, SUM, :], b[:, :, 1], b[:, :, 4], ALU.add)
            nc.vector.tensor_tensor(mo[:, DIFF, :], b[:, :, 1], b[:, :, 4], ALU.subtract)
            nc.vector.tensor_tensor(mo[:, SQ, :], b[:, :, 2], b[:, :, 5], ALU.add).then_inc(made.sem, 1)
            dve.wait_ge(made.sem, made.done(unit, n + 1))
            nc.vector.tensor_scalar(mo[:, NMEAN, :], mo[:, SUM, :], -0.5, None, ALU.mult)
            nc.vector.scalar_tensor_tensor(mo[:, DIFF2, :], mo[:, DIFF, :], 0.25, mo[:, DIFF, :], ALU.mult,
                                           ALU.mult).then_inc(made.sem, 1)
            dve.wait_ge(made.sem, made.done(unit, n + 2))
            nc.vector.scalar_tensor_tensor(mo[:, VAR, :], mo[:, SQ, :], 1.0 / D, mo[:, DIFF2, :], ALU.mult,
                                           ALU.add).then_inc(made.sem, 1)

        lstm_ctx = top.enter_context(ExitStack())
        Hhi = sb("Hhi", [P, NB, HS], F32R, lstm_ctx)
        Hlo = sb("Hlo", [P, NB, HS], F32R, lstm_ctx)
        WX = sb("WX", [P, 2, MAX_SKIP, 4 * D], F32R, lstm_ctx)
        WH = sb("WH", [P, 2, MAX_SKIP, 4 * D], F32R, lstm_ctx)
        bias = sb("bias", [P, MAX_SKIP * 4], F32, lstm_ctx)
        S = sb("S", [P, 2, T], F32, lstm_ctx)
        M = sb("M", [P, 2, T], F32, lstm_ctx)
        squares = sb("squares", [P, 1], F32, lstm_ctx)
        trace_r = sb("trace_r", [P, 1], F32, lstm_ctx)
        sq_mm = count("sq_mm")
        tr_mm = count("tr_mm")
        tr_used = count("tr_used")
        m_made = count("m_made")
        sum_sq = count("sum_sq")
        eig = sem("eig")
        PS_TR, PS_SQ = 6, 7
        EARLY = TILES // CHUNK + 1
        LATE = SQUARINGS - EARLY

        def pe_product(pe, lhs, sem, value):
            for m in range(2):
                for k in range(2):
                    last = nc.tensor.matmul(ps[:, PS_SQ, m * T:(m + 1) * T], lhs[:, k, m * P:(m + 1) * P], M[:, k, :],
                                            start=k == 0, stop=k == 1)
            last.then_inc(sem, value)

        def pe_squaring(pe, n):
            pe.wait_ge(m_made.sem, m_made.done(n - 1))
            pe_product(pe, M, sq_mm.sem, 1)
            pe.wait_ge(sum_sq.sem, sum_sq.done(n))
            pe.wait_ge(tr_used.sem, tr_used.done(n - 1))
            nc.tensor.matmul(ps[:, PS_TR, 0:1], ones[:], squares[:], start=True, stop=True).then_inc(tr_mm.sem, 1)

        def dve_squaring(dve, n):
            dve.wait_ge(tr_mm.sem, tr_mm.done(n))
            dve.wait_ge(m_made.sem, m_made.done(n - 1))
            nc.vector.reciprocal(trace_r[:], ps[:, PS_TR, 0:1]).then_inc(tr_used.sem, 1)

        def act_sum_squares(act, n, junk):
            act.wait_ge(tr_mm.sem, tr_mm.done(n - 1))
            nc.scalar.activation(junk[:], M[:], ACT.Square, accum_out=squares[:]).then_inc(sum_sq.sem, 1)

        def act_squaring(act, n, junk):
            act.wait_ge(tr_used.sem, tr_used.done(n))
            act.wait_ge(sq_mm.sem, sq_mm.done(n))
            nc.scalar.activation(M[:].rearrange("p a b -> p (a b)"), ps[:, PS_SQ, :], ACT.Copy,
                                 scale=trace_r[:]).then_inc(m_made.sem, 1)
            act.wait_ge(m_made.sem, m_made.done(n))
            act_sum_squares(act, n + 1, junk)

        with ExitStack() as ctx:
            W_raw = sb("W_raw", [P, 2, MAX_SKIP * 4 * D], F32, ctx)
            bias_raw = sb("bias_raw", [P, 2, MAX_SKIP * 4], F32, ctx)
            Wg = sb("Wg", [P, 2, D], F32, ctx)
            bg0 = sb("bg0", [P, D], F32, ctx)
            rowsum = sb("rowsum", [P, 2], F32, ctx)
            rowsum_b = sb("rowsum_b", [P, 2, T], F32, ctx)
            bias0 = sb("bias0", [P, UT, D], F32, ctx)
            eig_junk = sb("eig_junk", [P, 2, T], F32, ctx)
            norms = sb("norms", [P, 2], F32, ctx)
            norm_all = sb("norm_all", [P, 2], F32, ctx)
            shift = sb("shift", [P, 1], F32, ctx)
            u = sb("u0", [P, 2, UT, D], F32, ctx)
            A0 = sb("A0", [P, UW], F32, ctx)
            y0 = sb("y0", [P, UT, D], F32, ctx)
            h1 = sb("h1", [P, UT, D], F32, ctx)
            A1 = sb("A1", [P, UW], F32, ctx)
            y1 = sb("y1", [P, 2, UB, T], F32, ctx)

            u_made = count("u_made")
            a0_mm = count("a0_mm")
            a0_out = count("a0_out")
            w0_mm = count("w0_mm")
            y0_out = count("y0_out")
            h1_made = count("h1_made")
            a1_mm = count("a1_mm")
            a1_out = count("a1_out")
            w1_mm = count("w1_mm")
            y1_out = count("y1_out")
            hi_made = count("hi_made")
            lo_made = count("lo_made")
            split = sem("split")
            PS_A0, PS_W0, PS_A1, PS_W1 = 1, 2, 3, 4

            with nc.Block() as block:
                @block.sync
                def _(sp):
                    sp.dma_start(adj_sb[:], d["adj"]).then_inc(consts_loaded, 16)
                    sp.dma_start(adjT[:], d["adjT"]).then_inc(consts_loaded, 16)
                    for c in range(TILES // CHUNK):
                        tiles = slice(c * CHUNK, (c + 1) * CHUNK)
                        sp.dma_start(X[:, tiles, :], d["x"][:, tiles, :]).then_inc(x_loaded[c], 16)
                        if c == 0:
                            sp.dma_start(Wg[:], d["Wg"]).then_inc(consts_loaded, 16)
                            sp.dma_start(bg0[:], d["bg0"].to_broadcast([P, D])).then_inc(consts_loaded, 16)
                            sp.dma_start(cols[:], d["cols"]).then_inc(consts_loaded, 16)
                    sp.dma_start(W_raw[:, 0, :], d["Wih"]).then_inc(weights_loaded, 16)
                    sp.dma_start(W_raw[:, 1, :], d["Whh"]).then_inc(weights_loaded, 16)
                    sp.dma_start(bias_raw[:], d["lstm_b"]).then_inc(weights_loaded, 16)
                    sp.dma_start(rows[:], d["rows"].unsqueeze(0).broadcast_to([P, 9, D])).then_inc(weights_loaded, 16)
                    for W, n in ((Wc, "Wc"), (Wq, "Wq"), (Wk, "Wk"), (Wv, "Wv"), (Wo, "Wo"), (W1, "W1"), (W2, "W2")):
                        sp.dma_start(W[:], d[n]).then_inc(l1_loaded, 16)

                @block.gpsimd
                def _(pool):
                    nc.gpsimd.memset(ident2[:], 0.0).then_inc(const_made, 1)
                    nc.gpsimd.memset(ones[:], 1.0).then_inc(const_made, 1)
                    nc.gpsimd.memset(minus_half[:], -0.5).then_inc(const_made, 1)
                    nc.gpsimd.memset(eps[:], EPS).then_inc(const_made, 1)
                    pool.wait_ge(const_made, 4)
                    nc.gpsimd.affine_select(out=ident2[:], in_=ident2[:], compare_op=ALU.not_equal, fill=1.0, base=0,
                                            pattern=[[P, 2], [-1, T]], channel_multiplier=1).then_inc(const_made, 1)
                    pool.wait_ge(eig, 3)
                    nc.gpsimd.partition_all_reduce(norm_all[:], norms[:], P, RMAX).then_inc(eig, 1)
                    for H in (Hhi, Hlo):
                        nc.gpsimd.memset(H[:, :, T:HS].bitcast(F32), 0.0).then_inc(const_made, 1)
                    pool.wait_ge(weights_loaded, 64)
                    for n, W in enumerate((WX, WH)):
                        hi, lo = (W[:, k, :, :].rearrange("p a b -> p (a b)") for k in range(2))
                        nc.gpsimd.tensor_copy(hi, W_raw[:, n, :]).then_inc(split, 1)
                        pool.wait_ge(split, 2 * n + 1)
                        nc.gpsimd.tensor_tensor(lo, W_raw[:, n, :], hi.bitcast(F32), ALU.subtract).then_inc(split, 1)
                    nc.gpsimd.tensor_tensor(bias[:], bias_raw[:, 0, :], bias_raw[:, 1, :], ALU.add).then_inc(split, 1)
                    pool.wait_ge(split, 5)

                @block.vector
                def _(dve):
                    for c in (a0_out, y0_out, a1_out, y1_out, lo_made, tr_used):
                        c.start(dve)
                    dve.wait_ge(consts_loaded, 80)
                    nc.vector.tensor_tensor(S[:], adj_sb[:], adjT[:], ALU.add).then_inc(eig, 1)
                    nc.vector.tensor_scalar(maskb[:], adj_sb[:], 0.0, MASKED, ALU.is_le, ALU.mult)
                    nc.vector.tensor_reduce(rowsum[:], adj_sb[:], AX.X, ALU.add).then_inc(stats, 1)
                    dve.wait_ge(eig, 1)
                    nc.vector.tensor_scalar(S[:], S[:], 0.5, None, ALU.mult).then_inc(eig, 1)
                    dve.wait_ge(eig, 2)
                    nc.vector.tensor_reduce(norms[:], S[:], AX.X, ALU.add, apply_absolute_value=True).then_inc(eig, 1)
                    dve.wait_ge(stats, 1)
                    for k in range(UT):
                        nc.vector.tensor_scalar(bias0[:, k, :], bg0[:], rowsum[:, k % 2:k % 2 + 1], None, ALU.mult)
                    dve.wait_ge(const_made, 5)
                    nc.vector.tensor_copy(identb[:], ident)
                    dve.wait_ge(eig, 4)
                    nc.vector.tensor_reduce(shift[:], norm_all[:], AX.X, ALU.max).then_inc(eig, 1)
                    dve.wait_ge(eig, 5)
                    nc.vector.tensor_scalar(shift[:], shift[:], 1e-12, None, ALU.add).then_inc(eig, 1)
                    dve.wait_ge(eig, 6)
                    nc.vector.scalar_tensor_tensor(M[:], ident2[:], shift[:], S[:], ALU.mult, ALU.add).then_inc(eig, 1)
                    dve.wait_ge(eig, 8)
                    for k in range(2):
                        last = nc.vector.tensor_copy(rowsum_b[:, k, :], ps[:, 0, 0:T])
                    last.then_inc(eig, 1)

                    for c in range(TILES // CHUNK):
                        dve.wait_ge(x_loaded[c], 16)
                        for k in range(c * CHUNK, (c + 1) * CHUNK):
                            last = nc.vector.bn_stats(bn[:, k, :], X[:, k, :])
                        last.then_inc(bn_made, 1)
                        dve_squaring(dve, c)
                    dve.wait_ge(bn_made, TILES // CHUNK)
                    layernorm_stats(dve, None, 1)
                    dve_squaring(dve, EARLY - 1)

                    def take_a0(unit):
                        dve.wait_ge(a0_mm.sem, a0_mm.done(unit))
                        dve.wait_ge(w0_mm.sem, w0_mm.done(unit - 1))
                        nc.vector.tensor_copy(A0[:], ps[:, PS_A0, :]).then_inc(a0_out.sem, 1)

                    def take_y1(unit, par):
                        dve.wait_ge(w1_mm.sem, w1_mm.done(unit))
                        nc.vector.scalar_tensor_tensor(y1[:, par, :, :].rearrange("p a b -> p (a b)"),
                                                       rowsum_b[:].rearrange("p a b -> p (a b)"), cols[:, 0:1],
                                                       ps[:, PS_W1, :], ALU.mult, ALU.add).then_inc(y1_out.sem, 1)

                    def make_lo(unit, par):
                        dve.wait_ge(hi_made.sem, hi_made.done(unit))
                        b = bass.ds(unit * UB, UB)
                        nc.vector.scalar_tensor_tensor(Hlo[:, b, 0:T], y1[:, par, :, :], 0.0,
                                                       Hhi[:, b, 0:T].bitcast(F32), ALU.max,
                                                       ALU.subtract).then_inc(lo_made.sem, 1)

                    def body(unit, par, back, more):
                        dve.wait_ge(w0_mm.sem, w0_mm.done(unit))
                        dve.wait_ge(h1_made.sem, h1_made.done(unit - 1))
                        nc.vector.tensor_tensor(y0[:].rearrange("p a b -> p (a b)"), ps[:, PS_W0, :],
                                                bias0[:].rearrange("p a b -> p (a b)"), ALU.add).then_inc(y0_out.sem, 1)
                        if more:
                            take_a0(unit + 1)
                        if back > 1:
                            make_lo(unit - 2, par)
                        dve.wait_ge(a1_mm.sem, a1_mm.done(unit))
                        dve.wait_ge(w1_mm.sem, w1_mm.done(unit - 1))
                        nc.vector.tensor_copy(A1[:], ps[:, PS_A1, :]).then_inc(a1_out.sem, 1)
                        if back:
                            take_y1(unit - 1, 1 - par)

                    take_a0(0)
                    walk(dve, body)
                    make_lo(UNITS - 2, 0)
                    take_y1(UNITS - 1, 1)
                    make_lo(UNITS - 1, 1)

                @block.scalar
                def _(act):
                    for c in (u_made, h1_made, hi_made, m_made, sum_sq):
                        c.start(act)
                    act.wait_ge(eig, 7)
                    act_sum_squares(act, 0, eig_junk)
                    for n in range(EARLY - 1):
                        act_squaring(act, n, eig_junk)
                    for c in range(TILES // CHUNK):
                        act.wait_ge(x_loaded[c], 16)
                    layernorm_stats(None, act, 1)

                    def make_u(unit, par):
                        act.wait_ge(a0_mm.sem, a0_mm.done(unit - 2))
                        for k in range(UT):
                            tile = bass.ds(unit * UT + k, 1)
                            last = nc.scalar.activation(u[:, par, k, :], X[:, tile, :].rearrange("p a b -> p (a b)"),
                                                        ACT.Relu, bias=nmr[:, tile], scale=rstd[:, tile])
                        last.then_inc(u_made.sem, 1)

                    def make_hi(unit, par):
                        act.wait_ge(y1_out.sem, y1_out.done(unit))
                        nc.scalar.activation(Hhi[:, bass.ds(unit * UB, UB), 0:T], y1[:, par, :, :],
                                             ACT.Relu).then_inc(hi_made.sem, 1)

                    def body(unit, par, back, more):
                        act.wait_ge(y0_out.sem, y0_out.done(unit))
                        act.wait_ge(a1_mm.sem, a1_mm.done(unit - 1))
                        nc.scalar.activation(h1[:], y0[:], ACT.Relu).then_inc(h1_made.sem, 1)
                        if more > 1:
                            make_u(unit + 2, par)
                        if back:
                            make_hi(unit - 1, 1 - par)

                    make_u(0, 0)
                    act_squaring(act, EARLY - 1, eig_junk)
                    make_u(1, 1)
                    walk(act, body)
                    make_hi(UNITS - 1, 1)

                @block.tensor
                def _(pe):
                    for c in (a0_mm, w0_mm, a1_mm, w1_mm, sq_mm, tr_mm):
                        c.start(pe)
                    pe.wait_ge(const_made, 5)
                    pe.wait_ge(consts_loaded, 80)
                    pe.wait_ge(eig, 7)
                    for k in range(2):
                        last = nc.tensor.matmul(ps[:, 0, 0:T], ones[:], adjT[:, k, :], start=k == 0, stop=k == 1)
                    last.then_inc(eig, 1)
                    pe.wait_ge(eig, 9)

                    def graph(src, bank):
                        for b in range(UB):
                            for k in range(2):
                                last = nc.tensor.matmul(ps[:, bank, b * T:(b + 1) * T], src[:, 2 * b + k, :],
                                                        adjT[:, k, :], start=k == 0, stop=k == 1)
                        return last

                    def graph_u(unit, par):
                        pe.wait_ge(u_made.sem, u_made.done(unit))
                        pe.wait_ge(a0_out.sem, a0_out.done(unit - 1))
                        graph(u[:, par, :, :], PS_A0).then_inc(a0_mm.sem, 1)

                    def weights1(unit):
                        pe.wait_ge(a1_out.sem, a1_out.done(unit))
                        pe.wait_ge(y1_out.sem, y1_out.done(unit - 1))
                        nc.tensor.matmul(ps[:, PS_W1, :], Wg[:, 1, :], A1[:], start=True,
                                         stop=True).then_inc(w1_mm.sem, 1)

                    def body(unit, par, back, more):
                        pe.wait_ge(a0_out.sem, a0_out.done(unit))
                        pe.wait_ge(y0_out.sem, y0_out.done(unit - 1))
                        for k in range(UT):
                            last = nc.tensor.matmul(ps[:, PS_W0, k * P:(k + 1) * P], A0[:, k * P:(k + 1) * P],
                                                    Wg[:, 0, :], start=True, stop=True)
                        last.then_inc(w0_mm.sem, 1)
                        if more:
                            graph_u(unit + 1, 1 - par)
                        if back:
                            weights1(unit - 1)
                        pe.wait_ge(h1_made.sem, h1_made.done(unit))
                        pe.wait_ge(a1_out.sem, a1_out.done(unit - 1))
                        graph(h1, PS_A1).then_inc(a1_mm.sem, 1)

                    for n in range(EARLY):
                        pe_squaring(pe, n)
                    graph_u(0, 0)
                    walk(pe, body)
                    weights1(UNITS - 1)

        with ExitStack() as ctx:
            names = ("gi", "gf", "gg", "go", "cell", "tc", "h32")
            buf = {n: sb(f"{n}_l", [P, LANES, 512], F32, ctx) for n in names}
            hhi = sb("hhi_l", [P, LANES, 512], F32R, ctx)
            hlo = sb("hlo_l", [P, LANES, 512], F32R, ctx)
            NSTEP = len(STEPS)
            RSTEP = recurrent(NSTEP)
            gate_mm = [[count(f"gate_mm{L}_{g}", RSTEP if g == F else NSTEP) for g in range(4)] for L in range(LANES)]
            gate_act = [[count(f"gate_act{L}_{g}", RSTEP if g == F else NSTEP) for g in range(4)] for L in range(LANES)]
            terms = [count(f"terms{L}", 2 * RSTEP) for L in range(LANES)]
            cell_made = [count(f"cell_made{L}", NSTEP) for L in range(LANES)]
            tanh_made = [count(f"tanh_made{L}", NSTEP) for L in range(LANES)]
            h_made = [count(f"h_made{L}", NSTEP) for L in range(LANES)]
            h_hi = [count(f"h_hi{L}", NSTEP) for L in range(LANES)]
            h_lo = [count(f"h_lo{L}", NSTEP) for L in range(LANES)]

            def walk_steps(first, second, turn):
                for n in range(NSTEP):
                    starts = STEPS[n][4] == 0
                    for L in range(LANES):
                        first(turn, L, n)
                        if not starts:
                            second(turn, L, n)
                    if starts:
                        for L in range(LANES):
                            second(turn, L, n)

            def width(n):
                return STEPS[n][2] * STEPS[n][3]

            def state(H, turn, L, n, t, windows):
                p, b0, nb, _, _ = STEPS[n]
                return H[:, bass.ds(turn * (LANES * LANE_B) + (L * LANE_B + b0), nb), t:t + (windows - 1) * p + 1:p]

            with nc.Block() as block:
                @block.tensor
                def _(pe):
                    for L in range(LANES):
                        for g in range(4):
                            gate_mm[L][g].start(pe)

                    def step(turn, L, n):
                        p, b0, nb, windows, t = STEPS[n]
                        N = width(n)
                        pe.wait_ge(gate_act[L][O].sem, gate_act[L][O].done(turn, n))
                        if t == 0 and last_writer(n):
                            pe.wait_ge(h_lo[L].sem, h_lo[L].done(turn, last_writer(n)))
                        xs = [state(H, turn, L, n, t, windows) for H in (Hhi, Hlo)]
                        hs = [H[:, L, 0:N] for H in (hhi, hlo)]
                        order = (I, G, F, O) if t else (I, G, O)
                        def mm(W, g, w, v, start=False, stop=False):
                            return nc.tensor.matmul(ps[:, 4 * L + g, 0:N], W[:, w, p - 1, g * P:(g + 1) * P], v,
                                                    start=start, stop=stop)
                        for g in order:
                            mm(WX, g, 0, xs[0], start=True)
                            mm(WX, g, 0, xs[1])
                            last = mm(WX, g, 1, xs[0], stop=t == 0)
                            if t == 0:
                                last.then_inc(gate_mm[L][g].sem, 1)
                        if t == 0:
                            return
                        pe.wait_ge(h_hi[L].sem, h_hi[L].done(turn, n))
                        for g in (I, G):
                            mm(WH, g, 0, hs[0])
                            mm(WH, g, 1, hs[0])
                        pe.wait_ge(h_lo[L].sem, h_lo[L].done(turn, n))
                        for g in (I, G):
                            mm(WH, g, 0, hs[1], stop=True).then_inc(gate_mm[L][g].sem, 1)
                        for g in (F, O):
                            mm(WH, g, 0, hs[0])
                            mm(WH, g, 1, hs[0])
                            mm(WH, g, 0, hs[1], stop=True).then_inc(gate_mm[L][g].sem, 1)

                    with pe.Fori(0, LSTM_TURNS) as turn:
                        for n in range(NSTEP):
                            for L in range(LANES):
                                step(turn, L, n)

                @block.scalar
                def _(act):
                    for L in range(LANES):
                        tanh_made[L].start(act)
                        for g in range(4):
                            gate_act[L][g].start(act)
                    dst = {I: "gi", F: "gf", G: "gg", O: "go"}

                    def gates(turn, L, n):
                        p, b0, nb, windows, t = STEPS[n]
                        N = width(n)
                        act.wait_ge(cell_made[L].sem, cell_made[L].done(turn, n))
                        act.wait_ge(h_made[L].sem, h_made[L].done(turn, n))
                        for g in ((I, G, F, O) if t else (I, G, O)):
                            seen = recurrent(n + 1) if g == F else n + 1
                            act.wait_ge(gate_mm[L][g].sem, gate_mm[L][g].done(turn, seen))
                            a = nc.scalar.activation(buf[dst[g]][:, L, 0:N], ps[:, 4 * L + g, 0:N],
                                                     ACT.Tanh if g == G else ACT.Sigmoid,
                                                     bias=bias[:, 4 * (p - 1) + g:4 * (p - 1) + g + 1])
                            a.then_inc(gate_act[L][g].sem, 1)

                    def tanh_cell(turn, L, n):
                        N = width(n)
                        act.wait_ge(cell_made[L].sem, cell_made[L].done(turn, n + 1))
                        nc.scalar.activation(buf["tc"][:, L, 0:N], buf["cell"][:, L, 0:N],
                                             ACT.Tanh).then_inc(tanh_made[L].sem, 1)

                    with act.Fori(0, LSTM_TURNS) as turn:
                        walk_steps(gates, tanh_cell, turn)

                @block.vector
                def _(dve):
                    for L in range(LANES):
                        for c in (terms, cell_made, h_made, h_hi, h_lo):
                            c[L].start(dve)

                    def cell(turn, L, n):
                        p, b0, nb, windows, t = STEPS[n]
                        N = width(n)
                        v = {k: b[:, L, 0:N] for k, b in buf.items()}
                        dve.wait_ge(gate_act[L][G].sem, gate_act[L][G].done(turn, n + 1))
                        if t == 0:
                            dve.wait_ge(tanh_made[L].sem, tanh_made[L].done(turn, n))
                            nc.vector.tensor_tensor(v["cell"], v["gi"], v["gg"], ALU.mult).then_inc(cell_made[L].sem, 1)
                        else:
                            nc.vector.tensor_tensor(v["gi"], v["gi"], v["gg"], ALU.mult).then_inc(terms[L].sem, 1)
                            dve.wait_ge(gate_act[L][F].sem, gate_act[L][F].done(turn, recurrent(n + 1)))
                            nc.vector.tensor_tensor(v["gf"], v["gf"], v["cell"], ALU.mult).then_inc(terms[L].sem, 1)
                            dve.wait_ge(terms[L].sem, terms[L].done(turn, 2 * recurrent(n + 1)))
                            nc.vector.tensor_tensor(v["cell"], v["gi"], v["gf"], ALU.add).then_inc(cell_made[L].sem, 1)

                    def hidden(turn, L, n):
                        p, b0, nb, windows, t = STEPS[n]
                        N = width(n)
                        v = {k: b[:, L, 0:N] for k, b in buf.items()}
                        dve.wait_ge(tanh_made[L].sem, tanh_made[L].done(turn, n + 1))
                        nc.vector.tensor_tensor(v["h32"], v["go"], v["tc"], ALU.mult).then_inc(h_made[L].sem, 1)
                        dve.wait_ge(h_made[L].sem, h_made[L].done(turn, n + 1))
                        if t < p - 1:
                            h, hi, lo = v["h32"], hhi[:, L, 0:N], hlo[:, L, 0:N]
                        else:
                            h = v["h32"].rearrange("p (b w) -> p b w", b=nb)[:, :, 0:T // p]
                            hi, lo = (state(H, turn, L, n, t, T // p) for H in (Hhi, Hlo))
                        nc.vector.tensor_copy(hi, h).then_inc(h_hi[L].sem, 1)
                        dve.wait_ge(h_hi[L].sem, h_hi[L].done(turn, n + 1))
                        nc.vector.tensor_tensor(lo, h, hi.bitcast(F32), ALU.subtract).then_inc(h_lo[L].sem, 1)

                    with dve.Fori(0, LSTM_TURNS) as turn:
                        walk_steps(cell, hidden, turn)

        with ExitStack() as ctx:
            h32 = sb("h_sum", [P, 2, UB, T], F32, ctx)
            eig_junk = sb("ray_junk", [P, 2, T], F32, ctx)
            sq_junk = sb("sq_junk", [P, 2, T], F32, ctx)
            quotient = sb("quotient", [P, 2], F32, ctx)
            lam = sb("lam", [P, 3], F32, ctx)
            lt_made = sem("lt_made")
            sum_made = count("sum_made")
            h_turned = count("h_turned")
            x_added = count("x_added")
            with nc.Block() as block:
                @block.gpsimd
                def _(pool):
                    sum_made.start(pool)
                    with pool.Fori(0, UNITS // 2) as g:
                        for s in range(2):
                            b = bass.ds(g * (2 * UB) + s * UB, UB)
                            pool.wait_ge(h_turned.sem, h_turned.done(g * 2 + s - 2))
                            nc.gpsimd.tensor_tensor(h32[:, s, :, :], Hhi[:, b, 0:T].bitcast(F32),
                                                    Hlo[:, b, 0:T].bitcast(F32), ALU.add).then_inc(sum_made.sem, 1)

                @block.vector
                def _(dve):
                    x_added.start(dve)

                    def add(g, s):
                        dve.wait_ge(h_turned.sem, h_turned.done(g * 2 + s))
                        tiles = X[:, bass.ds(g * (2 * UT) + s * UT, UT), :]
                        nc.vector.tensor_tensor(tiles, ps[:, s, :].rearrange("p (a b) -> p a b", a=UT), tiles,
                                                ALU.add).then_inc(x_added.sem, 1)
                        dve.wait_ge(x_added.sem, x_added.done(g * 2 + s))
                        for k in range(UT):
                            tile = bass.ds(g * (2 * UT) + (s * UT + k), 1)
                            nc.vector.bn_stats(bn[:, tile, :].rearrange("p a b -> p (a b)"),
                                               X[:, tile, :].rearrange("p a b -> p (a b)")).then_inc(bn_made, 1)

                    with dve.Fori(0, LATE) as g:
                        add(g, 0)
                        dve_squaring(dve, g + EARLY)
                        add(g, 1)
                    dve.wait_ge(sq_mm.sem, sq_mm.done(SQUARINGS))
                    nc.vector.tensor_tensor_reduce(eig_junk[:].rearrange("p a b -> p (a b)"),
                                                   M[:].rearrange("p a b -> p (a b)"), ps[:, PS_SQ, :], 1.0, 0.0,
                                                   ALU.mult, ALU.add, quotient[:, 0:1]).then_inc(eig, 1)
                    dve.wait_ge(eig, 10)
                    nc.vector.tensor_tensor_reduce(eig_junk[:], M[:], M[:], 1.0, 0.0, ALU.mult, ALU.add,
                                                   quotient[:, 1:2]).then_inc(eig, 1)
                    for g in range(LATE, UNITS // 2):
                        for s in range(2):
                            add(g, s)
                    dve.wait_ge(bn_made, TILES // CHUNK + TILES)
                    layernorm_stats(dve, None, 8)
                    dve.wait_ge(eig, 12)
                    nc.vector.reciprocal(lam[:, 0:1], ps[:, PS_TR, 1:2]).then_inc(eig, 1)
                    dve.wait_ge(eig, 13)
                    nc.vector.tensor_tensor(lam[:, 1:2], ps[:, PS_TR, 0:1], lam[:, 0:1], ALU.mult).then_inc(eig, 1)
                    dve.wait_ge(eig, 14)
                    nc.vector.tensor_scalar(lam[:, 1:2], lam[:, 1:2], 1e-8, 0.5, ALU.add, ALU.mult).then_inc(eig, 1)
                    dve.wait_ge(eig, 15)
                    nc.vector.reciprocal(lam[:, 2:3], lam[:, 1:2]).then_inc(eig, 1)
                    dve.wait_ge(eig, 16)
                    nc.vector.scalar_tensor_tensor(LT[:], adjT[:], lam[:, 2:3], ident2[:], ALU.mult,
                                                   ALU.subtract).then_inc(lt_made, 1)
                    dve.wait_ge(lt_made, 1)

                @block.scalar
                def _(act):
                    with act.Fori(0, LATE) as g:
                        act_squaring(act, g + EARLY, sq_junk)
                    layernorm_stats(None, act, 8)

                @block.tensor
                def _(pe):
                    h_turned.start(pe)

                    def turn(g, s):
                        pe.wait_ge(sum_made.sem, sum_made.done(g * 2 + s))
                        pe.wait_ge(x_added.sem, x_added.done(g * 2 + s - 2))
                        for k in range(UT):
                            last = nc.tensor.transpose(ps[:, s, k * P:(k + 1) * P],
                                                       h32[:, s, k // 2, (k % 2) * P:(k % 2 + 1) * P], ident)
                        last.then_inc(h_turned.sem, 1)

                    with pe.Fori(0, LATE) as g:
                        turn(g, 0)
                        pe_squaring(pe, g + EARLY)
                        turn(g, 1)
                    pe.wait_ge(m_made.sem, m_made.done(SQUARINGS - 1))
                    pe_product(pe, S, sq_mm.sem, 1)
                    for g in range(LATE, UNITS // 2):
                        for s in range(2):
                            turn(g, s)
                    pe.wait_ge(eig, 11)
                    nc.tensor.matmul(ps[:, PS_TR, 0:2], ones[:], quotient[:], start=True, stop=True).then_inc(eig, 1)
        lstm_ctx.close()

        X2 = sb("X2", [P, TILES, D])
        X2T = sb("X2T", [P, NB * T])
        with ExitStack() as ctx:
            u = sb("u1", [P, 2, UT, D], F32, ctx)
            xpT = sb("xpT", [P, UW], F32, ctx)
            t1 = sb("t1", [P, UT, D], F32, ctx)
            z1 = sb("z1", [P, UT, D], F32, ctx)
            x1 = sb("x1", [P, UT, D], F32, ctx)
            x1b = sb("x1b", [P, 2, UT, D], F32, ctx)
            x1T = sb("x1T", [P, 2, UW], F32, ctx)
            bn1 = sb("bn1", [P, 2, UT, 6], F32, ctx)
            mo1 = sb("mo1", [P, 2, 6, UT], F32, ctx)
            ve1 = sb("ve1", [P, 2, UT], F32, ctx)
            rs1 = sb("rs1", [P, 2, UT], F32, ctx)
            nm1 = sb("nm1", [P, 2, UT], F32, ctx)
            q = [sb(f"q_{n}", [P, UW], F32R, ctx) for n in ("hi", "lo")]
            k_ = [sb(f"k_{n}", [P, UW], F32R, ctx) for n in ("hi", "lo")]
            V3 = sb("V3", [P, 2, 3, UT, HEADS, HD + 1], BF16, ctx)
            zero = sb("zero", [P, HD], F32, ctx)
            vrest = sb("vrest", [P, UT, HEADS, HD], F32, ctx)
            negmax = sb("negmax", [P, 2, HEADS], F32, ctx)
            prob = sb("prob", [P, 2, HEADS, T], F32, ctx)
            probT = sb("probT", [P, 2, 2, 2 * HEADS, P], F16, ctx)
            rden = sb("rden", [P, HEADS], F32, ctx)
            o_sb = sb("o_sb", [P, UT, D], F32, ctx)
            oT = sb("oT", [P, UW], F32, ctx)
            y2 = sb("y2", [P, UT, D], F32, ctx)
            z2 = sb("z2", [P, UT, D], F32, ctx)
            x2 = sb("x2", [P, UT, D], F32, ctx)

            u1_made = count("u1_made")
            xp_mm = count("xp_mm")
            xp_out = count("xp_out")
            wc_mm = count("wc_mm")
            t1_out = count("t1_out")
            ln_stats = [count("ln1_stats", 4), count("ln2_stats", 4)]
            ln_rstd = [count("ln1_rstd", 3), count("ln2_rstd", 3)]
            z_made = [count("z1_made"), count("z2_made")]
            zg_made = [count("zg1_made"), count("zg2_made")]
            zb_made = [count("zb1_made"), count("zb2_made")]
            x1_made = count("x1_made")
            x1b_made = count("x1b_made")
            x1T_mm = count("x1T_mm")
            x1T_out = count("x1T_out")
            q_mm = count("q_mm")
            k_mm = count("k_mm")
            v_mm = count("v_mm")
            q_hi = count("q_hi")
            q_lo = count("q_lo")
            k_hi = count("k_hi")
            k_lo = count("k_lo")
            v_1 = count("v_1")
            v_rest = count("v_rest")
            v_2 = count("v_2")
            v_3 = count("v_3")
            s_half = count("s_half", UT)
            s_mm = count("s_mm", UT)
            max_made = count("max_made", UT)
            exp_made = count("exp_made", UT)
            pT_mm = count("pT_mm", UT)
            pT_hi = count("pT_hi", UT)
            pT_lo = count("pT_lo", UT)
            o_mm = count("o_mm", UT)
            rden_made = count("rden_made", UT)
            o_out = count("o_out", UT)
            oT_mm = count("oT_mm")
            oT_out = count("oT_out")
            wo_mm = count("wo_mm")
            y2_out = count("y2_out")
            late_sums = count("late_sums", 2)
            x2T_mm = count("x2T_mm")
            x2T_out = count("x2T_out")
            v_ones = sem("v_ones")
            PS_T, PS_O, PS_G = 4, 6, 7

            def scores(s):
                return ps[:, 2 * (s % 2):2 * (s % 2) + 2, :].rearrange("p a (b c) -> p (a b) c", b=2)

            def head(j):
                return j // 2 + 2 * (j % 2)

            with nc.Block() as block:
                @block.gpsimd
                def _(pool):
                    for c in (*ln_rstd, *zg_made, *zb_made, x1b_made, v_2, v_3, late_sums):
                        c.start(pool)
                    nc.gpsimd.memset(zero[:], 0.0).then_inc(v_ones, 1)
                    for par in range(2):
                        for part in range(3):
                            nc.gpsimd.memset(V3[:, par, part, :, :, HD:HD + 1], float(part == 0)).then_inc(v_ones, 1)

                    pool.wait_ge(v_ones, 7)

                    def rstd_of(n, unit):
                        pool.wait_ge(ln_stats[n].sem, ln_stats[n].done(unit))
                        nc.gpsimd.tensor_tensor(ve1[:, n, :], mo1[:, n, VAR, :], eps[:],
                                                ALU.add).then_inc(ln_rstd[n].sem, 1)
                        pool.wait_ge(ln_rstd[n].sem, ln_rstd[n].done(unit, 1))
                        nc.gpsimd.tensor_tensor(rs1[:, n, :], ve1[:, n, :], minus_half[:],
                                                ALU.pow).then_inc(ln_rstd[n].sem, 1)
                        pool.wait_ge(ln_rstd[n].sem, ln_rstd[n].done(unit, 2))
                        nc.gpsimd.tensor_tensor(nm1[:, n, :], mo1[:, n, NMEAN, :], rs1[:, n, :],
                                                ALU.mult).then_inc(ln_rstd[n].sem, 1)

                    def scale(n, unit, z, gain, shift, dst):
                        pool.wait_ge(z_made[n].sem, z_made[n].done(unit))
                        nc.gpsimd.tensor_tensor(z[:], z[:], row(gain), ALU.mult).then_inc(zg_made[n].sem, 1)
                        pool.wait_ge(zg_made[n].sem, zg_made[n].done(unit))
                        nc.gpsimd.tensor_tensor(dst[:], z[:], row(shift), ALU.add).then_inc(zb_made[n].sem, 1)

                    def keep_x1(unit, par):
                        pool.wait_ge(x1_made.sem, x1_made.done(unit))
                        pool.wait_ge(y2_out.sem, y2_out.done(unit - 2))
                        nc.gpsimd.tensor_tensor(x1b[:, par, :, :], x1[:], row(BO), ALU.add).then_inc(x1b_made.sem, 1)

                    def split_v(unit, par):
                        parts = [V3[:, par, n, :, :, 0:HD].rearrange("p a h c -> p (a h) c") for n in range(3)]
                        rest = vrest[:].rearrange("p a h c -> p (a h) c")
                        zeros = zero[:].unsqueeze(1).broadcast_to([P, UT * HEADS, HD])
                        pool.wait_ge(v_rest.sem, v_rest.done(unit))
                        nc.gpsimd.tensor_tensor(parts[1], rest, zeros, ALU.add).then_inc(v_2.sem, 1)
                        pool.wait_ge(v_2.sem, v_2.done(unit))
                        nc.gpsimd.tensor_tensor(parts[2], rest, parts[1], ALU.subtract).then_inc(v_3.sem, 1)

                    def make_x2(unit):
                        pool.wait_ge(x2T_mm.sem, x2T_mm.done(unit - 1))
                        scale(1, unit, z2, G2, BE2, x2)
                        pool.wait_ge(zb_made[1].sem, zb_made[1].done(unit))
                        tiles = bass.ds(unit * UT, UT)
                        nc.gpsimd.tensor_tensor(X2[:, tiles, :], x2[:], row(B2), ALU.add).then_inc(late_sums.sem, 1)
                        nc.gpsimd.tensor_tensor(X[:, tiles, :], X[:, tiles, :], row(BE3),
                                                ALU.add).then_inc(late_sums.sem, 1)

                    def body(unit, par, back, more):
                        if more:
                            rstd_of(0, unit + 1)
                            scale(0, unit + 1, z1, G1, BE1, z1)
                        if back:
                            rstd_of(1, unit - 1)
                        if more:
                            keep_x1(unit + 1, 1 - par)
                            split_v(unit + 1, 1 - par)
                        if back:
                            make_x2(unit - 1)

                    rstd_of(0, 0)
                    scale(0, 0, z1, G1, BE1, z1)
                    keep_x1(0, 0)
                    split_v(0, 0)
                    walk(pool, body)
                    rstd_of(1, UNITS - 1)
                    make_x2(UNITS - 1)
                    pool.wait_ge(late_sums.sem, late_sums.done(UNITS - 1))

                @block.scalar
                def _(act):
                    for c in (u1_made, xp_out, *z_made, x1T_out, q_hi, k_hi, v_1, exp_made, pT_hi, oT_out, x2T_out):
                        c.start(act)

                    def make_u(unit, par):
                        act.wait_ge(x1_made.sem, x1_made.done(unit - 2))
                        for k in range(UT):
                            tile = bass.ds(unit * UT + k, 1)
                            last = nc.scalar.activation(u[:, par, k, :], X[:, tile, :].rearrange("p a b -> p (a b)"),
                                                        ACT.Relu, bias=nmr[:, tile], scale=rstd[:, tile])
                        last.then_inc(u1_made.sem, 1)

                    def take(unit, mm, dst, out):
                        act.wait_ge(mm.sem, mm.done(unit))
                        nc.scalar.activation(dst, ps[:, PS_G, :], ACT.Copy).then_inc(out.sem, 1)

                    def xp(unit):
                        act.wait_ge(wc_mm.sem, wc_mm.done(unit - 1))
                        take(unit, xp_mm, xpT[:], xp_out)

                    def turn_x1(unit, par):
                        act.wait_ge(v_mm.sem, v_mm.done(unit - 2))
                        take(unit, x1T_mm, x1T[:, par, :], x1T_out)

                    def turn_o(unit):
                        act.wait_ge(wo_mm.sem, wo_mm.done(unit - 1))
                        take(unit, oT_mm, oT[:], oT_out)

                    def turn_x2(unit):
                        take(unit, x2T_mm, X2T[:, bass.ds(unit * UW, UW)], x2T_out)

                    def normalise(n, unit, src, z):
                        act.wait_ge(ln_rstd[n].sem, ln_rstd[n].done(unit))
                        act.wait_ge((x1_made if n == 0 else zb_made[1]).sem,
                                    (x1_made if n == 0 else zb_made[1]).done(unit - 1))
                        for k in range(UT):
                            last = nc.scalar.activation(z[:, k, :], src[:, k, :], ACT.Identity,
                                                        bias=nm1[:, n, k:k + 1], scale=rs1[:, n, k:k + 1])
                        last.then_inc(z_made[n].sem, 1)

                    def qkv(unit, par):
                        act.wait_ge(q_mm.sem, q_mm.done(unit))
                        nc.scalar.activation(q[0][:], ps[:, 0, :], ACT.Copy, scale=SCALE).then_inc(q_hi.sem, 1)
                        act.wait_ge(k_mm.sem, k_mm.done(unit))
                        nc.scalar.activation(k_[0][:], ps[:, 1, :], ACT.Copy).then_inc(k_hi.sem, 1)
                        act.wait_ge(v_mm.sem, v_mm.done(unit))
                        act.wait_ge(o_mm.sem, o_mm.done(unit - 2))
                        nc.scalar.activation(V3[:, par, 0, :, :, 0:HD].rearrange("p a h c -> p (a h) c"),
                                             ps[:, PS_G, :].rearrange("p (a c) -> p a c", c=HD),
                                             ACT.Copy).then_inc(v_1.sem, 1)

                    def exps(unit, s):
                        act.wait_ge(max_made.sem, max_made.done(unit, s + 1))
                        act.wait_ge(pT_mm.sem, pT_mm.done(unit, s - 1))
                        for h in range(HEADS):
                            last = nc.scalar.activation(prob[:, s % 2, h, :], scores(s)[:, h, :], ACT.Exp,
                                                        bias=negmax[:, s % 2, h:h + 1])
                        last.then_inc(exp_made.sem, 1)

                    def turn_p(unit, s):
                        act.wait_ge(pT_mm.sem, pT_mm.done(unit, s + 1))
                        act.wait_ge(o_mm.sem, o_mm.done(unit, s - 1))
                        nc.scalar.activation(probT[:, s % 2, 0, :, :].rearrange("p a b -> p (a b)"),
                                             ps[:, PS_T:PS_T + 2, :].rearrange("p a b -> p (a b)"),
                                             ACT.Copy).then_inc(pT_hi.sem, 1)

                    def body(unit, par, back, more):
                        if more > 1:
                            make_u(unit + 2, par)
                        turn_p(unit, 0)
                        exps(unit, 1)
                        if more:
                            normalise(0, unit + 1, t1, z1)
                        if back:
                            turn_o(unit - 1)
                        turn_p(unit, 1)
                        exps(unit, 2)
                        if back > 1:
                            turn_x2(unit - 2)
                        if more:
                            turn_x1(unit + 1, 1 - par)
                        turn_p(unit, 2)
                        exps(unit, 3)
                        if more:
                            qkv(unit + 1, 1 - par)
                        if back:
                            normalise(1, unit - 1, y2, z2)
                        turn_p(unit, 3)
                        if more > 1:
                            xp(unit + 2)
                        if more:
                            exps(unit + 1, 0)

                    make_u(0, 0)
                    xp(0)
                    make_u(1, 1)
                    normalise(0, 0, t1, z1)
                    turn_x1(0, 0)
                    qkv(0, 0)
                    xp(1)
                    exps(0, 0)
                    walk(act, body)
                    turn_o(UNITS - 1)
                    turn_x2(UNITS - 2)
                    normalise(1, UNITS - 1, y2, z2)
                    turn_x2(UNITS - 1)

                @block.vector
                def _(dve):
                    for c in (t1_out, *ln_stats, x1_made, q_lo, k_lo, v_rest, max_made, pT_lo, rden_made, o_out,
                              y2_out):
                        c.start(dve)

                    def moments(n, unit, src):
                        for k in range(UT):
                            last = nc.vector.bn_stats(bn1[:, n, k, :], src[:, k, :])
                        last.then_inc(ln_stats[n].sem, 1)
                        dve.wait_ge(ln_stats[n].sem, ln_stats[n].done(unit, 1))
                        moments_of(dve, bn1[:, n, :, :], mo1[:, n, :, :], ln_stats[n], unit, 1)

                    def conv(unit):
                        dve.wait_ge(wc_mm.sem, wc_mm.done(unit))
                        dve.wait_ge(z_made[0].sem, z_made[0].done(unit - 1))
                        nc.vector.tensor_tensor(t1[:], ps[:, PS_G, :].rearrange("p (a b) -> p a b", a=UT), row(BC),
                                                ALU.add).then_inc(t1_out.sem, 1)

                    def moments_t1(unit):
                        dve.wait_ge(t1_out.sem, t1_out.done(unit))
                        moments(0, unit, t1)

                    def make_x1(unit, par):
                        dve.wait_ge(zb_made[0].sem, zb_made[0].done(unit))
                        dve.wait_ge(x1T_mm.sem, x1T_mm.done(unit - 1))
                        dve.wait_ge(x1b_made.sem, x1b_made.done(unit - 1))
                        nc.vector.scalar_tensor_tensor(x1[:].rearrange("p a b -> p (a b)"),
                                                       z1[:].rearrange("p a b -> p (a b)"), 0.0,
                                                       u[:, par, :, :].rearrange("p a b -> p (a b)"),
                                                       ALU.max, ALU.add).then_inc(x1_made.sem, 1)

                    def qkv(unit, par):
                        dve.wait_ge(q_hi.sem, q_hi.done(unit))
                        nc.vector.scalar_tensor_tensor(q[1][:], ps[:, 0, :], SCALE, q[0][:].bitcast(F32), ALU.mult,
                                                       ALU.subtract).then_inc(q_lo.sem, 1)
                        dve.wait_ge(k_hi.sem, k_hi.done(unit))
                        nc.vector.tensor_tensor(k_[1][:], ps[:, 1, :], k_[0][:].bitcast(F32),
                                                ALU.subtract).then_inc(k_lo.sem, 1)
                        dve.wait_ge(v_1.sem, v_1.done(unit))
                        dve.wait_ge(v_3.sem, v_3.done(unit - 1))
                        nc.vector.tensor_tensor(vrest[:].rearrange("p a h c -> p (a h) c"),
                                                ps[:, PS_G, :].rearrange("p (a c) -> p a c", c=HD),
                                                V3[:, par, 0, :, :, 0:HD].rearrange("p a h c -> p (a h) c"),
                                                ALU.subtract).then_inc(v_rest.sem, 1)

                    def row_max(unit, s):
                        dve.wait_ge(s_mm.sem, s_mm.done(unit, s + 1))
                        dve.wait_ge(exp_made.sem, exp_made.done(unit, s - 1))
                        nc.vector.tensor_reduce(negmax[:, s % 2, :], scores(s), AX.X, ALU.max,
                                                negate=True).then_inc(max_made.sem, 1)

                    def turn_p(unit, s):
                        dve.wait_ge(pT_hi.sem, pT_hi.done(unit, s + 1))
                        hi, lo = (probT[:, s % 2, n, :, :].rearrange("p a b -> p (a b)") for n in range(2))
                        nc.vector.tensor_tensor(lo, ps[:, PS_T:PS_T + 2, :].rearrange("p a b -> p (a b)"), hi,
                                                ALU.subtract).then_inc(pT_lo.sem, 1)

                    def make_o(unit, s):
                        dve.wait_ge(o_mm.sem, o_mm.done(unit, s + 1))
                        acc = ps[:, PS_O, 0:HEADS * (HD + 1)].rearrange("p (h c) -> p h c", h=HEADS)
                        nc.vector.reciprocal(rden[:].unsqueeze(2), acc[:, :, HD:HD + 1]).then_inc(rden_made.sem, 1)
                        dve.wait_ge(rden_made.sem, rden_made.done(unit, s + 1))
                        dve.wait_ge(oT_mm.sem, oT_mm.done(unit - 1))
                        nc.vector.tensor_tensor(o_sb[:, s, :].rearrange("p (h c) -> p h c", h=HEADS), acc[:, :, 0:HD],
                                                rden[:].unsqueeze(2).broadcast_to([P, HEADS, HD]),
                                                ALU.mult).then_inc(o_out.sem, 1)

                    def add_o(unit, par):
                        dve.wait_ge(wo_mm.sem, wo_mm.done(unit))
                        dve.wait_ge(x1b_made.sem, x1b_made.done(unit))
                        dve.wait_ge(z_made[1].sem, z_made[1].done(unit - 1))
                        nc.vector.tensor_tensor(y2[:], ps[:, PS_O, :].rearrange("p (a b) -> p a b", a=UT),
                                                x1b[:, par, :, :], ALU.add).then_inc(y2_out.sem, 1)

                    def moments_y2(unit):
                        dve.wait_ge(y2_out.sem, y2_out.done(unit))
                        moments(1, unit, y2)

                    def body(unit, par, back, more):
                        if more:
                            conv(unit + 1)
                        row_max(unit, 1)
                        if back:
                            make_o(unit - 1, 3)
                        if more:
                            moments_t1(unit + 1)
                        turn_p(unit, 0)
                        row_max(unit, 2)
                        make_o(unit, 0)
                        turn_p(unit, 1)
                        if back:
                            add_o(unit - 1, 1 - par)
                        if more:
                            make_x1(unit + 1, 1 - par)
                        row_max(unit, 3)
                        make_o(unit, 1)
                        if back:
                            moments_y2(unit - 1)
                        turn_p(unit, 2)
                        if more:
                            qkv(unit + 1, 1 - par)
                        make_o(unit, 2)
                        turn_p(unit, 3)
                        if more:
                            row_max(unit + 1, 0)

                    conv(0)
                    moments_t1(0)
                    make_x1(0, 0)
                    dve.wait_ge(v_ones, 7)
                    qkv(0, 0)
                    row_max(0, 0)
                    walk(dve, body)
                    make_o(UNITS - 1, 3)
                    add_o(UNITS - 1, 1)
                    moments_y2(UNITS - 1)

                @block.tensor
                def _(pe):
                    for c in (s_half, xp_mm, wc_mm, x1T_mm, q_mm, k_mm, v_mm, s_mm, pT_mm, o_mm, oT_mm, wo_mm, x2T_mm):
                        c.start(pe)
                    pe.wait_ge(l1_loaded, 7 * 16)

                    def xp(unit, par):
                        pe.wait_ge(u1_made.sem, u1_made.done(unit))
                        pe.wait_ge(v_rest.sem, v_rest.done(unit - 1))
                        for b in range(UB):
                            for k in range(2):
                                last = nc.tensor.matmul(ps[:, PS_G, b * T:(b + 1) * T], u[:, par, 2 * b + k, :],
                                                        LT[:, k, :], start=k == 0, stop=k == 1)
                        last.then_inc(xp_mm.sem, 1)

                    def conv(unit):
                        pe.wait_ge(xp_out.sem, xp_out.done(unit))
                        for k in range(UT):
                            last = nc.tensor.matmul(ps[:, PS_G, k * P:(k + 1) * P], xpT[:, k * P:(k + 1) * P], Wc[:],
                                                    start=True, stop=True)
                        last.then_inc(wc_mm.sem, 1)

                    def turn(src, unit, sem):
                        for k in range(UT):
                            last = nc.tensor.transpose(ps[:, PS_G, k * P:(k + 1) * P], src[:, k, :], ident)
                        last.then_inc(sem, 1)

                    def turn_o(unit):
                        pe.wait_ge(o_out.sem, o_out.done(unit))
                        turn(o_sb, unit, oT_mm.sem)

                    def turn_x1(unit):
                        pe.wait_ge(x1_made.sem, x1_made.done(unit))
                        pe.wait_ge(oT_out.sem, oT_out.done(unit - 2))
                        pe.wait_ge(x2T_out.sem, x2T_out.done(unit - 3))
                        turn(x1, unit, x1T_mm.sem)

                    def turn_x2(unit):
                        pe.wait_ge(zb_made[1].sem, zb_made[1].done(unit))
                        pe.wait_ge(oT_out.sem, oT_out.done(unit + 1))
                        turn(x2, unit, x2T_mm.sem)

                    def out_proj(unit):
                        pe.wait_ge(oT_out.sem, oT_out.done(unit))
                        for k in range(UT):
                            last = nc.tensor.matmul(ps[:, PS_O, k * P:(k + 1) * P], oT[:, k * P:(k + 1) * P], Wo[:],
                                                    start=True, stop=True)
                        last.then_inc(wo_mm.sem, 1)

                    def qkv(unit, par):
                        pe.wait_ge(x1T_out.sem, x1T_out.done(unit))
                        pe.wait_ge(exp_made.sem, exp_made.done(unit - 1, 3))
                        nc.tensor.matmul(ps[:, 0, :], Wq[:], x1T[:, par, :], start=True, stop=True)\
                            .then_inc(q_mm.sem, 1)
                        nc.tensor.matmul(ps[:, 1, :], Wk[:], x1T[:, par, :], start=True, stop=True)\
                            .then_inc(k_mm.sem, 1)
                        for k in range(UT):
                            last = nc.tensor.matmul(ps[:, PS_G, k * P:(k + 1) * P], x1T[:, par, k * P:(k + 1) * P],
                                                    Wv[:], start=True, stop=True)
                        last.then_inc(v_mm.sem, 1)

                    def score(unit, s, half):
                        if s == 0 and half == 0:
                            pe.wait_ge(q_lo.sem, q_lo.done(unit))
                            pe.wait_ge(k_lo.sem, k_lo.done(unit))
                        if half == 0:
                            pe.wait_ge(exp_made.sem, exp_made.done(unit, s - 1))
                        else:
                            pe.wait_ge(s_half.sem, s_half.done(unit, s + 1))
                        b, qt = divmod(s, 2)
                        for bank in range(2):
                            nc.tensor.matmul(scores(s)[:, 2 * bank + half, :], identb[:], maskb[:, qt, :],
                                             start=True, stop=False)
                        for n, (a, c) in enumerate(((0, 0), (0, 1), (1, 0))):
                            for bank in range(2):
                                j = 2 * bank + half
                                rows_h = slice(head(j) * HD, (head(j) + 1) * HD)
                                last = nc.tensor.matmul(scores(s)[:, j, :], q[a][rows_h, s * P:(s + 1) * P],
                                                        k_[c][rows_h, b * T:(b + 1) * T], start=False, stop=n == 2)
                        last.then_inc((s_half if half == 0 else s_mm).sem, 1)

                    def turn_p(unit, s):
                        pe.wait_ge(exp_made.sem, exp_made.done(unit, s + 1))
                        pe.wait_ge(pT_lo.sem, pT_lo.done(unit, s))
                        for j in range(HEADS):
                            for k in range(2):
                                at = (j % 2 * 2 + k) * P
                                last = nc.tensor.transpose(ps[:, PS_T + j // 2, at:at + P],
                                                           prob[:, s % 2, j, k * P:(k + 1) * P], ident)
                        last.then_inc(pT_mm.sem, 1)

                    def weigh_v(unit, par, s):
                        pe.wait_ge(pT_lo.sem, pT_lo.done(unit, s + 1))
                        pe.wait_ge(o_out.sem, o_out.done(unit, s))
                        if s == 0:
                            pe.wait_ge(v_3.sem, v_3.done(unit))
                        if s == 1:
                            pe.wait_ge(y2_out.sem, y2_out.done(unit - 1))
                        for j in range(HEADS):
                            h = head(j)
                            for k in range(2):
                                for n, (a, c) in enumerate(((0, 0), (0, 1), (0, 2), (1, 0), (1, 1))):
                                    last = nc.tensor.matmul(ps[:, PS_O, h * (HD + 1):(h + 1) * (HD + 1)],
                                                            probT[:, s % 2, a, 2 * j + k, :],
                                                            V3[:, par, c, s // 2 * 2 + k, h, :],
                                                            start=k + n == 0, stop=(k, n) == (1, 4))
                        last.then_inc(o_mm.sem, 1)

                    def body(unit, par, back, more):
                        if more:
                            conv(unit + 1)
                        score(unit, 1, 1)
                        if back:
                            weigh_v(unit - 1, 1 - par, 3)
                        turn_p(unit, 0)
                        score(unit, 2, 0)
                        if more:
                            pe.wait_ge(t1_out.sem, t1_out.done(unit + 1))
                        if back:
                            turn_o(unit - 1)
                        score(unit, 2, 1)
                        weigh_v(unit, par, 0)
                        turn_p(unit, 1)
                        score(unit, 3, 0)
                        if back:
                            pe.wait_ge(o_out.sem, o_out.done(unit, 1))
                            out_proj(unit - 1)
                        score(unit, 3, 1)
                        if back > 1:
                            turn_x2(unit - 2)
                        weigh_v(unit, par, 1)
                        if more:
                            turn_x1(unit + 1)
                        turn_p(unit, 2)
                        if more:
                            qkv(unit + 1, 1 - par)
                        weigh_v(unit, par, 2)
                        turn_p(unit, 3)
                        if more:
                            score(unit + 1, 0, 0)
                        if more > 1:
                            xp(unit + 2, par)
                        if more:
                            score(unit + 1, 0, 1)
                            score(unit + 1, 1, 0)

                    xp(0, 0)
                    conv(0)
                    turn_x1(0)
                    qkv(0, 0)
                    score(0, 0, 0)
                    xp(1, 1)
                    score(0, 0, 1)
                    score(0, 1, 0)
                    walk(pe, body)
                    weigh_v(UNITS - 1, 1, 3)
                    turn_o(UNITS - 1)
                    turn_x2(UNITS - 2)
                    out_proj(UNITS - 1)
                    pe.wait_ge(x2T_out.sem, x2T_out.done(UNITS - 2))
                    pe.wait_ge(zb_made[1].sem, zb_made[1].done(UNITS - 1))
                    turn(x2, UNITS - 1, x2T_mm.sem)

        with ExitStack() as ctx:
            hid = sb("hid", [P, 2, 2, UW], F32, ctx)
            y3 = sb("y3", [P, 2, UT, D], F32, ctx)
            z3 = sb("z3", [P, 2, UT, D], F32, ctx)
            res = sb("res", [P, 2, UT, D], F32, ctx)
            bn3 = sb("bn3", [P, 2, UT, 6], F32, ctx)
            mo3 = sb("mo3", [P, 2, 6, UT], F32, ctx)
            ve3 = sb("ve3", [P, 2, UT], F32, ctx)
            rs3 = sb("rs3", [P, 2, UT], F32, ctx)
            nm3 = sb("nm3", [P, 2, UT], F32, ctx)
            hid_mm = count("hid_mm", 2)
            gelu_made = count("gelu_made", 2)
            m_mm = count("m_mm")
            y3_out = count("y3_out")
            st3 = count("st3", 4)
            rs3_made = count("rs3_made", 3)
            z3_made = count("z3_made")
            zg3_made = count("zg3_made")
            res_made = count("res_made")
            stored = [count(f"stored{s}", 16) for s in range(2)]

            def pairs(engine, body):
                body(0, 0, 0, 0, True)
                body(1, 1, 0, 1, True)
                with engine.Fori(1, UNITS // 2 - 1) as g:
                    body(g * 2, 0, g, 2, True)
                    body(g * 2 + 1, 1, g, 2, True)
                body(UNITS - 2, 0, UNITS // 2 - 1, 2, True)
                body(UNITS - 1, 1, UNITS // 2 - 1, 2, False)

            with nc.Block() as block:
                @block.sync
                def _(sp):
                    for s in range(2):
                        stored[s].start(sp)
                    with sp.Fori(0, UNITS // 2) as g:
                        for s in range(2):
                            sp.wait_ge(res_made.sem, res_made.done(g * 2 + s))
                            sp.dma_start(out[:, bass.ds(g * (2 * UT) + s * UT, UT), :],
                                         res[:, s, :, :]).then_inc(stored[s].sem, 16)
                    for s in range(2):
                        sp.wait_ge(stored[s].sem, stored[s].done(UNITS // 2 - 1))

                @block.tensor
                def _(pe):
                    hid_mm.start(pe)
                    m_mm.start(pe)

                    def hidden(unit, s):
                        for j in range(2):
                            pe.wait_ge(gelu_made.sem, gelu_made.done(unit - 2, j + 1))
                            nc.tensor.matmul(ps[:, 2 * s + j, :], W1[:, j * P:(j + 1) * P],
                                             X2T[:, bass.ds(unit * UW, UW)], start=True,
                                             stop=True).then_inc(hid_mm.sem, 1)

                    def body(unit, s, turn, back, more):
                        if more:
                            hidden(unit + 1, 1 - s)
                        pe.wait_ge(gelu_made.sem, gelu_made.done(unit))
                        pe.wait_ge(y3_out.sem, y3_out.done(unit - 2))
                        for k in range(UT):
                            for j in range(2):
                                last = nc.tensor.matmul(ps[:, 4 + s, k * P:(k + 1) * P],
                                                        hid[:, s, j, k * P:(k + 1) * P], W2[:, j, :],
                                                        start=j == 0, stop=j == 1)
                        last.then_inc(m_mm.sem, 1)

                    hidden(0, 0)
                    pairs(pe, body)

                @block.scalar
                def _(act):
                    gelu_made.start(act)
                    z3_made.start(act)

                    def gelu(unit, s):
                        act.wait_ge(m_mm.sem, m_mm.done(unit - 2))
                        for j in range(2):
                            act.wait_ge(hid_mm.sem, hid_mm.done(unit, j + 1))
                            nc.scalar.activation(hid[:, s, j, :], ps[:, 2 * s + j, :], ACT.Gelu,
                                                 bias=cols[:, 1 + j:2 + j]).then_inc(gelu_made.sem, 1)

                    def normalise(unit, s):
                        act.wait_ge(rs3_made.sem, rs3_made.done(unit))
                        act.wait_ge(res_made.sem, res_made.done(unit - 2))
                        for k in range(UT):
                            last = nc.scalar.activation(z3[:, s, k, :], y3[:, s, k, :], ACT.Identity,
                                                        bias=nm3[:, s, k:k + 1], scale=rs3[:, s, k:k + 1])
                        last.then_inc(z3_made.sem, 1)

                    def body(unit, s, turn, back, more):
                        if more:
                            gelu(unit + 1, 1 - s)
                        if back:
                            normalise(unit - 1, 1 - s)

                    gelu(0, 0)
                    pairs(act, body)
                    normalise(UNITS - 1, 1)

                @block.gpsimd
                def _(pool):
                    for c in (rs3_made, zg3_made):
                        c.start(pool)

                    def rstd_of(unit, s):
                        pool.wait_ge(st3.sem, st3.done(unit))
                        nc.gpsimd.tensor_tensor(ve3[:, s, :], mo3[:, s, VAR, :], eps[:],
                                                ALU.add).then_inc(rs3_made.sem, 1)
                        pool.wait_ge(rs3_made.sem, rs3_made.done(unit, 1))
                        nc.gpsimd.tensor_tensor(rs3[:, s, :], ve3[:, s, :], minus_half[:],
                                                ALU.pow).then_inc(rs3_made.sem, 1)
                        pool.wait_ge(rs3_made.sem, rs3_made.done(unit, 2))
                        nc.gpsimd.tensor_tensor(nm3[:, s, :], mo3[:, s, NMEAN, :], rs3[:, s, :],
                                                ALU.mult).then_inc(rs3_made.sem, 1)

                    def scale(unit, s):
                        pool.wait_ge(z3_made.sem, z3_made.done(unit))
                        nc.gpsimd.tensor_tensor(z3[:, s, :, :], z3[:, s, :, :], row(G3),
                                                ALU.mult).then_inc(zg3_made.sem, 1)

                    def body(unit, s, turn, back, more):
                        rstd_of(unit, s)
                        if back:
                            scale(unit - 1, 1 - s)

                    pairs(pool, body)
                    scale(UNITS - 1, 1)

                @block.vector
                def _(dve):
                    for c in (y3_out, st3, res_made):
                        c.start(dve)

                    def result(unit, s, turn):
                        dve.wait_ge(zg3_made.sem, zg3_made.done(unit))
                        dve.wait_ge(stored[s].sem, stored[s].done(turn - 1))
                        nc.vector.tensor_tensor(res[:, s, :, :], z3[:, s, :, :], X[:, bass.ds(unit * UT, UT), :],
                                                ALU.add).then_inc(res_made.sem, 1)

                    def body(unit, s, turn, back, more):
                        dve.wait_ge(m_mm.sem, m_mm.done(unit))
                        dve.wait_ge(z3_made.sem, z3_made.done(unit - 2))
                        nc.vector.tensor_tensor(y3[:, s, :, :], ps[:, 4 + s, :].rearrange("p (a b) -> p a b", a=UT),
                                                X2[:, bass.ds(unit * UT, UT), :], ALU.add).then_inc(y3_out.sem, 1)
                        dve.wait_ge(y3_out.sem, y3_out.done(unit))
                        for k in range(UT):
                            last = nc.vector.bn_stats(bn3[:, s, k, :], y3[:, s, k, :])
                        last.then_inc(st3.sem, 1)
                        dve.wait_ge(st3.sem, st3.done(unit, 1))
                        moments_of(dve, bn3[:, s, :, :], mo3[:, s, :, :], st3, unit, 1)
                        if back > 1:
                            result(unit - 2, s, turn - 1)

                    pairs(dve, body)
                    result(UNITS - 2, 0, UNITS // 2 - 1)
                    result(UNITS - 1, 1, UNITS // 2 - 1)


def kernel(**inputs):
    import numpy as np
    import concourse.bacc as bacc
    from concourse.bass_utils import run_bass_kernel_spmd

    a = {k: np.asarray(v) for k, v in inputs.items()}

    def halves(m):
        return m.reshape(2, P, -1).transpose(1, 0, 2)

    def lstm(m):
        return m.transpose(2, 0, 1).reshape(D, -1)

    def lstm_bias(m):
        return m.reshape(MAX_SKIP * 4, D).T

    n0, n1 = "L0_gnn_", "L1_gnn_"
    arrays = {
        "x": a["x"].reshape(TILES, P, D).transpose(1, 0, 2),
        "adj": halves(a["adj"]),
        "adjT": halves(a["adj"].T),
        "Wg": np.stack([a[n0 + "Wg0"], a[n0 + "Wg1"]], 1),
        "bg0": a[n0 + "bg0"][None],
        "Wih": lstm(a[n0 + "Wih"]),
        "Whh": lstm(a[n0 + "Whh"]),
        "lstm_b": np.stack([lstm_bias(a[n0 + "bih"]), lstm_bias(a[n0 + "bhh"])], 1),
        "rows": np.stack([a[n1 + k] for k in ("bc", "g1", "be1", "bo", "g2", "be2", "b2", "g3", "be3")]),
        "cols": np.stack([a[n0 + "bg1"], *a[n1 + "b1"].reshape(2, D)], 1),
        "Wc": a[n1 + "Wc"], "Wq": a[n1 + "Wq"], "Wk": a[n1 + "Wk"], "Wv": a[n1 + "Wv"], "Wo": a[n1 + "Wo"],
        "W1": a[n1 + "W1"], "W2": halves(a[n1 + "W2"]),
    }
    arrays = {k: np.ascontiguousarray(v) for k, v in arrays.items()}
    nc = bacc.Bacc("TRN2", target_bir_lowering=False, num_devices=1)
    d = {k: nc.dram_tensor(f"in_{k}", v.shape, F32, kind="ExternalInput").ap() for k, v in arrays.items()}
    out = nc.dram_tensor("out", (P, TILES, D), F32, kind="ExternalOutput").ap()
    build(nc, d, out)
    r = run_bass_kernel_spmd(nc, [{f"in_{k}": v for k, v in arrays.items()}], core_ids=[0])
    return r.results[0]["out"].transpose(1, 0, 2).reshape(NB, T, D)
```
